# Optimizing a Trainium2 kernel written in Bass

```python
import numpy as np
import jax
import jax.numpy as jnp

def _softmax(x, axis=-1):
    return jax.nn.softmax(x, axis=axis)

def _gelu(x):
    return jax.nn.gelu(x, approximate=True)

def _silu(x):
    return jax.nn.silu(x)

def _sigmoid(x):
    return jax.nn.sigmoid(x)

def _layernorm(x, axis=-1, eps=1e-05):
    m = jnp.mean(x, axis=axis, keepdims=True)
    v = jnp.var(x, axis=axis, keepdims=True)
    return (x - m) / jnp.sqrt(v + eps)

def _scatter_add(tgt, idx, src, axis=0):
    return tgt.at[idx].add(src)

def _segment_sum(src, seg, n):
    return jax.ops.segment_sum(src, seg, n)
kernel_name = 'mk_adaln_d1_jaxref_r4_43455f'

def setup_inputs(seed: int=0):
    np.random.seed(seed)
    _w = jnp.asarray

    def _L0_attn_setup():
        import jax, jax.numpy as jnp
        import numpy as np
        HID = 512
        D_SSM = 1024
        G = 1
        S = 128
        H = 64
        P = D_SSM // H
        K = 4
        EPS = 1e-05
        CONV_DIM = D_SSM + 2 * G * S
        PROJ = 2 * D_SSM + 2 * G * S + H
        MULT = [0.25, 0.5, 0.75, 1.0, 1.25]

        def _mup_vector():
            v = np.ones(PROJ, np.float32)
            gs = G * S
            v[:D_SSM] *= MULT[0]
            v[D_SSM:2 * D_SSM] *= MULT[1]
            v[2 * D_SSM:2 * D_SSM + gs] *= MULT[2]
            v[2 * D_SSM + gs:2 * D_SSM + 2 * gs] *= MULT[3]
            v[2 * D_SSM + 2 * gs:] *= MULT[4]
            return jnp.asarray(v)

        def _reference_tuple_inner(hidden_states, residual, W_in, conv_w, conv_b, A_log, D, dt_bias, norm_w, W_out, mup_vector):
            B, L, _ = hidden_states.shape
            Hg = H // G
            proj = hidden_states @ W_in * mup_vector
            z, xBC, dt = jnp.split(proj, [D_SSM, D_SSM + CONV_DIM], axis=-1)
            xp = jnp.pad(xBC, ((0, 0), (K - 1, 0), (0, 0)))
            conv = conv_b + sum((conv_w[:, k] * xp[:, k:k + L] for k in range(K)))
            xBC = jax.nn.silu(conv)
            x = xBC[..., :D_SSM].reshape(B, L, G, Hg, P)
            Bm = xBC[..., D_SSM:D_SSM + G * S].reshape(B, L, G, S)
            Cm = xBC[..., D_SSM + G * S:].reshape(B, L, G, S)
            dt = jax.nn.softplus(dt + dt_bias).reshape(B, L, G, Hg)
            dA = jnp.exp(dt * (-jnp.exp(A_log)).reshape(G, Hg))
            xs = (x.transpose(1, 0, 2, 3, 4), Bm.transpose(1, 0, 2, 3), Cm.transpose(1, 0, 2, 3), dA.transpose(1, 0, 2, 3), dt.transpose(1, 0, 2, 3))

            def step(state, inp):
                x_t, B_t, C_t, dA_t, dt_t = inp
                state = state * dA_t[..., None, None] + (dt_t[..., None] * x_t)[..., None] * B_t[:, :, None, None, :]
                y_t = jnp.einsum('bghps,bgs->bghp', state, C_t)
                return (state, y_t)
            state0 = jnp.zeros((B, G, Hg, P, S), hidden_states.dtype)
            _, ys = jax.lax.scan(step, state0, xs)
            y = ys.transpose(1, 0, 2, 3, 4) + D.reshape(G, Hg)[..., None] * x
            y = y.reshape(B, L, D_SSM)
            g = y * jax.nn.silu(z)
            g = g * jax.lax.rsqrt(jnp.mean(jnp.square(g), axis=-1, keepdims=True) + EPS) * norm_w
            out = g @ W_out
            return (out, residual)
        key = jax.random.key(seed)
        ks = jax.random.split(key, 10)
        B, L = (2, 512)
        return {'hidden_states': jax.random.normal(ks[0], (B, L, HID), jnp.float32), 'residual': jax.random.normal(ks[1], (B, L, HID), jnp.float32), 'W_in': jax.random.normal(ks[2], (HID, PROJ), jnp.float32) * 0.02, 'conv_w': jax.random.normal(ks[3], (CONV_DIM, K), jnp.float32) * 0.2, 'conv_b': jax.random.normal(ks[4], (CONV_DIM,), jnp.float32) * 0.02, 'A_log': jax.random.uniform(ks[5], (H,), jnp.float32, 0.0, 1.0), 'D': jax.random.normal(ks[6], (H,), jnp.float32) * 0.5, 'dt_bias': jax.random.normal(ks[7], (H,), jnp.float32) * 0.5, 'norm_w': jnp.ones((D_SSM,), jnp.float32), 'W_out': jax.random.normal(ks[8], (D_SSM, HID), jnp.float32) * 0.02, 'mup_vector': _mup_vector()}
    _L0_attn_in = _L0_attn_setup()

    def _L0_ffn_setup():
        import jax, jax.numpy as jnp
        import numpy as np
        SWIGLU_ALPHA = 1.702
        SWIGLU_LIMIT = 7.0
        B, S, H, E, K, I = (2, 512, 512, 32, 4, 256)
        key = jax.random.key(seed)
        ks = jax.random.split(key, 8)
        return {'hidden_states': jax.random.normal(ks[0], (B, S, H), jnp.float32), 'gate_w': jax.random.normal(ks[1], (E, H), jnp.float32) * 0.02, 'gate_b': jnp.zeros((E,), jnp.float32), 'w_gate': jax.random.normal(ks[2], (E, H, I), jnp.float32) * 0.02, 'b_gate': jnp.zeros((E, I), jnp.float32), 'w_up': jax.random.normal(ks[3], (E, H, I), jnp.float32) * 0.02, 'b_up': jnp.zeros((E, I), jnp.float32), 'w_down': jax.random.normal(ks[4], (E, I, H), jnp.float32) * 0.02, 'b_down': jnp.zeros((E, H), jnp.float32)}
    _L0_ffn_in = _L0_ffn_setup()
    _L0_c = _w((lambda *s: np.random.randn(*s).astype(np.float32) * 0.05)(4, 512))
    _L0_wmod = _w((lambda *s: np.random.randn(*s).astype(np.float32) * 0.05)(512, 6 * 512) * 512 ** (-0.5))
    _d = {'L0_attn_hidden_states': _L0_attn_in['hidden_states'], 'L0_attn_residual': _L0_attn_in['residual'], 'L0_attn_W_in': _L0_attn_in['W_in'], 'L0_attn_conv_w': _L0_attn_in['conv_w'], 'L0_attn_conv_b': _L0_attn_in['conv_b'], 'L0_attn_A_log': _L0_attn_in['A_log'], 'L0_attn_D': _L0_attn_in['D'], 'L0_attn_dt_bias': _L0_attn_in['dt_bias'], 'L0_attn_norm_w': _L0_attn_in['norm_w'], 'L0_attn_W_out': _L0_attn_in['W_out'], 'L0_attn_mup_vector': _L0_attn_in['mup_vector'], 'L0_ffn_gate_w': _L0_ffn_in['gate_w'], 'L0_ffn_gate_b': _L0_ffn_in['gate_b'], 'L0_ffn_w_gate': _L0_ffn_in['w_gate'], 'L0_ffn_b_gate': _L0_ffn_in['b_gate'], 'L0_ffn_w_up': _L0_ffn_in['w_up'], 'L0_ffn_b_up': _L0_ffn_in['b_up'], 'L0_ffn_w_down': _L0_ffn_in['w_down'], 'L0_ffn_b_down': _L0_ffn_in['b_down'], 'L0_c': _L0_c, 'L0_wmod': _L0_wmod}
    _x0 = _d['L0_attn_hidden_states']
    _d['L0_attn_hidden_states'] = jax.random.normal(jax.random.fold_in(jax.random.key(seed), 1), (4, 512, 512), dtype=_x0.dtype)
    del _x0
    return _d

def reference(L0_attn_hidden_states, L0_attn_residual, L0_attn_W_in, L0_attn_conv_w, L0_attn_conv_b, L0_attn_A_log, L0_attn_D, L0_attn_dt_bias, L0_attn_norm_w, L0_attn_W_out, L0_attn_mup_vector, L0_ffn_gate_w, L0_ffn_gate_b, L0_ffn_w_gate, L0_ffn_b_gate, L0_ffn_w_up, L0_ffn_b_up, L0_ffn_w_down, L0_ffn_b_down, L0_c, L0_wmod):

    def _L0_attn_ref(hidden_states, residual, W_in, conv_w, conv_b, A_log, D, dt_bias, norm_w, W_out, mup_vector):
        import jax, jax.numpy as jnp
        import numpy as np
        HID = 512
        D_SSM = 1024
        G = 1
        S = 128
        H = 64
        P = D_SSM // H
        K = 4
        EPS = 1e-05
        CONV_DIM = D_SSM + 2 * G * S
        PROJ = 2 * D_SSM + 2 * G * S + H
        MULT = [0.25, 0.5, 0.75, 1.0, 1.25]

        def _mup_vector():
            v = np.ones(PROJ, np.float32)
            gs = G * S
            v[:D_SSM] *= MULT[0]
            v[D_SSM:2 * D_SSM] *= MULT[1]
            v[2 * D_SSM:2 * D_SSM + gs] *= MULT[2]
            v[2 * D_SSM + gs:2 * D_SSM + 2 * gs] *= MULT[3]
            v[2 * D_SSM + 2 * gs:] *= MULT[4]
            return jnp.asarray(v)

        def _reference_tuple_inner(hidden_states, residual, W_in, conv_w, conv_b, A_log, D, dt_bias, norm_w, W_out, mup_vector):
            B, L, _ = hidden_states.shape
            Hg = H // G
            proj = hidden_states @ W_in * mup_vector
            z, xBC, dt = jnp.split(proj, [D_SSM, D_SSM + CONV_DIM], axis=-1)
            xp = jnp.pad(xBC, ((0, 0), (K - 1, 0), (0, 0)))
            conv = conv_b + sum((conv_w[:, k] * xp[:, k:k + L] for k in range(K)))
            xBC = jax.nn.silu(conv)
            x = xBC[..., :D_SSM].reshape(B, L, G, Hg, P)
            Bm = xBC[..., D_SSM:D_SSM + G * S].reshape(B, L, G, S)
            Cm = xBC[..., D_SSM + G * S:].reshape(B, L, G, S)
            dt = jax.nn.softplus(dt + dt_bias).reshape(B, L, G, Hg)
            dA = jnp.exp(dt * (-jnp.exp(A_log)).reshape(G, Hg))
            xs = (x.transpose(1, 0, 2, 3, 4), Bm.transpose(1, 0, 2, 3), Cm.transpose(1, 0, 2, 3), dA.transpose(1, 0, 2, 3), dt.transpose(1, 0, 2, 3))

            def step(state, inp):
                x_t, B_t, C_t, dA_t, dt_t = inp
                state = state * dA_t[..., None, None] + (dt_t[..., None] * x_t)[..., None] * B_t[:, :, None, None, :]
                y_t = jnp.einsum('bghps,bgs->bghp', state, C_t)
                return (state, y_t)
            state0 = jnp.zeros((B, G, Hg, P, S), hidden_states.dtype)
            _, ys = jax.lax.scan(step, state0, xs)
            y = ys.transpose(1, 0, 2, 3, 4) + D.reshape(G, Hg)[..., None] * x
            y = y.reshape(B, L, D_SSM)
            g = y * jax.nn.silu(z)
            g = g * jax.lax.rsqrt(jnp.mean(jnp.square(g), axis=-1, keepdims=True) + EPS) * norm_w
            out = g @ W_out
            return (out, residual)
        return _reference_tuple_inner(hidden_states, residual, W_in, conv_w, conv_b, A_log, D, dt_bias, norm_w, W_out, mup_vector)[0]

    def _L0_ffn_ref(hidden_states, gate_w, gate_b, w_gate, b_gate, w_up, b_up, w_down, b_down):
        import jax, jax.numpy as jnp
        import numpy as np
        SWIGLU_ALPHA = 1.702
        SWIGLU_LIMIT = 7.0
        B, S, H, E, K, I = (2, 512, 512, 32, 4, 256)
        Bb, Ss, Hh = hidden_states.shape
        x = hidden_states.reshape(-1, Hh)
        logits = x @ gate_w.T + gate_b
        topk_logits, topk_idx = jax.lax.top_k(logits, K)
        topk_weight = jax.nn.softmax(topk_logits.astype(jnp.float32), axis=-1)
        flat_idx = topk_idx.reshape(-1)
        xs = jnp.repeat(x, K, axis=0)
        order = jnp.argsort(flat_idx)
        xt = xs[order]
        gid = flat_idx[order]
        group_sizes = jnp.bincount(flat_idx, length=E).astype(jnp.int32)
        gate = jax.lax.ragged_dot(xt, w_gate, group_sizes) + b_gate[gid]
        up = jax.lax.ragged_dot(xt, w_up, group_sizes) + b_up[gid]
        gate = jnp.minimum(gate, SWIGLU_LIMIT)
        up = jnp.clip(up, -SWIGLU_LIMIT, SWIGLU_LIMIT)
        glu = gate * jax.nn.sigmoid(SWIGLU_ALPHA * gate)
        activated = (up + 1.0) * glu
        outs = jax.lax.ragged_dot(activated, w_down, group_sizes) + b_down[gid]
        inv = jnp.argsort(order)
        outs = outs[inv].reshape(-1, K, Hh)
        y = jnp.sum(outs * topk_weight[..., None], axis=1).astype(x.dtype)
        return y.reshape(Bb, Ss, Hh)
    x = L0_attn_hidden_states
    mod = (_silu(L0_c) @ L0_wmod).reshape(L0_c.shape[0], 6, 1, -1)
    sa, ca, ga, sb, cb, gb = (mod[:, 0], mod[:, 1], mod[:, 2], mod[:, 3], mod[:, 4], mod[:, 5])
    ga = (2 * (ga >= 0) - 1) * jnp.maximum(jnp.abs(ga), 0.25)
    gb = (2 * (gb >= 0) - 1) * jnp.maximum(jnp.abs(gb), 0.25)
    h = _layernorm(x, axis=-1) * (1 + ca) + sa
    x = x + ga * _L0_attn_ref(h, L0_attn_residual, L0_attn_W_in, L0_attn_conv_w, L0_attn_conv_b, L0_attn_A_log, L0_attn_D, L0_attn_dt_bias, L0_attn_norm_w, L0_attn_W_out, L0_attn_mup_vector)
    h = _layernorm(x, axis=-1) * (1 + cb) + sb
    x = x + gb * _L0_ffn_ref(h, L0_ffn_gate_w, L0_ffn_gate_b, L0_ffn_w_gate, L0_ffn_b_gate, L0_ffn_w_up, L0_ffn_b_up, L0_ffn_w_down, L0_ffn_b_down)
    return x

_drawn_inputs = setup_inputs


def setup_inputs(seed=0):
    import zlib

    import numpy as np

    out = dict(_drawn_inputs(seed))
    spreads = {'L0_attn_norm_w': (1.0, 0.6),
     'L0_ffn_gate_b': (0.0, 0.8),
     'L0_ffn_b_gate': (0.0, 0.8),
     'L0_ffn_b_up': (0.0, 0.8),
     'L0_ffn_b_down': (0.0, 0.623)}
    factors = {'L0_attn_conv_b': 3.924,
     'L0_attn_A_log': 8.0,
     'L0_attn_dt_bias': 8.0,
     'L0_ffn_gate_w': 3.45,
     'L0_ffn_w_gate': 4.982,
     'L0_ffn_w_up': 8.0,
     'L0_ffn_w_down': 4.654}
    for name, (base, spread) in spreads.items():
        noise = np.random.default_rng([zlib.crc32(name.encode()), seed]).standard_normal(out[name].shape)
        drawn = base * np.exp(spread * noise) if base else spread * noise
        out[name] = jnp.asarray(drawn.astype(out[name].dtype))
    for name, factor in factors.items():
        out[name] = (out[name] * factor).astype(out[name].dtype)
    return out
```

```python
from contextlib import ExitStack

import numpy as np

import concourse.bass as bass
from concourse import mybir

F32 = mybir.dt.float32
BF16 = mybir.dt.bfloat16
I32 = mybir.dt.int32
U32 = mybir.dt.uint32
ALU = mybir.AluOpType
ACT = mybir.ActivationFunctionType
AX = mybir.AxisListType

P = 128
BATCH, SEQ, HID = 4, 512, 512
KH = HID // P
DI = 1024
HEADS, HD = 64, 16
STATE = 128
TAPS = 4
CONV = DI + 2 * STATE
NCH = CONV // P
PROJ = 2 * DI + 2 * STATE + HEADS
NQ = SEQ // P
NT = BATCH * NQ
EXP, TOPK, FF = 32, 4, 256
SLOTS = 96
RING = 4
AHEAD = RING - 1
WEXP = KH * 2 * FF + 2 * HID
EPS = 1e-5
GRP = 8
NG = HEADS // GRP
DEC = 3 + 12
ROWS = DEC + P // 2
FAR = -32768.0
LOWEST = -88.0
CH = [8, 9, 0, 1, 2, 3, 4, 5, 6, 7]
TURNED = [0] + list(range(2, NCH))


def plan_banks():
    order = [("h", k) for k in range(KH)] + ["dt"] + [("ch", n) for n in range(4)] + ["cum", ("ch", 4), "cumT"]
    order += [("turn", 0), ("ch", 5)]
    for n in range(2, 6):
        order += [("turn", n), ("ch", n + 4)]
    for n in range(6, 10):
        order += [("turn", n), ("z", n - 6)]
    order += [("z", j) for j in range(4, 2 * NQ)]
    uses = [0] * 8
    place = {}
    for i, name in enumerate(order):
        uses[i % 8] += 1
        place[name] = (i % 8, uses[i % 8])
    stage_a = list(uses)
    for q in range(NQ):
        for half in range(2):
            uses[4 + half] += 1
            place[("y", q, half)] = (4 + half, uses[4 + half])
    work = []
    for q in range(NQ + 1):
        if q < NQ:
            work += [("cb", q)] + [("inter", q, i) for i in range(2) if q]
        for a in range(NG):
            work += epilogue_at(q, a)
            if a == 1 and q < NQ - 1:
                work += [("u", q, 0), ("u", q, 1)]
    for i, name in enumerate(work):
        uses[6 + i % 2] += 1
        place[name] = (6 + i % 2, uses[6 + i % 2])
    return order, place, stage_a


def epilogue_at(q, a):
    if not q:
        return []
    return {0: [("gT", q - 1, 0), ("gT", q - 1, 1)], 2: [("wo", q - 1)], 4: [("h2T", q - 1)],
            5: [("lg", q - 1)]}.get(a, [])


def build(nc, ins, out):
    x, cT, wmod, w_in, w_out, convp, vecs, mup, nw, gwT, wexp, bexp = ins
    order_a, place, stage_a = plan_banks()

    mod_d = nc.dram_tensor("mod_d", [BATCH, 6 * HID], F32, kind="Internal").ap()
    cum_d = nc.dram_tensor("cum_d", [HEADS, 3, SEQ], BF16, kind="Internal").ap()
    x2_d = nc.dram_tensor("x2_d", [NT * P, HID], F32, kind="Internal").ap()
    h2_d = nc.dram_tensor("h2_d", [NT * P, HID], F32, kind="Internal").ap()

    with ExitStack() as whole:
        def sb(name, shape, dt=F32, ctx=whole):
            return ctx.enter_context(nc.sbuf_tensor(name, shape, dt))

        def sem(name):
            return whole.enter_context(nc.semaphore(name))

        bank = [whole.enter_context(nc.psum_tensor(f"bank{i}", [P, 512], F32)) for i in range(8)]
        ident = sb("ident", [P, P])
        upto = sb("upto", [P, P])
        ones = sb("ones", [P, P])
        before = sb("before", [P, P])
        top_v = sb("top_v", [P, NT, 8])
        top_i = sb("top_i", [P, NT, 8], U32)
        mixer(nc, place, order_a, stage_a, x, cT, wmod, w_in, w_out, convp, vecs, mup, nw, gwT,
              mod_d, cum_d, x2_d, h2_d, bank, ident, upto, ones, before, top_v, top_i)
        experts(nc, wexp, bexp, mod_d, x2_d, h2_d, out, bank, ident, ones, before, top_v, top_i)


def mixer(nc, place, order_a, stage_a, x, cT, wmod, w_in, w_out, convp, vecs, mup, nw, gwT,
          mod_d, cum_d, x2_d, h2_d, bank, ident, upto, ones, before, top_v, top_i):
    with ExitStack() as ctx:
        def sb(name, shape, dt=F32):
            return ctx.enter_context(nc.sbuf_tensor(name, shape, dt))

        def sem(name):
            return ctx.enter_context(nc.semaphore(name))

        win = sb("win", [P, KH, PROJ])
        wout = sb("wout", [P, 8, HID])
        gw = sb("gw", [P, KH, EXP])
        cvp = sb("cvp", [P, NCH, TAPS + 1])
        nwc = sb("nwc", [P, 8])
        vrow = sb("vrow", [P, 3 * HEADS + EXP])
        modc = sb("modc", [P, 8, BATCH])
        modb = sb("modb", [P, 8])
        sct = sb("sct", [P, KH, BATCH])
        x_in = sb("x_in", [P, NQ, HID])
        hT = sb("hT", [P, KH, SEQ])
        pre = sb("pre", [P, 4, SEQ + TAPS - 1])
        cv = sb("cv", [P, 4, SEQ])
        BT = sb("BT", [P, SEQ])
        CT = sb("CT", [P, SEQ])
        x_t = sb("x_t", [P, NQ, DI])
        B_t = sb("B_t", [P, NQ, STATE])
        zs = sb("zs", [P, NQ, DI])
        dt = sb("dt", [P, NQ * HEADS])
        ecum = sb("ecum", [P, NQ * HEADS])
        edec = sb("edec", [P, NQ * HEADS])
        etot = sb("etot", [P, NQ * HEADS])
        cums = sb("cums", [P, NQ * HEADS])
        parts = sb("parts", [HEADS, 3, SEQ], BF16)
        ga_b = sb("ga_b", [P, HID])
        cb_b = sb("cb_b", [P, HID])
        sb_b = sb("sb_b", [P, HID])
        mv = sb("mv", [ROWS, 2, 32 * P], BF16)
        st = sb("st", [ROWS, 2, 8 * P], BF16)
        one_of_4 = sb("one_of_4", [ROWS, 4, P], BF16)
        two_of_t = sb("two_of_t", [ROWS, 4, P], BF16)
        state = sb("state", [P, DI])
        big = sb("big", [P, 4 * DI])
        xres = sb("xres", [P, HID])
        x2 = sb("x2", [P, HID])
        h2 = sb("h2", [P, HID])
        h2T = sb("h2T", [P, KH, P])
        cbm = sb("cbm", [P, P])
        lg = sb("lg", [P, EXP])
        bnst = sb("bnst", [P, NQ, 6])
        mv4 = sb("mv4", [P, NQ, 2])
        rs4 = sb("rs4", [P, NQ])
        mhalf = sb("mhalf", [P, NQ])
        ss = sb("ss", [P, 2])
        rms = sb("rms", [P, 1])
        bn2 = sb("bn2", [P, 6])
        mv2 = sb("mv2", [P, 2])
        rs2 = sb("rs2", [P, 1])
        tv = sb("tv", [P, NQ, 8])
        ti = sb("ti", [P, NQ, 8], U32)

        E = [pre[:, :, :].rearrange("p a t -> p (a t)")[:, i * GRP * P:(i + 1) * GRP * P] for i in range(2)]
        M = [cv[:, 2 * i:2 * i + 2, :].rearrange("p a t -> p (a t)") for i in range(2)]
        gT = hT[:, 0:2, :].rearrange("p a (k t) -> p (a k) t", t=P)
        xw = hT[:, 2:4, :].rearrange("p a t -> p (a t)")
        xdt = [big[:, i * DI:(i + 1) * DI] for i in range(2)]
        ybuf = big[:, 2 * DI:3 * DI]
        g = big[:, 3 * DI:4 * DI]
        modr = big[0:BATCH, 0:6 * HID]
        tmp = [big[:, 2 * DI + 256 * i:2 * DI + 256 * (i + 1)] for i in range(6)]
        rest = big[0:HEADS, 0:SEQ]
        wm = [x_t[:, 2 * i:2 * i + 2, :].rearrange("p a (k n) -> p (a k) n", n=HID) for i in range(2)]
        mupb = zs[:, :, :].rearrange("p a b -> p (a b)")[:, 0:PROJ]

        s_const = sem("s_const")
        s_ld = sem("s_ld")
        s_wm = [sem("s_wm0"), sem("s_wm1")]
        s_silu = sem("s_silu")
        s_mod = sem("s_mod")
        s_row = sem("s_row")
        s_mup = sem("s_mup")
        s_expa = sem("s_expa")
        s_rows = sem("s_rows")
        s_modT = sem("s_modT")
        s_v = sem("s_v")

        with nc.Block() as block:
            @block.sync
            def _(sp):
                sp.dma_start(sct[:, :, :], cT).then_inc(s_ld, 16)
                sp.dma_start(vrow[:, :], vecs[0:1, :].broadcast_to([P, 3 * HEADS + EXP])).then_inc(s_ld, 16)
                for j in range(6):
                    if j >= 2:
                        sp.wait_ge(s_mod, j - 1)
                    sp.dma_start(wm[j % 2], wmod[j]).then_inc(s_wm[j % 2], 16)
                sp.dma_start(x_in[:, :, :], x[0].rearrange("(q p) d -> p q d", p=P)).then_inc(s_rows, 16)
                sp.wait_ge(s_row, 1)
                sp.dma_start(mod_d[:, :], modr).then_inc(s_rows, 16)
                sp.wait_ge(s_rows, 32)

            @block.scalar
            def _(act):
                act.dma_start(mupb, mup[0:1, :].broadcast_to([P, PROJ])).then_inc(s_ld, 16)
                act.dma_start(nwc[:, :], nw).then_inc(s_ld, 16)
                act.dma_start(gw[:, :, :], gwT).then_inc(s_ld, 16)
                act.dma_start(cvp[:, :, :], convp).then_inc(s_ld, 16)
                act.dma_start(win[:, :, :], w_in).then_inc(s_ld, 16)
                act.dma_start(wout[:, :, :], w_out).then_inc(s_ld, 16)
                act.wait_ge(s_ld, 16 * 8)
                nc.scalar.activation(sct[:, :, :], sct[:, :, :], ACT.Silu).then_inc(s_silu, 1)
                nc.scalar.activation(vrow[:, HEADS:2 * HEADS], vrow[:, HEADS:2 * HEADS], ACT.Exp).then_inc(s_expa, 1)

            @block.gpsimd
            def _(pool):
                nc.gpsimd.memset(ones[:, :], 1.0).then_inc(s_const, 1)
                nc.gpsimd.memset(mhalf[:, :], -0.5).then_inc(s_const, 1)
                nc.gpsimd.memset(one_of_4[:, :, :], -1.0).then_inc(s_const, 1)
                nc.gpsimd.memset(st[:, :, :], 1.0).then_inc(s_const, 1)
                nc.gpsimd.memset(two_of_t[:, :, :], FAR).then_inc(s_const, 1)
                pool.wait_ge(s_const, 5)
                nc.gpsimd.affine_select(out=upto[:, :], in_=ones[:, :], compare_op=ALU.is_ge, fill=0.0, base=0,
                                        pattern=[[1, P]], channel_multiplier=-1).then_inc(s_const, 1)
                nc.gpsimd.affine_select(out=before[:, :], in_=ones[:, :], compare_op=ALU.is_ge, fill=0.0, base=-1,
                                        pattern=[[1, P]], channel_multiplier=-1).then_inc(s_const, 1)
                def keep(tile, pattern, base, by_row, op=ALU.is_ge):
                    nc.gpsimd.affine_select(out=tile, in_=tile, compare_op=op, fill=0.0, base=base, pattern=pattern,
                                            channel_multiplier=by_row).then_inc(s_const, 1)

                keep(st[:, :, :].rearrange("p f (g s) -> p (f g) s", s=P), [[0, 16], [1, P]], 2 * (DEC - 1), -2)
                keep(two_of_t[:, :, :], [[0, 4], [1, P]], 2 * DEC, -2)
                pool.wait_ge(s_const, 9)
                keep(two_of_t[:, :, :], [[0, 4], [-1, P]], 1 - 2 * DEC, 2)
                keep(one_of_4[:, :, :], [[0, 4], [0, P]], DEC - 1, -1)
                for n, off in enumerate(o for o in range(-3, 12) if o % 4):
                    pool.wait_ge(s_const, 11 + n)
                    keep(one_of_4[:, :, :], [[-1, 4], [0, P]], -3 - off, 1, ALU.not_equal)
                pool.wait_ge(s_const, 23)
                nc.gpsimd.tensor_tensor(one_of_4[:, :, :], one_of_4[:, :, :], two_of_t[:, :, :],
                                        ALU.add).then_inc(s_const, 1)
                nc.gpsimd.tensor_tensor(ident[:, :], upto[:, :], before[:, :], ALU.subtract).then_inc(s_const, 1)

            @block.tensor
            def _(pe):
                pe.wait_ge(s_silu, 1)
                for j in range(6):
                    pe.wait_ge(s_wm[j % 2], 16 * (j // 2 + 1))
                    for k in range(KH):
                        last = nc.tensor.matmul(bank[j][0:BATCH, :], sct[:, k, :], wm[j % 2][:, k, :],
                                                start=(k == 0), stop=(k == KH - 1))
                    last.then_inc(s_mod, 1)
                pe.wait_ge(s_row, 1)
                pe.wait_ge(s_const, 25)
                for j in range(8):
                    last = nc.tensor.transpose(bank[6][:, 4 * j:4 * j + 4], modr[:, P * j:P * (j + 1)],
                                               ident[0:BATCH, 0:BATCH])
                last.then_inc(s_modT, 1)

            @block.vector
            def _(dve):
                steps = [0]

                def link(instruction):
                    steps[0] += 1
                    instruction.then_inc(s_v, 1)
                    dve.wait_ge(s_v, steps[0])

                dve.wait_ge(s_ld, 16 * 8)
                for k in range(KH):
                    nc.vector.tensor_tensor(win[:, k, :], win[:, k, :], mupb, ALU.mult).then_inc(s_mup, 1)
                dve.wait_ge(s_expa, 1)
                nc.vector.tensor_scalar(vrow[:, HEADS:2 * HEADS], vrow[:, HEADS:2 * HEADS], -1.0, None,
                                        ALU.mult).then_inc(s_mup, 1)
                for k in range(8):
                    nc.vector.tensor_scalar(wout[:, k, :], wout[:, k, :], nwc[:, k:k + 1], None,
                                            ALU.mult).then_inc(s_mup, 1)
                sgn = x2[0:BATCH, :]
                for j in range(6):
                    row = modr[:, j * HID:(j + 1) * HID]
                    dve.wait_ge(s_mod, j + 1)
                    if j in (0, 3):
                        link(nc.vector.tensor_copy(row, bank[j][0:BATCH, :]))
                    elif j in (1, 4):
                        link(nc.vector.tensor_scalar(row, bank[j][0:BATCH, :], 1.0, None, ALU.add))
                    else:
                        link(nc.vector.tensor_scalar(sgn, bank[j][0:BATCH, :], 0.0, 2.0, ALU.is_ge, ALU.mult))
                        link(nc.vector.tensor_copy(row, bank[j][0:BATCH, :]))
                        link(nc.vector.scalar_tensor_tensor(out=row, in0=bank[j][0:BATCH, :], scalar=-1.0, in1=row,
                                                            op0=ALU.mult, op1=ALU.max))
                        link(nc.vector.tensor_scalar(row, row, 0.25, None, ALU.max))
                        last = nc.vector.scalar_tensor_tensor(out=row, in0=sgn, scalar=-1.0, in1=row,
                                                              op0=ALU.add, op1=ALU.mult)
                        if j == 5:
                            last.then_inc(s_row, 1)
                        else:
                            link(last)
                dve.wait_ge(s_const, 25)
                nc.vector.tensor_copy(mv[:, :, :].rearrange("p f (g c) -> p (f g) c", c=4 * P),
                                      one_of_4[:, :, :].rearrange("p (o j) t -> p o (j t)", o=1)
                                      .broadcast_to([ROWS, 16, 4 * P])).then_inc(s_mup, 1)
                dve.wait_ge(s_modT, 1)
                link(nc.vector.tensor_copy(modc[:, :, :].rearrange("p a b -> p (a b)"), bank[6][:, 0:32]))

        full = [sem(f"full{i}") for i in range(8)]
        free = [sem(f"free{i}") for i in range(8)]
        names = """s_a s_agg s_arg s_bc s_conv s_cumd s_dtv s_exp s_exps s_g s_h2 s_heads
                   s_lg s_m s_modb s_parts s_pl2 s_pool s_pre s_rms s_rs2 s_rstd s_sh
                   s_silu2 s_ss s_std s_step s_sx s_u s_x2b s_xd s_xdt s_xn s_xn2 s_xres
                   s_xw s_yacc""".split()
        S = {n: sem(n) for n in names}
        s_xin = sem("s_xin")
        rows_in = [sem(f"rows_in{i}") for i in range(2)]
        per_loop = full + free + list(S.values()) + rows_in + [s_xin]

        def b3(ap, n):
            return ap.rearrange("p (h o) -> p h o", o=1).broadcast_to([P, ap.shape[1], n])

        def h3(ap):
            return ap.rearrange("p (h d) -> p h d", d=HD)

        def read(eng, name):
            eng.wait_ge(free[place[name][0]], place[name][1])

        with nc.Fori(0, BATCH) as b:
            with nc.Block() as block:
                @block.sync
                def _(sp):
                    for j, dst in ((2, ga_b), (4, cb_b), (3, sb_b)):
                        sp.dma_start(dst[:, :], mod_d[bass.ds(b, 1), j * HID:(j + 1) * HID]
                                     .broadcast_to([P, HID])).then_inc(S["s_bc"], 16)
                    sp.wait_ge(S["s_parts"], 3)
                    sp.dma_start(cum_d[:, :, :], parts[:, :, :]).then_inc(S["s_cumd"], 16)
                    sp.wait_ge(S["s_cumd"], 16)
                    cq = cum_d.rearrange("(f g j) i (q t) -> q f i j g t", f=2, j=4, t=P)
                    cm = cum_d.rearrange("(f h) i (q t) -> q f i h t", f=2, t=P)

                    def decay_rows(q, f):
                        n = 2 * q + f
                        if q:
                            sp.wait_ge(S["s_arg"], 8 * (q - 1) + 4 * f + 4)
                        sp.dma_start(mv[0:3, f, :].rearrange("i (h t) -> i h t", t=P), cm[q, f]).then_inc(rows_in[f], 16)
                        for i in range(3):
                            sp.dma_start(st[3 + 4 * i:7 + 4 * i, f, :].rearrange("j (g t) -> j g t", t=P),
                                         cq[q, f, i]).then_inc(rows_in[f], 16)

                    decay_rows(0, 0)
                    decay_rows(0, 1)
                    read(sp, ("h", KH - 1))
                    sp.dma_start(x_in[:, :, :], x[bass.ds((b + 1) % BATCH, 1)]
                                 .rearrange("o (q p) d -> p (o q) d", p=P)).then_inc(s_xin, 16)

                    def residual(q):
                        if q:
                            sp.wait_ge(S["s_x2b"], q)
                        sp.dma_start(xres[:, :], x[bass.ds(b, 1), q * P:(q + 1) * P, :]
                                     .rearrange("o p d -> (o p) d")).then_inc(S["s_xres"], 16)

                    def store(q):
                        sp.wait_ge(S["s_x2b"], q + 1)
                        sp.dma_start(x2_d[bass.ds(b * SEQ + q * P, P), :], x2[:, :]).then_inc(S["s_sx"], 16)
                        sp.wait_ge(S["s_h2"], q + 1)
                        sp.dma_start(h2_d[bass.ds(b * SEQ + q * P, P), :], h2[:, :]).then_inc(S["s_sh"], 16)

                    residual(0)
                    for q in range(NQ):
                        if q + 1 < NQ:
                            decay_rows(q + 1, 0)
                            decay_rows(q + 1, 1)
                        if q:
                            store(q - 1)
                            residual(q)
                    store(NQ - 1)
                    sp.wait_ge(S["s_sx"], 16 * NQ)
                    sp.wait_ge(S["s_sh"], 16 * NQ)
                    sp.wait_ge(s_xin, 16)

                @block.tensor
                def _(pe):
                    def open_bank(name):
                        k, n = place[name]
                        if n > 1:
                            pe.wait_ge(free[k], n - 1)
                        return bank[k]

                    def close_bank(name, last):
                        last.then_inc(full[place[name][0]], 1)

                    for q in range(NQ):
                        pe.wait_ge(S["s_xn"], q + 1)
                        for k in range(KH):
                            last = nc.tensor.transpose(bank[k][:, q * P:(q + 1) * P], x_in[:, q, k * P:(k + 1) * P],
                                                       ident[:, :])
                            if q == NQ - 1:
                                close_bank(("h", k), last)
                    for k in range(KH):
                        read(pe, ("h", k))
                    for name in order_a[KH:]:
                        kind = name if isinstance(name, str) else name[0]
                        t = open_bank(name)
                        if kind == "dt":
                            for q in range(NQ):
                                for k in range(KH):
                                    last = nc.tensor.matmul(t[:, q * HEADS:(q + 1) * HEADS],
                                                            hT[:, k, q * P:(q + 1) * P], win[:, k, PROJ - HEADS:PROJ],
                                                            start=(k == 0), stop=(k == KH - 1))
                        elif kind == "ch":
                            c0 = DI + CH[name[1]] * P
                            for k in range(KH):
                                last = nc.tensor.matmul(t[:, :], win[:, k, c0:c0 + P], hT[:, k, :],
                                                        start=(k == 0), stop=(k == KH - 1))
                        elif kind == "cum":
                            pe.wait_ge(S["s_a"], 1)
                            nc.tensor.matmul(t[:, 0:256], upto[:, :], tmp[0], start=True, stop=True)
                            last = nc.tensor.matmul(t[:, 256:512], ones[:, :], tmp[0], start=True, stop=True)
                        elif kind == "cumT":
                            read(pe, "cum")
                            for q in range(NQ):
                                last = nc.tensor.transpose(t[0:HEADS, q * P:(q + 1) * P],
                                                           cums[:, q * HEADS:(q + 1) * HEADS], ident[:, :])
                        elif kind == "turn":
                            n = name[1]
                            pe.wait_ge(S["s_silu2"], n + 1)
                            src = BT if n == 0 else cv[:, n % 4, :]
                            for q in range(NQ):
                                last = nc.tensor.transpose(t[:, q * P:(q + 1) * P], src[:, q * P:(q + 1) * P],
                                                           ident[:, :])
                        else:
                            q, half = divmod(name[1], 2)
                            for k in range(KH):
                                last = nc.tensor.matmul(t[:, :], hT[:, k, q * P:(q + 1) * P],
                                                        win[:, k, half * 512:(half + 1) * 512],
                                                        start=(k == 0), stop=(k == KH - 1))
                        close_bank(name, last)

                    def arg(q, a):
                        n = q * NG + a
                        if n == 0:
                            for k in range(4):
                                pe.wait_ge(free[k], stage_a[k])
                        if n >= 2:
                            pe.wait_ge(S["s_exp"], n - 1)
                        if a % 4 == 0:
                            pe.wait_ge(rows_in[a // 4], 64 * (q + 1))
                        for i in range(2):
                            gl = (a % 4) * 2 + i
                            last = nc.tensor.matmul(bank[2 * (n % 2) + i][:, :], st[:, a // 4, gl * P:(gl + 1) * P],
                                                    mv[:, a // 4, gl * 512:(gl + 1) * 512], start=True, stop=True)
                        last.then_inc(S["s_arg"], 1)

                    def heads(q, a):
                        n = q * NG + a
                        name = ("y", q, a // 4)
                        if a % 4 == 0:
                            t = open_bank(name)
                        t = bank[place[name][0]]
                        if a == 0:
                            pe.wait_ge(S["s_xdt"], q + 1)
                        pe.wait_ge(S["s_m"], n + 1)
                        for i in range(GRP):
                            h = a * GRP + i
                            c = (h * HD) % 512
                            last = nc.tensor.matmul(t[:, c:c + HD], M[n % 2][:, i * P:(i + 1) * P],
                                                    xdt[q % 2][:, h * HD:(h + 1) * HD], start=True, stop=True)
                        last.then_inc(S["s_heads"], 1)

                    def epilogue(name):
                        t = open_bank(name)
                        q = name[1]
                        if name[0] == "gT":
                            pe.wait_ge(S["s_g"], 2 * q + name[2] + 1)
                            for k in range(4):
                                c = (4 * name[2] + k) * P
                                last = nc.tensor.transpose(t[:, k * P:(k + 1) * P], g[:, c:c + P], ident[:, :])
                        elif name[0] == "wo":
                            for i in range(2):
                                read(pe, ("gT", q, i))
                            for k in range(8):
                                last = nc.tensor.matmul(t[:, :], gT[:, k, :], wout[:, k, :], start=(k == 0),
                                                        stop=(k == 7))
                        elif name[0] == "h2T":
                            pe.wait_ge(S["s_h2"], q + 1)
                            for k in range(KH):
                                last = nc.tensor.transpose(t[:, k * P:(k + 1) * P], h2[:, k * P:(k + 1) * P],
                                                           ident[:, :])
                        else:
                            read(pe, ("h2T", q))
                            for k in range(KH):
                                last = nc.tensor.matmul(t[:, 0:EXP], h2T[:, k, :], gw[:, k, :], start=(k == 0),
                                                        stop=(k == KH - 1))
                        close_bank(name, last)

                    for q in range(NQ + 1):
                        if q < NQ:
                            name = ("cb", q)
                            t = open_bank(name)
                            if q == 0:
                                read(pe, ("turn", NCH - 1))
                            close_bank(name, nc.tensor.matmul(t[:, 0:P], BT[:, q * P:(q + 1) * P],
                                                              CT[:, q * P:(q + 1) * P], start=True, stop=True))
                            for i in range(2 if q else 0):
                                name = ("inter", q, i)
                                t = open_bank(name)
                                read(pe, ("u", q - 1, i))
                                close_bank(name, nc.tensor.matmul(t[:, :], CT[:, q * P:(q + 1) * P],
                                                                  state[:, i * 512:(i + 1) * 512],
                                                                  start=True, stop=True))
                            arg(q, 0)
                            arg(q, 1)
                        for a in range(NG):
                            if q < NQ:
                                heads(q, a)
                                if a + 2 < NG:
                                    arg(q, a + 2)
                            for name in epilogue_at(q, a):
                                epilogue(name)
                            if a == 1 and q < NQ - 1:
                                for i in range(2):
                                    name = ("u", q, i)
                                    t = open_bank(name)
                                    pe.wait_ge(S["s_xw"], q + 1)
                                    close_bank(name, nc.tensor.matmul(t[:, :], B_t[:, q, :], xw[:, i * 512:(i + 1) * 512],
                                                                      start=True, stop=True))

                @block.scalar
                def _(act):
                    def filled(name):
                        k, n = place[name]
                        act.wait_ge(full[k], n)
                        return bank[k]

                    act.wait_ge(S["s_modb"], 1)
                    for k in range(KH):
                        t = filled(("h", k))
                        ins = nc.scalar.activation(hT[:, k, :], t[:, :], ACT.Identity, bias=modb[:, k:k + 1],
                                                   scale=modb[:, 4 + k:5 + k])
                        ins.then_inc(free[k], 1)
                    act.wait_ge(S["s_dtv"], 1)
                    nc.scalar.activation(tmp[1], tmp[1], ACT.Exp, scale=-1.0).then_inc(S["s_u"], 1)

                    def to_pre(n):
                        if n >= 4:
                            act.wait_ge(S["s_conv"], n - 3)
                        t = filled(("ch", n))
                        k = place[("ch", n)][0]
                        nc.scalar.activation(pre[:, n % 4, TAPS - 1:], t[:, :], ACT.Copy).then_inc(free[k], 1)

                    for n in range(4):
                        to_pre(n)
                    t = filled("cum")
                    nc.scalar.activation(ecum[:, :], t[:, 0:256], ACT.Exp).then_inc(S["s_exps"], 1)
                    nc.scalar.activation(etot[:, :], t[:, 256:512], ACT.Exp).then_inc(S["s_exps"], 1)
                    read(act, "cum")
                    nc.scalar.activation(edec[:, :], edec[:, :], ACT.Exp).then_inc(S["s_exps"], 1)

                    def turned(n):
                        t = filled(("turn", n))
                        k = place[("turn", n)][0]
                        c = CH[n]
                        dst = B_t[:, :, :] if n == 0 else x_t[:, :, c * P:(c + 1) * P]
                        nc.scalar.activation(dst, t[:, :].rearrange("p (q c) -> p q c", c=P), ACT.Copy) \
                            .then_inc(free[k], 1)

                    for n in range(NCH):
                        act.wait_ge(S["s_conv"], n + 1)
                        dst = {0: BT[:, :], 1: CT[:, :]}.get(n, cv[:, n % 4, :])
                        nc.scalar.activation(dst, cv[:, n % 4, :], ACT.Silu).then_inc(S["s_silu2"], 1)
                        if n + 4 < NCH:
                            to_pre(n + 4)
                        if n - 1 in TURNED:
                            turned(n - 1)
                    turned(NCH - 1)
                    for j in range(2 * NQ):
                        t = filled(("z", j))
                        k = place[("z", j)][0]
                        ins = nc.scalar.activation(zs[:, j // 2, (j % 2) * 512:(j % 2 + 1) * 512], t[:, :], ACT.Silu)
                        ins.then_inc(free[k], 1)

                    def after(q, a):
                        for name in epilogue_at(q, a):
                            if name[0] == "gT":
                                i = name[2]
                                t = filled(name)
                                ins = nc.scalar.activation(gT[:, 4 * i:4 * i + 4, :].rearrange("p k t -> p (k t)"),
                                                           t[:, :], ACT.Copy)
                                ins.then_inc(free[place[name][0]], 1)
                            if name[0] == "h2T":
                                t = filled(name)
                                ins = nc.scalar.activation(h2T[:, :, :].rearrange("p k t -> p (k t)"), t[:, :], ACT.Copy)
                                ins.then_inc(free[place[name][0]], 1)

                    for q in range(NQ + 1):
                        for a in range(NG):
                            if q < NQ:
                                n = q * NG + a
                                act.wait_ge(S["s_arg"], n + 1)
                                if n >= 2:
                                    act.wait_ge(S["s_m"], n - 1)
                                for i in range(2):
                                    ins = nc.scalar.activation(E[n % 2][:, i * 512:(i + 1) * 512],
                                                               bank[2 * (n % 2) + i][:, :], ACT.Exp)
                                ins.then_inc(S["s_exp"], 1)
                            after(q, a)
                        if q < NQ:
                            for i in range(2):
                                act.wait_ge(S["s_g"], 2 * q + i + 1)
                                if q and i == 0:
                                    act.wait_ge(S["s_rms"], q)
                                nc.scalar.activation(ybuf[:, i * 512:(i + 1) * 512], g[:, i * 512:(i + 1) * 512],
                                                     ACT.Square, accum_out=ss[:, i:i + 1]).then_inc(S["s_ss"], 1)

                @block.gpsimd
                def _(pool):
                    steps = [0]

                    def link(instruction):
                        steps[0] += 1
                        instruction.then_inc(S["s_pool"], 1)
                        pool.wait_ge(S["s_pool"], steps[0])

                    nc.gpsimd.memset(pre[:, :, 0:TAPS - 1], 0.0).then_inc(S["s_pre"], 1)
                    pool.wait_ge(S["s_rstd"], NQ)
                    link(nc.gpsimd.tensor_scalar(rs4[:, :], mv4[:, :, 1], EPS, None, ALU.add))
                    nc.gpsimd.tensor_tensor(rs4[:, :], rs4[:, :], mhalf[:, :], ALU.pow).then_inc(S["s_pl2"], 1)

                    def norm_rows(q):
                        pool.wait_ge(S["s_ss"], 2 * (q + 1))
                        link(nc.gpsimd.tensor_tensor(rms[:, :], ss[:, 0:1], ss[:, 1:2], ALU.add))
                        link(nc.gpsimd.tensor_scalar(rms[:, :], rms[:, :], 1.0 / DI, EPS, ALU.mult, ALU.add))
                        nc.gpsimd.tensor_tensor(rms[:, :], rms[:, :], mhalf[:, 0:1], ALU.pow).then_inc(S["s_rms"], 1)

                    def norm2(q):
                        pool.wait_ge(S["s_agg"], q + 1)
                        link(nc.gpsimd.tensor_scalar(rs2[:, :], mv2[:, 1:2], EPS, None, ALU.add))
                        nc.gpsimd.tensor_tensor(rs2[:, :], rs2[:, :], mhalf[:, 0:1], ALU.pow).then_inc(S["s_rs2"], 1)
                        pool.wait_ge(S["s_xn2"], q + 1)
                        if q == 0:
                            pool.wait_ge(S["s_bc"], 48)
                        link(nc.gpsimd.tensor_tensor(h2[:, :], h2[:, :], cb_b[:, :], ALU.mult))
                        nc.gpsimd.tensor_tensor(h2[:, :], h2[:, :], sb_b[:, :], ALU.add).then_inc(S["s_h2"], 1)

                    def chunk_inputs(q):
                        c = slice(q * HEADS, (q + 1) * HEADS)
                        if q >= 2:
                            pool.wait_ge(S["s_heads"], NG * (q - 1))
                        nc.gpsimd.tensor_tensor(h3(xdt[q % 2]), h3(x_t[:, q, :]), b3(dt[:, c], HD),
                                                ALU.mult).then_inc(S["s_xdt"], 1)
                        if q < NQ - 1:
                            pool.wait_ge(S["s_xdt"], q + 1)
                            if q:
                                k, n = place[("u", q - 1, 1)]
                                pool.wait_ge(full[k], n)
                            nc.gpsimd.tensor_tensor(h3(xw), h3(xdt[q % 2]), b3(edec[:, c], HD),
                                                    ALU.mult).then_inc(S["s_xw"], 1)
                        d_row = b3(vrow[:, 2 * HEADS:3 * HEADS], HD)
                        if q == 0:
                            nc.gpsimd.tensor_tensor(h3(ybuf), h3(x_t[:, q, :]), d_row, ALU.mult).then_inc(S["s_yacc"], 1)
                        else:
                            nc.gpsimd.tensor_tensor(h3(x_t[:, q, :]), h3(x_t[:, q, :]), d_row,
                                                    ALU.mult).then_inc(S["s_xd"], 1)

                    for n in TURNED:
                        read(pool, ("turn", n))
                    pool.wait_ge(S["s_exps"], 3)
                    k, n = place[("z", 2 * NQ - 1)]
                    pool.wait_ge(full[k], n)
                    chunk_inputs(0)
                    for q in range(NQ + 1):
                        if 0 < q < NQ:
                            pool.wait_ge(S["s_xd"], q)
                            for i in range(2):
                                read(pool, ("inter", q, i))
                            nc.gpsimd.tensor_tensor(ybuf, ybuf, x_t[:, q, :], ALU.add).then_inc(S["s_yacc"], 1)
                            if q < NQ - 1:
                                c = slice(q * HEADS, (q + 1) * HEADS)
                                nc.gpsimd.tensor_tensor(h3(state[:, :]), h3(state[:, :]), b3(etot[:, c], HD),
                                                        ALU.mult).then_inc(S["s_std"], 1)
                        if q:
                            norm2(q - 1)
                        if q + 1 < NQ:
                            chunk_inputs(q + 1)
                        if q < NQ:
                            norm_rows(q)

                @block.vector
                def _(dve):
                    steps = [0]

                    def link(instruction):
                        steps[0] += 1
                        instruction.then_inc(S["s_step"], 1)
                        dve.wait_ge(S["s_step"], steps[0])

                    def filled(name):
                        k, n = place[name]
                        dve.wait_ge(full[k], n)
                        return bank[k]

                    def reads(name, instruction):
                        instruction.then_inc(free[place[name][0]], 1)
                        read(dve, name)

                    nc.vector.tensor_copy(modb[:, :], modc[:, :, bass.ds(b, 1)].rearrange("p a o -> p (a o)")) \
                        .then_inc(S["s_modb"], 1)
                    for q in range(NQ):
                        link(nc.vector.bn_stats(bnst[:, q, :], x_in[:, q, :]))
                        nc.vector.bn_aggr(mv4[:, q, :], bnst[:, q, :]).then_inc(S["s_rstd"], 1)
                    dve.wait_ge(S["s_pl2"], 1)
                    for q in range(NQ):
                        nc.vector.tensor_scalar(x_in[:, q, :], x_in[:, q, :], mv4[:, q, 0:1], rs4[:, q:q + 1],
                                                ALU.subtract, ALU.mult).then_inc(S["s_xn"], 1)

                    t = filled("dt")
                    v, u, s, s2, p = dt[:, :], tmp[1], tmp[2], tmp[3], tmp[4]
                    reads("dt", nc.vector.tensor_tensor(v.rearrange("p (q h) -> p q h", q=NQ),
                                                        t[:, 0:256].rearrange("p (q h) -> p q h", q=NQ),
                                                        vrow[:, 0:HEADS].rearrange("p (o h) -> p o h", o=1)
                                                        .broadcast_to([P, NQ, HEADS]), ALU.add))
                    nc.vector.scalar_tensor_tensor(out=u, in0=v, scalar=-1.0, in1=v, op0=ALU.mult,
                                                   op1=ALU.max).then_inc(S["s_dtv"], 1)
                    dve.wait_ge(S["s_u"], 1)
                    link(nc.vector.tensor_scalar(s, u, 2.0, None, ALU.add))
                    link(nc.vector.reciprocal(s, s))
                    link(nc.vector.tensor_tensor(s, s, u, ALU.mult))
                    link(nc.vector.tensor_tensor(s2, s, s, ALU.mult))
                    link(nc.vector.tensor_scalar(p, s2, 1.0 / 13, None, ALU.mult))
                    for d in (11, 9, 7, 5, 3):
                        link(nc.vector.scalar_tensor_tensor(out=p, in0=p, scalar=1.0 / d, in1=s2, op0=ALU.add,
                                                            op1=ALU.mult))
                    link(nc.vector.scalar_tensor_tensor(out=p, in0=p, scalar=1.0, in1=s, op0=ALU.add, op1=ALU.mult))
                    link(nc.vector.tensor_scalar(v, v, 0.0, None, ALU.max))
                    link(nc.vector.scalar_tensor_tensor(out=v, in0=p, scalar=2.0, in1=v, op0=ALU.mult, op1=ALU.add))
                    link(nc.vector.tensor_tensor(tmp[0].rearrange("p (q h) -> p q h", q=NQ),
                                                 v.rearrange("p (q h) -> p q h", q=NQ),
                                                 vrow[:, HEADS:2 * HEADS].rearrange("p (o h) -> p o h", o=1)
                                                 .broadcast_to([P, NQ, HEADS]), ALU.mult))
                    nc.vector.tensor_scalar(tmp[0], tmp[0], LOWEST, None, ALU.max).then_inc(S["s_a"], 1)

                    def conv(n):
                        c = CH[n]
                        if n == 0:
                            dve.wait_ge(S["s_pre"], 1)
                        if n >= 4:
                            if n - 4 in TURNED[1:]:
                                k, m = place[("turn", n - 4)]
                                dve.wait_ge(full[k], m)
                            else:
                                dve.wait_ge(S["s_silu2"], n - 3)
                        k, m = place[("ch", n)]
                        dve.wait_ge(free[k], m)
                        link(nc.vector.tensor_scalar(cv[:, n % 4, :], pre[:, n % 4, 0:SEQ], cvp[:, c, 0:1],
                                                     cvp[:, c, TAPS:TAPS + 1], ALU.mult, ALU.add))
                        for tap in range(1, TAPS):
                            ins = nc.vector.scalar_tensor_tensor(out=cv[:, n % 4, :], in0=pre[:, n % 4, tap:tap + SEQ],
                                                                 scalar=cvp[:, c, tap:tap + 1], in1=cv[:, n % 4, :],
                                                                 op0=ALU.mult, op1=ALU.add)
                            if tap < TAPS - 1:
                                link(ins)
                            else:
                                ins.then_inc(S["s_conv"], 1)

                    for n in range(3):
                        conv(n)
                    t = filled("cum")
                    dve.wait_ge(S["s_exps"], 2)
                    link(nc.vector.tensor_copy(cums[:, :], t[:, 0:256]))
                    reads("cum", nc.vector.tensor_tensor(edec[:, :], t[:, 256:512], cums[:, :], ALU.subtract))
                    conv(3)
                    t = filled("cumT")
                    nc.vector.tensor_copy(parts[:, 0, :], t[0:HEADS, :]).then_inc(S["s_parts"], 1)
                    dve.wait_ge(S["s_parts"], 1)
                    reads("cumT", nc.vector.tensor_tensor(rest, t[0:HEADS, :], parts[:, 0, :], ALU.subtract))
                    nc.vector.tensor_copy(parts[:, 1, :], rest).then_inc(S["s_parts"], 1)
                    dve.wait_ge(S["s_parts"], 2)
                    link(nc.vector.tensor_tensor(rest, rest, parts[:, 1, :], ALU.subtract))
                    nc.vector.tensor_copy(parts[:, 2, :], rest).then_inc(S["s_parts"], 1)
                    for n in range(4, NCH):
                        conv(n)

                    def after(q, a):
                        for name in epilogue_at(q, a):
                            if name[0] == "wo":
                                p1 = name[1]
                                t = filled(name)
                                dve.wait_ge(S["s_rms"], p1 + 1)
                                if p1 == 0:
                                    dve.wait_ge(S["s_bc"], 48)
                                else:
                                    dve.wait_ge(S["s_sx"], 16 * p1)
                                reads(name, nc.vector.scalar_tensor_tensor(
                                    out=x2[:, :], in0=t[:, :], scalar=rms[:, 0:1], in1=ga_b[:, :], op0=ALU.mult,
                                    op1=ALU.mult))
                                dve.wait_ge(S["s_xres"], 16 * (p1 + 1))
                                nc.vector.tensor_tensor(x2[:, :], x2[:, :], xres[:, :], ALU.add).then_inc(S["s_x2b"], 1)
                                dve.wait_ge(S["s_x2b"], p1 + 1)
                                link(nc.vector.bn_stats(bn2[:, :], x2[:, :]))
                                nc.vector.bn_aggr(mv2[:, :], bn2[:, :]).then_inc(S["s_agg"], 1)
                            if name[0] == "lg":
                                p1 = name[1]
                                t = filled(name)
                                reads(name, nc.vector.tensor_tensor(lg[:, :], t[:, 0:EXP], vrow[:, 3 * HEADS:], ALU.add))
                                link(nc.vector.max(tv[:, p1, :], lg[:, :]))
                                nc.vector.max_index(ti[:, p1, :], tv[:, p1, :], lg[:, :]).then_inc(S["s_lg"], 1)
                        if q and a == 3:
                            p1 = q - 1
                            dve.wait_ge(S["s_rs2"], p1 + 1)
                            if p1:
                                dve.wait_ge(S["s_sh"], 16 * p1)
                                k, n = place[("h2T", p1 - 1)]
                                dve.wait_ge(full[k], n)
                            nc.vector.tensor_scalar(h2[:, :], x2[:, :], mv2[:, 0:1], rs2[:, 0:1], ALU.subtract,
                                                    ALU.mult).then_inc(S["s_xn2"], 1)

                    def gate(q, i):
                        half = slice(i * 512, (i + 1) * 512)
                        dve.wait_ge(S["s_heads"], NG * q + 4 * (i + 1))
                        t = bank[place[("y", q, i)][0]]
                        if i == 0:
                            dve.wait_ge(S["s_yacc"], q + 1)
                        read(dve, ("z", 2 * q + i))
                        reads(("y", q, i), nc.vector.tensor_tensor(ybuf[:, half], ybuf[:, half], t[:, :], ALU.add))
                        if q:
                            k, n = place[("gT", q - 1, i)]
                            dve.wait_ge(full[k], n)
                            dve.wait_ge(S["s_ss"], 2 * q)
                        nc.vector.tensor_tensor(g[:, half], ybuf[:, half], zs[:, q, half], ALU.mult).then_inc(S["s_g"], 1)

                    for q in range(NQ + 1):
                        if q < NQ:
                            t = filled(("cb", q))
                            reads(("cb", q), nc.vector.tensor_tensor(cbm[:, :], t[:, 0:P], upto[:, :], ALU.mult))
                            for i in range(2 if q else 0):
                                t = filled(("inter", q, i))
                                dve.wait_ge(S["s_ss"], 2 * q)
                                c = slice(q * HEADS + i * 32, q * HEADS + (i + 1) * 32)
                                reads(("inter", q, i), nc.vector.tensor_tensor(
                                    h3(ybuf[:, i * 512:(i + 1) * 512]), h3(t[:, :]), b3(ecum[:, c], HD), ALU.mult))
                        for a in range(NG):
                            if q < NQ:
                                n = q * NG + a
                                dve.wait_ge(S["s_exp"], n + 1)
                                if n >= 2:
                                    dve.wait_ge(S["s_heads"], n - 1)
                                if n == 0:
                                    read(dve, ("turn", NCH - 1))
                                nc.vector.tensor_tensor(
                                    M[n % 2].rearrange("p (h t) -> p h t", t=P),
                                    E[n % 2].rearrange("p (h t) -> p h t", t=P),
                                    cbm[:, :].rearrange("p (o t) -> p o t", o=1).broadcast_to([P, GRP, P]),
                                    ALU.mult).then_inc(S["s_m"], 1)
                            if q < NQ - 1 and a == 2:
                                for i in range(2):
                                    t = filled(("u", q, i))
                                    half = slice(i * 512, (i + 1) * 512)
                                    if q == 0:
                                        ins = nc.vector.tensor_copy(state[:, half], t[:, :])
                                    else:
                                        dve.wait_ge(S["s_std"], q)
                                        ins = nc.vector.tensor_tensor(state[:, half], state[:, half], t[:, :], ALU.add)
                                    reads(("u", q, i), ins)
                            after(q, a)
                            if q < NQ and a == 5:
                                gate(q, 0)
                        if q < NQ:
                            gate(q, 1)
                    dve.wait_ge(S["s_lg"], NQ)
                    nc.vector.tensor_copy(top_v[:, bass.ds(b * NQ, NQ), :], tv[:, :, :]).then_inc(S["s_step"], 1)
                    nc.vector.tensor_copy(top_i[:, bass.ds(b * NQ, NQ), :], ti[:, :, :]).then_inc(S["s_step"], 1)
            with nc.Block() as block:
                @block.gpsimd
                def _(pool):
                    for s in per_loop:
                        pool.sem_clear(s)


def experts(nc, wexp, bexp, mod_d, x2_d, h2_d, out, bank, ident, ones, before, top_v, top_i):
    TK = NT * TOPK
    COLS = SLOTS + 4
    perm_d = nc.dram_tensor("perm_d", [P * SLOTS, 1], I32, kind="Internal").ap()
    ys_d = nc.dram_tensor("ys_d", [SLOTS * P, HID], F32, kind="Internal").ap()
    with ExitStack() as ctx:
        def sb(name, shape, dt=F32, c=ctx):
            return c.enter_context(nc.sbuf_tensor(name, shape, dt))

        def sem(name):
            return ctx.enter_context(nc.semaphore(name))

        idx = sb("idx", [P, COLS], I32)
        tab_e = sb("tab_e", [1, COLS], I32)
        tab_n = sb("tab_n", [1, COLS], I32)
        tab_r = sb("tab_r", [1, COLS + 1], I32)
        dest = sb("dest", [P, TK], I32)
        wts = sb("wts", [P, TK])

        with ExitStack() as rt:
            def tb(name, shape, dt=F32):
                return sb(name, shape, dt, rt)

            iota_e = tb("iota_e", [P, EXP])
            iota_s = tb("iota_s", [P, COLS])
            tok = tb("tok", [P, NT], I32)
            zero = tb("zero", [P, SLOTS], I32)
            topf = tb("topf", [P, TK])
            hot = tb("hot", [P, TK, EXP])
            chosen = tb("chosen", [P, NT, EXP])
            acc = tb("acc", [P, NT + 1, EXP])
            cnt_i = tb("cnt_i", [P, EXP], I32)
            ntf = tb("ntf", [P, EXP])
            cin = tb("cin", [P, EXP])
            base = tb("base", [P, EXP])
            pos = tb("pos", [P, NT, EXP])
            destf = tb("destf", [P, TK])
            desti = tb("desti", [P, TK], I32)
            hi_i = tb("hi_i", [P, TK], I32)
            addr = tb("addr", [P, TK], I32)
            cmp = tb("cmp", [P, COLS, EXP])
            eid = tb("eid", [P, COLS])
            new = tb("new", [P, COLS])
            cnew = tb("cnew", [P, COLS])
            ev = tb("ev", [P, TK])
            ws = tb("ws", [P, NT])
            r_const = sem("r_const")
            r_step = sem("r_step")
            r_chosen = sem("r_chosen")
            r_pos = sem("r_pos")
            r_addr = sem("r_addr")
            r_zero = sem("r_zero")
            r_ev = sem("r_ev")
            r_exp = sem("r_exp")
            r_scat = sem("r_scat")
            r_idx = sem("r_idx")
            with nc.Block() as block:
                @block.gpsimd
                def _(pool):
                    nc.gpsimd.iota(iota_e[:, :], pattern=[[1, EXP]], base=0, channel_multiplier=0,
                                   allow_small_or_imprecise_dtypes=True).then_inc(r_const, 1)
                    nc.gpsimd.iota(iota_s[:, :], pattern=[[1, COLS]], base=0, channel_multiplier=0,
                                   allow_small_or_imprecise_dtypes=True).then_inc(r_const, 1)
                    nc.gpsimd.iota(tok[:, :], pattern=[[P, NT]], base=0, channel_multiplier=1).then_inc(r_const, 1)
                    nc.gpsimd.memset(zero[:, :], 0).then_inc(r_const, 1)
                    nc.gpsimd.memset(idx[:, SLOTS:], 0).then_inc(r_const, 1)
                    pool.wait_ge(r_zero, 16)
                    pool.wait_ge(r_addr, 1)
                    for c in range(TK):
                        pool.indirect_dma_start(perm_d, bass.IndirectOffsetOnAxis(addr[:, c:c + 1], 0),
                                                tok[:, c // TOPK:c // TOPK + 1], None).then_inc(r_scat, 16)

                @block.sync
                def _(sp):
                    sp.wait_ge(r_const, 5)
                    sp.dma_start(perm_d.rearrange("(p s) o -> p (s o)", p=P), zero[:, :]).then_inc(r_zero, 16)
                    sp.wait_ge(r_scat, 16 * TK)
                    sp.dma_start(idx[:, 0:SLOTS], perm_d.rearrange("(p s) o -> p (s o)", p=P)).then_inc(r_idx, 16)
                    sp.wait_ge(r_idx, 16)

                @block.scalar
                def _(act):
                    act.wait_ge(r_ev, 1)
                    nc.scalar.activation(ev[:, :], ev[:, :], ACT.Exp).then_inc(r_exp, 1)

                @block.tensor
                def _(pe):
                    pe.wait_ge(r_chosen, 1)
                    nc.tensor.matmul(bank[0][:, :], before[:, :], chosen[:, :, :].rearrange("p t e -> p (t e)"),
                                     start=True, stop=False)
                    nc.tensor.matmul(bank[0][:, :], ones[:, :], acc[:, 0:NT, :].rearrange("p t e -> p (t e)"),
                                     start=False, stop=True)
                    nc.tensor.matmul(bank[1][:, 0:EXP], ones[:, :], acc[:, NT, :], start=True,
                                     stop=True).then_inc(r_pos, 1)

                @block.vector
                def _(dve):
                    steps = [0]

                    def link(instruction):
                        steps[0] += 1
                        instruction.then_inc(r_step, 1)
                        dve.wait_ge(r_step, steps[0])

                    def col(ap, n):
                        return ap.rearrange("p (c o) -> p c o", o=1).broadcast_to([P, ap.shape[1], n])

                    def row(ap, n):
                        return ap.rearrange("p (o e) -> p o e", o=1).broadcast_to([P, n, ap.shape[1]])

                    e4 = ev[:, :].rearrange("p (t k) -> p t k", k=TOPK)
                    nc.vector.tensor_tensor(e4, top_v[:, :, 0:TOPK], top_v[:, :, 0:1].broadcast_to([P, NT, TOPK]),
                                            ALU.subtract).then_inc(r_ev, 1)
                    link(nc.vector.tensor_copy(topf[:, :].rearrange("p (t k) -> p t k", k=TOPK), top_i[:, :, 0:TOPK]))
                    dve.wait_ge(r_const, 5)
                    link(nc.vector.tensor_tensor(hot[:, :, :], row(iota_e[:, :], TK), col(topf[:, :], EXP),
                                                 ALU.is_equal))
                    link(nc.vector.tensor_reduce(chosen[:, :, :], hot[:, :, :].rearrange("p (t k) e -> p t e k", k=TOPK),
                                                 AX.X, ALU.add))
                    link(nc.vector.memset(acc[:, 0, :], 0.0))
                    for t in range(NT):
                        ins = nc.vector.tensor_tensor(acc[:, t + 1, :], acc[:, t, :], chosen[:, t, :], ALU.add)
                        if t == NT - 1:
                            ins.then_inc(r_chosen, 1)
                        else:
                            link(ins)
                    dve.wait_ge(r_exp, 1)
                    link(nc.vector.tensor_reduce(ws[:, :], e4, AX.X, ALU.add))
                    link(nc.vector.reciprocal(ws[:, :], ws[:, :]))
                    link(nc.vector.tensor_tensor(wts[:, :].rearrange("p (t k) -> p t k", k=TOPK), e4,
                                                 col(ws[:, :], TOPK), ALU.mult))
                    dve.wait_ge(r_pos, 1)
                    link(nc.vector.tensor_scalar(cnt_i[:, :], bank[1][:, 0:EXP], float(P - 1), None, ALU.add))
                    link(nc.vector.tensor_scalar(cnt_i[:, :], cnt_i[:, :], 7, None, ALU.logical_shift_right))
                    link(nc.vector.tensor_copy(ntf[:, :], cnt_i[:, :]))
                    link(nc.vector.tensor_tensor_scan(cin[:, :], ones[:, 0:EXP], ntf[:, :], 0.0, ALU.mult, ALU.add))
                    link(nc.vector.tensor_tensor(base[:, :], cin[:, :], ntf[:, :], ALU.subtract))
                    link(nc.vector.scalar_tensor_tensor(out=pos[:, :, :], in0=row(base[:, :], NT), scalar=float(P),
                                                        in1=bank[0][:, :].rearrange("p (t e) -> p t e", e=EXP),
                                                        op0=ALU.mult, op1=ALU.add))
                    link(nc.vector.tensor_tensor(hot[:, :, :].rearrange("p (t k) e -> p t k e", k=TOPK),
                                                 hot[:, :, :].rearrange("p (t k) e -> p t k e", k=TOPK),
                                                 pos[:, :, :].rearrange("p t (o e) -> p t o e", o=1)
                                                 .broadcast_to([P, NT, TOPK, EXP]), ALU.mult))
                    link(nc.vector.tensor_reduce(destf[:, :], hot[:, :, :], AX.X, ALU.add))
                    link(nc.vector.tensor_copy(desti[:, :], destf[:, :]))
                    link(nc.vector.tensor_scalar(hi_i[:, :], desti[:, :], 7, None, ALU.logical_shift_right))
                    link(nc.vector.tensor_scalar(desti[:, :], desti[:, :], P - 1, None, ALU.bitwise_and))
                    nc.vector.scalar_tensor_tensor(out=addr[:, :], in0=desti[:, :], scalar=float(SLOTS), in1=hi_i[:, :],
                                                   op0=ALU.mult, op1=ALU.add).then_inc(r_addr, 1)
                    link(nc.vector.tensor_scalar(dest[:, :], destf[:, :], float(P), None, ALU.add))
                    link(nc.vector.tensor_tensor(cmp[:, :, :], row(cin[:, :], COLS), col(iota_s[:, :], EXP), ALU.is_le))
                    link(nc.vector.tensor_reduce(eid[:, :], cmp[:, :, :], AX.X, ALU.add))
                    link(nc.vector.tensor_scalar(eid[:, :], eid[:, :], float(EXP - 1), None, ALU.min))
                    link(nc.vector.memset(new[:, 0:1], 1.0))
                    link(nc.vector.tensor_tensor(new[:, 1:], eid[:, 1:], eid[:, 0:COLS - 1], ALU.not_equal))
                    link(nc.vector.tensor_tensor_scan(cnew[:, :], ones[:, 0:COLS], new[:, :], -1.0, ALU.mult, ALU.add))
                    link(nc.vector.tensor_copy(tab_e[:, :], eid[0:1, :]))
                    link(nc.vector.tensor_copy(tab_n[:, :], new[0:1, :]))
                    link(nc.vector.memset(tab_r[:, 0:1], 0))
                    link(nc.vector.tensor_copy(tab_r[:, 1:], cnew[0:1, :]))
                    link(nc.vector.tensor_scalar(tab_r[:, :], tab_r[:, :], RING - 1, None, ALU.bitwise_and))

        with ExitStack() as ex:
            def eb(name, shape, dt=F32):
                return sb(name, shape, dt, ex)

            wr = eb("wr", [P, RING, WEXP])
            br = eb("br", [P, RING, 2 * FF + HID])
            xg = [eb(f"xg{i}", [P, HID]) for i in range(2)]
            idc = [eb(f"idc{i}", [P, 1], I32) for i in range(2)]
            xT = [eb(f"xT{i}", [P, KH * P]) for i in range(2)]
            gu = [eb(f"gu{i}", [P, 2 * FF]) for i in range(2)]
            sg = [eb(f"sg{i}", [P, FF]) for i in range(2)]
            ac = [eb(f"ac{i}", [P, FF]) for i in range(2)]
            aT = [eb(f"aT{i}", [P, 2 * P]) for i in range(2)]
            yo = [eb(f"yo{i}", [P, HID]) for i in range(2)]
            w_in_ring = [sem(f"w_in_ring{i}") for i in range(4)]
            gathered = [sem(f"gathered{i}") for i in range(2)]
            stored = [sem(f"stored{i}") for i in range(2)]
            idx_first = sem("idx_first")
            idx_set = sem("idx_set")
            x_turned = sem("x_turned")
            x_ready = sem("x_ready")
            gu_made = sem("gu_made")
            gu_read = sem("gu_read")
            clamped = sem("clamped")
            sig_made = sem("sig_made")
            act_made = sem("act_made")
            act_turned = sem("act_turned")
            act_ready = sem("act_ready")
            y_made = sem("y_made")
            y_read = sem("y_read")
            e_step = sem("e_step")
            XTB, GUB, ATB, YB = bank[0:2], bank[2:4], bank[4:6], bank[6:8]

            with nc.Block() as block:
                @block.sync
                def _(sp):
                    def load(i, u):
                        e = sp.value_load(tab_e[0:1, bass.ds(i, 1)], min_val=0, max_val=EXP - 1)
                        n = sp.value_load(tab_n[0:1, bass.ds(i, 1)], min_val=0, max_val=1)
                        r = sp.value_load(tab_r[0:1, bass.ds(i + 1, 1)], min_val=0, max_val=RING - 1)
                        sp.dma_start(wr[:, bass.ds(r, 1), :].rearrange("p o w -> p (o w)"),
                                     wexp[bass.ds(e, 1)].rearrange("o p w -> (o p) w"),
                                     cond=(n == 1)).then_inc(w_in_ring[u % 4], 16)
                        sp.dma_start(br[:, bass.ds(r, 1), :].rearrange("p o w -> p (o w)"),
                                     bexp[bass.ds(e, 1), :].broadcast_to([P, 2 * FF + HID]),
                                     cond=(n == 1)).then_inc(w_in_ring[u % 4], 16)

                    for i in range(AHEAD):
                        load(i, i)
                    with sp.Fori(0, SLOTS // 4) as j:
                        for u in range(4):
                            i = 4 * j + u
                            sp.wait_ge(y_read, i + 3)
                            sp.dma_start(ys_d[bass.ds(i * P, P), :], yo[u % 2][:, :]).then_inc(stored[u % 2], 16)
                            load(i + AHEAD, u + AHEAD)
                    for k in range(2):
                        sp.wait_ge(stored[k], 16 + 16 * SLOTS // 2)
                    for u in range(AHEAD):
                        sp.wait_ge(w_in_ring[u], 32 * (SLOTS // 4 + 1))

                @block.gpsimd
                def _(pool):
                    def gather(i, u, copied, count):
                        nc.gpsimd.tensor_copy(idc[u % 2][:, :], idx[:, bass.ds(i, 1)]).then_inc(copied, 1)
                        pool.wait_ge(e_step, 1)
                        pool.wait_ge(copied, count)
                        pool.indirect_dma_start(xg[u % 2][:, :], None, h2_d,
                                                bass.IndirectOffsetOnAxis(idc[u % 2][:, :], 0)).then_inc(gathered[u % 2], 16)

                    gather(0, 0, idx_first, 1)
                    gather(1, 1, idx_first, 2)
                    with pool.Fori(0, SLOTS // 4) as j:
                        for u in range(4):
                            i = 4 * j + u
                            pool.wait_ge(x_turned, i + 1)
                            gather(i + 2, u, idx_set, i + 1)
                    for k in range(2):
                        pool.wait_ge(gathered[k], 16 * (SLOTS // 2 + 1))

                @block.tensor
                def _(pe):
                    def turn_x(v, count):
                        pe.wait_ge(gathered[v], count)
                        for k in range(KH):
                            last = nc.tensor.transpose(XTB[v][:, k * P:(k + 1) * P], xg[v][:, k * P:(k + 1) * P],
                                                       ident[:, :])
                        last.then_inc(x_turned, 1)

                    turn_x(0, 16)
                    with pe.Fori(0, SLOTS // 4) as j:
                        for u in range(4):
                            i = 4 * j + u
                            r = pe.value_load(tab_r[0:1, bass.ds(i + 1, 1)], min_val=0, max_val=RING - 1)
                            rp = pe.value_load(tab_r[0:1, bass.ds(i, 1)], min_val=0, max_val=RING - 1)
                            pe.wait_ge(w_in_ring[u], 32 * j + 32)
                            pe.wait_ge(x_ready, i + 1)
                            pe.wait_ge(gu_read, i + 1)
                            for k in range(KH):
                                last = nc.tensor.matmul(GUB[u % 2][:, :], xT[u % 2][:, k * P:(k + 1) * P],
                                                        wr[:, bass.ds(r, 1), k * 512:(k + 1) * 512]
                                                        .rearrange("p o w -> p (o w)"),
                                                        start=(k == 0), stop=(k == KH - 1))
                            last.then_inc(gu_made, 1)
                            v = (u + 1) % 2
                            pe.wait_ge(act_made, i + 1)
                            pe.wait_ge(act_ready, i + 1)
                            for k in range(2):
                                last = nc.tensor.transpose(ATB[v][:, k * P:(k + 1) * P], ac[v][:, k * P:(k + 1) * P],
                                                           ident[:, :])
                            last.then_inc(act_turned, 1)
                            turn_x(v, 32 * j + 16 * ((u + 1) // 2 + 1))
                            pe.wait_ge(act_ready, i + 3)
                            pe.wait_ge(y_read, i + 1)
                            for k in range(2):
                                last = nc.tensor.matmul(YB[v][:, :], aT[v][:, k * P:(k + 1) * P],
                                                        wr[:, bass.ds(rp, 1), 2048 + k * 512:2048 + (k + 1) * 512]
                                                        .rearrange("p o w -> p (o w)"), start=(k == 0), stop=(k == 1))
                            last.then_inc(y_made, 1)

                @block.scalar
                def _(act):
                    def x_out(i, u):
                        act.wait_ge(x_turned, i + 1)
                        nc.scalar.activation(xT[u % 2][:, :], XTB[u % 2][:, :], ACT.Copy).then_inc(x_ready, 1)

                    x_out(0, 0)
                    with act.Fori(0, SLOTS // 4) as j:
                        for u in range(4):
                            i = 4 * j + u
                            v = (u + 1) % 2
                            act.wait_ge(act_turned, i + 1)
                            nc.scalar.activation(aT[v][:, :], ATB[v][:, 0:2 * P], ACT.Copy).then_inc(act_ready, 1)
                            act.wait_ge(clamped, i + 1)
                            nc.scalar.activation(sg[u % 2][:, :], gu[u % 2][:, 0:FF], ACT.Sigmoid,
                                                 scale=1.702).then_inc(sig_made, 1)
                            x_out(i + 1, u + 1)

                @block.vector
                def _(dve):
                    for k in range(2):
                        nc.vector.memset(yo[k][:, :], 0.0).then_inc(stored[k], 16)
                    nc.vector.memset(ac[0][:, :], 0.0).then_inc(gu_read, 2)
                    nc.vector.memset(aT[1][:, :], 0.0).then_inc(act_ready, 2)
                    nc.vector.memset(aT[0][:, :], 0.0).then_inc(y_read, 2)
                    nc.vector.memset(ac[1][:, :], 0.0).then_inc(act_made, 1)
                    nc.vector.memset(sg[0][:, :], 0.0).then_inc(e_step, 1)
                    with dve.Fori(0, SLOTS // 4) as j:
                        for u in range(4):
                            i = 4 * j + u
                            v = (u + 1) % 2
                            r = dve.value_load(tab_r[0:1, bass.ds(i + 1, 1)], min_val=0, max_val=RING - 1)
                            rp = dve.value_load(tab_r[0:1, bass.ds(i, 1)], min_val=0, max_val=RING - 1)
                            c = u % 2
                            dve.wait_ge(gu_made, i + 1)
                            ins = nc.vector.tensor_tensor(gu[c][:, :], GUB[c][:, :],
                                                          br[:, bass.ds(r, 1), 0:512].rearrange("p o w -> p (o w)"), ALU.add)
                            ins.then_inc(gu_read, 1)
                            dve.wait_ge(gu_read, i + 3)
                            nc.vector.tensor_scalar(gu[c][:, 0:FF], gu[c][:, 0:FF], 7.0, None, ALU.min).then_inc(clamped, 1)
                            nc.vector.tensor_scalar(gu[c][:, FF:], gu[c][:, FF:], 7.0, -7.0, ALU.min,
                                                    ALU.max).then_inc(e_step, 1)
                            dve.wait_ge(sig_made, i + 1)
                            dve.wait_ge(clamped, i + 1)
                            nc.vector.tensor_tensor(sg[c][:, :], sg[c][:, :], gu[c][:, 0:FF], ALU.mult).then_inc(e_step, 1)
                            dve.wait_ge(e_step, 2 * i + 3)
                            nc.vector.scalar_tensor_tensor(out=ac[c][:, :], in0=gu[c][:, FF:], scalar=1.0, in1=sg[c][:, :],
                                                           op0=ALU.add, op1=ALU.mult).then_inc(act_made, 1)
                            dve.wait_ge(y_made, i + 1)
                            dve.wait_ge(stored[c], 32 * j + 16 * (u // 2 + 1))
                            nc.vector.tensor_tensor(yo[c][:, :], YB[v][:, :],
                                                    br[:, bass.ds(rp, 1), 512:1024].rearrange("p o w -> p (o w)"),
                                                    ALU.add).then_inc(y_read, 1)

        with ExitStack() as cb:
            def kb(name, shape, dt=F32):
                return sb(name, shape, dt, cb)

            yk = [kb(f"yk{i}", [P, TOPK, HID]) for i in range(2)]
            xr = [kb(f"xr{i}", [P, HID]) for i in range(2)]
            d4 = [kb(f"d4{i}", [P, TOPK], I32) for i in range(2)]
            w4 = [kb(f"w4{i}", [P, TOPK]) for i in range(2)]
            ac2 = [kb(f"ac2{i}", [P, HID]) for i in range(2)]
            gb = kb("gb", [P, BATCH, HID])
            c_gb = sem("c_gb")
            c_d4 = sem("c_d4")
            c_y = [sem(f"c_y{i}") for i in range(2)]
            c_x = [sem(f"c_x{i}") for i in range(2)]
            c_out = [sem(f"c_out{i}") for i in range(2)]
            c_done = sem("c_done")
            c_step = sem("c_step")
            with nc.Block() as block:
                @block.gpsimd
                def _(pool):
                    with pool.Fori(0, BATCH) as b:
                        for u in range(NQ):
                            t = NQ * b + u
                            pool.wait_ge(c_done, t + 1)
                            nc.gpsimd.tensor_copy(d4[u % 2][:, :], dest[:, bass.ds(t * TOPK, TOPK)]).then_inc(c_d4, 1)
                            pool.wait_ge(c_gb, 16 * BATCH)
                            pool.wait_ge(c_d4, t + 1)
                            for k in range(TOPK):
                                pool.indirect_dma_start(yk[u % 2][:, k, :], None, ys_d,
                                                        bass.IndirectOffsetOnAxis(d4[u % 2][:, k:k + 1], 0)) \
                                    .then_inc(c_y[u % 2], 16)

                @block.sync
                def _(sp):
                    for b in range(BATCH):
                        sp.dma_start(gb[:, b, :], mod_d[b:b + 1, 5 * HID:6 * HID].broadcast_to([P, HID])).then_inc(c_gb, 16)
                    with sp.Fori(0, BATCH) as b:
                        for u in range(NQ):
                            t = NQ * b + u
                            sp.wait_ge(c_done, t + 1)
                            sp.dma_start(xr[u % 2][:, :], x2_d[bass.ds(t * P, P), :]).then_inc(c_x[u % 2], 16)
                    for k in range(2):
                        sp.wait_ge(c_out[k], 16 + 16 * NT // 2)

                @block.scalar
                def _(act):
                    with act.Fori(0, BATCH) as b:
                        for u in range(NQ):
                            act.wait_ge(c_done, NQ * b + u + 3)
                            act.dma_start(out[bass.ds(b, 1), u * P:(u + 1) * P, :].rearrange("o p d -> (o p) d"),
                                          ac2[u % 2][:, :]).then_inc(c_out[u % 2], 16)

                @block.vector
                def _(dve):
                    nc.vector.memset(w4[0][:, :], 0.0).then_inc(c_done, 2)
                    for k in range(2):
                        nc.vector.memset(ac2[k][:, :], 0.0).then_inc(c_out[k], 16)
                    dve.wait_ge(c_done, 2)
                    dve.wait_ge(c_out[1], 16)
                    dve.wait_ge(c_gb, 16 * BATCH)
                    with dve.Fori(0, BATCH) as b:
                        for u in range(NQ):
                            t = NQ * b + u
                            c = u % 2
                            n = [0]

                            def link(instruction):
                                n[0] += 1
                                instruction.then_inc(c_step, 1)
                                dve.wait_ge(c_step, t * 6 + n[0])

                            link(nc.vector.tensor_copy(w4[c][:, :], wts[:, bass.ds(t * TOPK, TOPK)]))
                            dve.wait_ge(c_y[c], 128 * b + 64 * (u // 2 + 1))
                            dve.wait_ge(c_out[c], 32 * b + 16 * (u // 2 + 1))
                            link(nc.vector.tensor_scalar(ac2[c][:, :], yk[c][:, 0, :], w4[c][:, 0:1], None, ALU.mult))
                            for k in range(1, TOPK):
                                link(nc.vector.scalar_tensor_tensor(out=ac2[c][:, :], in0=yk[c][:, k, :],
                                                                    scalar=w4[c][:, k:k + 1], in1=ac2[c][:, :],
                                                                    op0=ALU.mult, op1=ALU.add))
                            link(nc.vector.tensor_tensor(ac2[c][:, :], ac2[c][:, :],
                                                         gb[:, bass.ds(b, 1), :].rearrange("p o d -> p (o d)"), ALU.mult))
                            dve.wait_ge(c_x[c], 32 * b + 16 * (u // 2 + 1))
                            nc.vector.tensor_tensor(ac2[c][:, :], ac2[c][:, :], xr[c][:, :], ALU.add).then_inc(c_done, 1)


def layouts(i):
    f = {k[3:]: np.asarray(v) for k, v in i.items()}

    def rows(a):
        return a.reshape(-1, P, *a.shape[1:]).swapaxes(0, 1)

    c_rows = rows(f["c"].T)
    wmod = f["wmod"].reshape(KH, P, 6, HID).transpose(2, 1, 0, 3)
    conv = np.concatenate([f["attn_conv_w"], f["attn_conv_b"][:, None]], axis=1)
    vecs = np.concatenate([f["attn_dt_bias"], f["attn_A_log"], f["attn_D"], f["ffn_gate_b"]])[None]
    gate_up = np.concatenate([f["ffn_w_gate"], f["ffn_w_up"]], axis=2)
    gate_up = gate_up.reshape(EXP, KH, P, 2 * FF).transpose(0, 2, 1, 3).reshape(EXP, P, KH * 2 * FF)
    down = f["ffn_w_down"].reshape(EXP, 2, P, HID).transpose(0, 2, 1, 3).reshape(EXP, P, 2 * HID)
    return {
        "x": f["attn_hidden_states"], "cT": c_rows, "wmod": wmod, "w_in": rows(f["attn_W_in"]),
        "w_out": rows(f["attn_W_out"]), "convp": rows(conv), "vecs": vecs, "mup": f["attn_mup_vector"][None],
        "nw": f["attn_norm_w"].reshape(8, P).T, "gwT": rows(f["ffn_gate_w"].T),
        "wexp": np.concatenate([gate_up, down], axis=2),
        "bexp": np.concatenate([f["ffn_b_gate"], f["ffn_b_up"], f["ffn_b_down"]], axis=1),
    }


def kernel(**inputs):
    import concourse.bacc as _bacc
    from concourse.bass_utils import run_bass_kernel_spmd as _run

    nc = _bacc.Bacc("TRN2", target_bir_lowering=False, num_devices=1)
    arrays, args = {}, []
    for name, a in layouts(inputs).items():
        a = np.ascontiguousarray(a)
        arrays[f"in_{name}"] = a
        args.append(nc.dram_tensor(f"in_{name}", a.shape, mybir.dt.from_np(a.dtype), kind="ExternalInput").ap())
    out = nc.dram_tensor("out_0", (BATCH, SEQ, HID), F32, kind="ExternalOutput").ap()
    build(nc, args, out)
    return _run(nc, [arrays], core_ids=[0]).results[0]["out_0"]
```

```python
from contextlib import ExitStack

import numpy as np

import concourse.bass as bass
from concourse import mybir

F32 = mybir.dt.float32
BF16 = mybir.dt.bfloat16
I32 = mybir.dt.int32
U32 = mybir.dt.uint32
ALU = mybir.AluOpType
ACT = mybir.ActivationFunctionType
AX = mybir.AxisListType

P = 128
BATCH, SEQ, HID = 4, 512, 512
KH = HID // P
DI = 1024
HEADS, HD = 64, 16
STATE = 128
TAPS = 4
CONV = DI + 2 * STATE
NCH = CONV // P
PROJ = 2 * DI + 2 * STATE + HEADS
NQ = SEQ // P
NT = BATCH * NQ
EXP, TOPK, FF = 32, 4, 256
SLOTS = 96
RING = 4
AHEAD = RING - 1
WEXP = KH * 2 * FF + 2 * HID
EPS = 1e-5
GRP = 8
NG = HEADS // GRP
DEC = 3 + 12
ROWS = DEC + P // 2
FAR = -32768.0
LOWEST = -88.0
CH = [8, 9, 0, 1, 2, 3, 4, 5, 6, 7]
TURNED = [0] + list(range(2, NCH))


def plan_banks():
    order = [("h", k) for k in range(KH)] + ["dt"] + [("ch", n) for n in range(4)] + ["cum", ("ch", 4), "cumT"]
    order += [("turn", 0), ("ch", 5)]
    for n in range(2, 6):
        order += [("turn", n), ("ch", n + 4)]
    for n in range(6, 10):
        order += [("turn", n), ("z", n - 6)]
    order += [("z", j) for j in range(4, 2 * NQ)]
    uses = [0] * 8
    place = {}
    for i, name in enumerate(order):
        uses[i % 8] += 1
        place[name] = (i % 8, uses[i % 8])
    stage_a = list(uses)
    for q in range(NQ):
        for half in range(2):
            uses[4 + half] += 1
            place[("y", q, half)] = (4 + half, uses[4 + half])
    for i, name in enumerate(w for q in range(-1, NQ + 1) for a in range(NG) for w in work_at(q, a)):
        uses[6 + i % 2] += 1
        place[name] = (6 + i % 2, uses[6 + i % 2])
    return order, place, stage_a


def work_at(q, a):
    if a == 0 and 0 < q < NQ:
        return [("inter", q, 0), ("inter", q, 1)]
    if a == 1 and q > 0:
        return [("ss", q - 1), ("wo", q - 1)]
    if a == 3 and 0 <= q < NQ - 1:
        return [("u", q, 0), ("u", q, 1)]
    if a == 4 and q < NQ - 1:
        return [("cb", q + 1)]
    if a == 5 and q > 0:
        return [("h2T", q - 1)]
    if a == 6 and q > 0:
        return [("lg", q - 1)]
    if a == 7 and 0 <= q < NQ - 1:
        return [("ex", q + 1, 0), ("ex", q + 1, 1)]
    return []


def build(nc, ins, out):
    x, cT, wmod, w_in, w_out, convp, vecs, mup, nw, dcol, gwT, wexp, bexp = ins
    order_a, place, stage_a = plan_banks()

    mod_d = nc.dram_tensor("mod_d", [BATCH, 6 * HID], F32, kind="Internal").ap()
    cum_d = nc.dram_tensor("cum_d", [HEADS, 3, SEQ], BF16, kind="Internal").ap()
    x2_d = nc.dram_tensor("x2_d", [NT * P, HID], F32, kind="Internal").ap()
    h2_d = nc.dram_tensor("h2_d", [NT * P, HID], F32, kind="Internal").ap()

    with ExitStack() as whole:
        def sb(name, shape, dt=F32, ctx=whole):
            return ctx.enter_context(nc.sbuf_tensor(name, shape, dt))

        def sem(name):
            return whole.enter_context(nc.semaphore(name))

        bank = [whole.enter_context(nc.psum_tensor(f"bank{i}", [P, 512], F32)) for i in range(8)]
        ident = sb("ident", [P, P])
        upto = sb("upto", [P, P])
        ones = sb("ones", [P, P])
        top_v = sb("top_v", [P, NT, TOPK])
        top_i = sb("top_i", [P, NT, TOPK], U32)
        mixer(nc, place, order_a, stage_a, x, cT, wmod, w_in, w_out, convp, vecs, mup, nw, dcol, gwT,
              mod_d, cum_d, x2_d, h2_d, bank, ident, upto, ones, top_v, top_i)
        experts(nc, wexp, bexp, mod_d, x2_d, h2_d, out, bank, ident, upto, ones, top_v, top_i)


def mixer(nc, place, order_a, stage_a, x, cT, wmod, w_in, w_out, convp, vecs, mup, nw, dcol, gwT,
          mod_d, cum_d, x2_d, h2_d, bank, ident, upto, ones, top_v, top_i):
    with ExitStack() as ctx:
        def sb(name, shape, dt=F32):
            return ctx.enter_context(nc.sbuf_tensor(name, shape, dt))

        def sem(name):
            return ctx.enter_context(nc.semaphore(name))

        win = sb("win", [P, KH, PROJ])
        wout = sb("wout", [P, 8, HID])
        gw = sb("gw", [P, KH, EXP])
        cvp = sb("cvp", [P, NCH, TAPS + 1])
        nwc = sb("nwc", [P, 8])
        dc = sb("dc", [P, 8])
        vrow = sb("vrow", [P, 2 * HEADS + EXP])
        modc = sb("modc", [P, 8, BATCH])
        modb = sb("modb", [P, 8])
        sct = sb("sct", [P, KH, BATCH])
        x_in = sb("x_in", [P, NQ, HID])
        hT = sb("hT", [P, KH, SEQ])
        pre = sb("pre", [P, 4, SEQ + TAPS - 1])
        cv = sb("cv", [P, 4, SEQ])
        BT = sb("BT", [P, SEQ])
        CT = sb("CT", [P, SEQ])
        x_t = sb("x_t", [P, NQ, DI])
        B_t = sb("B_t", [P, NQ - 1, STATE])
        Dx = sb("Dx", [P, 8, SEQ])
        zs = sb("zs", [P, 8, SEQ])
        dt = sb("dt", [P, NQ * HEADS])
        edec = sb("edec", [P, NQ * HEADS])
        etot = sb("etot", [P, NQ * HEADS])
        parts = sb("parts", [HEADS, 3, SEQ], BF16)
        ga_b = sb("ga_b", [P, HID])
        cb_b = sb("cb_b", [P, HID])
        sb_b = sb("sb_b", [P, HID])
        mv = sb("mv", [ROWS, 2, 32 * P], BF16)
        st = sb("st", [ROWS, 2, 8 * P], BF16)
        head_of = sb("head_of", [HEADS, 4 * P], BF16)
        state = sb("state", [P, DI])
        yg = sb("yg", [P, 2, 8, P])
        xdt = [sb(f"xdt{i}", [P, HEADS, 2 * HD]) for i in range(2)]
        cbm = [sb(f"cbm{i}", [P, P]) for i in range(2)]
        lg = sb("lg", [P, EXP])
        bnst = sb("bnst", [P, NQ, 6])
        mv4 = sb("mv4", [P, NQ, 2])
        rs4 = sb("rs4", [P, NQ])
        mhalf = sb("mhalf", [P, NQ])
        ss = sb("ss", [P, 1])
        rms = sb("rms", [P, 1])
        bn2 = sb("bn2", [P, 6])
        mv2 = sb("mv2", [P, 2])
        rs2 = sb("rs2", [P, 1])
        tv = sb("tv", [P, NQ, 8])
        ti = sb("ti", [P, NQ, 8], U32)

        M = [pre[:, :, :].rearrange("p a t -> p (a t)")[:, i * GRP * P:(i + 1) * GRP * P] for i in range(2)]
        M += [cv[:, 0:2, :].rearrange("p a t -> p (a t)")]
        ecx = cv[:, 2:4, :].rearrange("p a t -> p (a t)")
        h2T = hT[:, 0, :].rearrange("p (k t) -> p k t", t=P)
        x2 = hT[:, 1, :]
        before = cbm[0]
        xw = hT[:, 2:4, :].rearrange("p a t -> p (a t)")
        flat = yg[:, :, :, :].rearrange("p i j t -> p (i j t)")
        tmp = [flat[:, 256 * i:256 * (i + 1)] for i in range(6)]
        cums = tmp[5]
        rest = flat[0:HEADS, 3 * SEQ:4 * SEQ]
        modr = Dx[0:BATCH, 0:6, :].rearrange("p a b -> p (a b)")
        wm = [x_t[:, 2 * i:2 * i + 2, :].rearrange("p a (k n) -> p (a k) n", n=HID) for i in range(2)]
        mupb = zs[:, :, :].rearrange("p a b -> p (a b)")[:, 0:PROJ]

        s_const = sem("s_const")
        s_ld = sem("s_ld")
        s_wm = [sem("s_wm0"), sem("s_wm1")]
        s_silu = sem("s_silu")
        s_mod = sem("s_mod")
        s_row = sem("s_row")
        s_mup = sem("s_mup")
        s_expa = sem("s_expa")
        s_rows = sem("s_rows")
        s_modT = sem("s_modT")
        s_v = sem("s_v")

        with ExitStack() as setup:
          one_of_4 = setup.enter_context(nc.sbuf_tensor("one_of_4", [ROWS, 4, P], BF16))
          two_of_t = setup.enter_context(nc.sbuf_tensor("two_of_t", [ROWS, 4, P], BF16))
          with nc.Block() as block:
              @block.sync
              def _(sp):
                  sp.dma_start(sct[:, :, :], cT).then_inc(s_ld, 16)
                  sp.dma_start(vrow[:, :], vecs[0:1, :].broadcast_to([P, 2 * HEADS + EXP])).then_inc(s_ld, 16)
                  for j in range(6):
                      if j >= 2:
                          sp.wait_ge(s_mod, j - 1)
                      sp.dma_start(wm[j % 2], wmod[j]).then_inc(s_wm[j % 2], 16)
                  sp.dma_start(x_in[:, :, :], x[0].rearrange("(q p) d -> p q d", p=P)).then_inc(s_rows, 16)
                  sp.wait_ge(s_row, 1)
                  sp.dma_start(mod_d[:, :], modr).then_inc(s_rows, 16)
                  sp.wait_ge(s_rows, 32)

              @block.scalar
              def _(act):
                  act.dma_start(mupb, mup[0:1, :].broadcast_to([P, PROJ])).then_inc(s_ld, 16)
                  act.dma_start(nwc[:, :], nw).then_inc(s_ld, 16)
                  act.dma_start(dc[:, :], dcol).then_inc(s_ld, 16)
                  act.dma_start(gw[:, :, :], gwT).then_inc(s_ld, 16)
                  act.dma_start(cvp[:, :, :], convp).then_inc(s_ld, 16)
                  act.dma_start(win[:, :, :], w_in).then_inc(s_ld, 16)
                  act.dma_start(wout[:, :, :], w_out).then_inc(s_ld, 16)
                  act.wait_ge(s_ld, 16 * 9)
                  nc.scalar.activation(sct[:, :, :], sct[:, :, :], ACT.Silu).then_inc(s_silu, 1)
                  nc.scalar.activation(vrow[:, HEADS:2 * HEADS], vrow[:, HEADS:2 * HEADS], ACT.Exp).then_inc(s_expa, 1)

              @block.gpsimd
              def _(pool):
                  nc.gpsimd.memset(ones[:, :], 1.0).then_inc(s_const, 1)
                  nc.gpsimd.memset(mhalf[:, :], -0.5).then_inc(s_const, 1)
                  nc.gpsimd.memset(one_of_4[:, :, :], -1.0).then_inc(s_const, 1)
                  nc.gpsimd.memset(st[:, :, :], 1.0).then_inc(s_const, 1)
                  nc.gpsimd.memset(two_of_t[:, :, :], FAR).then_inc(s_const, 1)
                  pool.wait_ge(s_const, 5)
                  nc.gpsimd.affine_select(out=upto[:, :], in_=ones[:, :], compare_op=ALU.is_ge, fill=0.0, base=0,
                                          pattern=[[1, P]], channel_multiplier=-1).then_inc(s_const, 1)
                  nc.gpsimd.affine_select(out=before[:, :], in_=ones[:, :], compare_op=ALU.is_ge, fill=0.0, base=-1,
                                          pattern=[[1, P]], channel_multiplier=-1).then_inc(s_const, 1)
                  def keep(tile, pattern, base, by_row, op=ALU.is_ge):
                      nc.gpsimd.affine_select(out=tile, in_=tile, compare_op=op, fill=0.0, base=base, pattern=pattern,
                                              channel_multiplier=by_row).then_inc(s_const, 1)

                  keep(st[:, :, :].rearrange("p f (g s) -> p (f g) s", s=P), [[0, 16], [1, P]], 2 * (DEC - 1), -2)
                  keep(two_of_t[:, :, :], [[0, 4], [1, P]], 2 * DEC, -2)
                  pool.wait_ge(s_const, 9)
                  keep(two_of_t[:, :, :], [[0, 4], [-1, P]], 1 - 2 * DEC, 2)
                  keep(one_of_4[:, :, :], [[0, 4], [0, P]], DEC - 1, -1)
                  for n, off in enumerate(o for o in range(-3, 12) if o % 4):
                      pool.wait_ge(s_const, 11 + n)
                      keep(one_of_4[:, :, :], [[-1, 4], [0, P]], -3 - off, 1, ALU.not_equal)
                  pool.wait_ge(s_const, 23)
                  nc.gpsimd.tensor_tensor(one_of_4[:, :, :], one_of_4[:, :, :], two_of_t[:, :, :],
                                          ALU.add).then_inc(s_const, 1)
                  nc.gpsimd.tensor_tensor(ident[:, :], upto[:, :], before[:, :], ALU.subtract).then_inc(s_const, 1)
                  for i in range(2):
                      nc.gpsimd.memset(xdt[i][:, :, :], 0.0).then_inc(s_const, 1)

              @block.tensor
              def _(pe):
                  pe.wait_ge(s_silu, 1)
                  for j in range(6):
                      pe.wait_ge(s_wm[j % 2], 16 * (j // 2 + 1))
                      for k in range(KH):
                          last = nc.tensor.matmul(bank[j][0:BATCH, :], sct[:, k, :], wm[j % 2][:, k, :],
                                                  start=(k == 0), stop=(k == KH - 1))
                      last.then_inc(s_mod, 1)
                  pe.wait_ge(s_row, 1)
                  pe.wait_ge(s_const, 27)
                  for j in range(8):
                      last = nc.tensor.transpose(bank[6][:, 4 * j:4 * j + 4], modr[:, P * j:P * (j + 1)],
                                                 ident[0:BATCH, 0:BATCH])
                  last.then_inc(s_modT, 1)

              @block.vector
              def _(dve):
                  steps = [0]

                  def link(instruction):
                      steps[0] += 1
                      instruction.then_inc(s_v, 1)
                      dve.wait_ge(s_v, steps[0])

                  dve.wait_ge(s_ld, 16 * 9)
                  for k in range(KH):
                      nc.vector.tensor_tensor(win[:, k, :], win[:, k, :], mupb, ALU.mult).then_inc(s_mup, 1)
                  dve.wait_ge(s_expa, 1)
                  nc.vector.tensor_scalar(vrow[:, HEADS:2 * HEADS], vrow[:, HEADS:2 * HEADS], -1.0, None,
                                          ALU.mult).then_inc(s_mup, 1)
                  for k in range(8):
                      nc.vector.tensor_scalar(wout[:, k, :], wout[:, k, :], nwc[:, k:k + 1], None,
                                              ALU.mult).then_inc(s_mup, 1)
                  sgn = x2[0:BATCH, :]
                  for j in range(6):
                      row = modr[:, j * HID:(j + 1) * HID]
                      dve.wait_ge(s_mod, j + 1)
                      if j in (0, 3):
                          link(nc.vector.tensor_copy(row, bank[j][0:BATCH, :]))
                      elif j in (1, 4):
                          link(nc.vector.tensor_scalar(row, bank[j][0:BATCH, :], 1.0, None, ALU.add))
                      else:
                          link(nc.vector.tensor_scalar(sgn, bank[j][0:BATCH, :], 0.0, 2.0, ALU.is_ge, ALU.mult))
                          link(nc.vector.tensor_copy(row, bank[j][0:BATCH, :]))
                          link(nc.vector.scalar_tensor_tensor(out=row, in0=bank[j][0:BATCH, :], scalar=-1.0, in1=row,
                                                              op0=ALU.mult, op1=ALU.max))
                          link(nc.vector.tensor_scalar(row, row, 0.25, None, ALU.max))
                          last = nc.vector.scalar_tensor_tensor(out=row, in0=sgn, scalar=-1.0, in1=row,
                                                                op0=ALU.add, op1=ALU.mult)
                          if j == 5:
                              last.then_inc(s_row, 1)
                          else:
                              link(last)
                  dve.wait_ge(s_const, 27)
                  nc.vector.tensor_copy(mv[:, :, :].rearrange("p f (g c) -> p (f g) c", c=4 * P),
                                        one_of_4[:, :, :].rearrange("p (o j) t -> p o (j t)", o=1)
                                        .broadcast_to([ROWS, 16, 4 * P])).then_inc(s_mup, 1)
                  dve.wait_ge(s_modT, 1)
                  for r in range(0, HEADS, 32):
                      link(nc.vector.tensor_copy(head_of[r:r + 32, :].rearrange("p (h c) -> p h c", c=HD),
                                                 ident[r:r + 32, r:r + 32].rearrange("p (h o) -> p h o", o=1)
                                                 .broadcast_to([32, 32, HD])))
                  link(nc.vector.tensor_copy(modc[:, :, :].rearrange("p a b -> p (a b)"), bank[6][:, 0:32]))

        h2 = sb("h2", [P, HID])

        full = [sem(f"full{i}") for i in range(8)]
        free = [sem(f"free{i}") for i in range(8)]
        names = """s_a s_agg s_arg s_bc s_conv s_cumd s_dtv s_dx s_ecx s_exp s_exps s_g s_h2 s_heads
                   s_lg s_m s_modb s_parts s_pl2 s_pool s_pre s_rms s_rs2 s_rstd s_sh
                   s_silu2 s_std s_step s_sx s_u s_x2b s_xdt s_xn s_xn2 s_xres
                   s_xw s_yacc""".split()
        S = {n: sem(n) for n in names}
        s_xin = sem("s_xin")
        rows_in = [sem(f"rows_in{i}") for i in range(2)]
        per_loop = full + free + list(S.values()) + rows_in + [s_xin]

        def b3(ap, n):
            return ap.rearrange("p (h o) -> p h o", o=1).broadcast_to([P, ap.shape[1], n])

        def h3(ap):
            return ap.rearrange("p (h d) -> p h d", d=HD)

        def read(eng, name):
            eng.wait_ge(free[place[name][0]], place[name][1])

        with nc.Fori(0, BATCH) as b:
            with nc.Block() as block:
                @block.sync
                def _(sp):
                    for j, dst in ((2, ga_b), (4, cb_b), (3, sb_b)):
                        sp.dma_start(dst[:, :], mod_d[bass.ds(b, 1), j * HID:(j + 1) * HID]
                                     .broadcast_to([P, HID])).then_inc(S["s_bc"], 16)
                    sp.wait_ge(S["s_parts"], 3)
                    sp.dma_start(cum_d[:, :, :], parts[:, :, :]).then_inc(S["s_cumd"], 16)
                    sp.wait_ge(S["s_cumd"], 16)
                    cq = cum_d.rearrange("(f g j) i (q t) -> q f i j g t", f=2, j=4, t=P)
                    cm = cum_d.rearrange("(f h) i (q t) -> q f i h t", f=2, t=P)

                    def decay_rows(q, f):
                        n = 2 * q + f
                        if q:
                            sp.wait_ge(S["s_arg"], 8 * (q - 1) + 4 * f + 4)
                        sp.dma_start(mv[0:3, f, :].rearrange("i (h t) -> i h t", t=P), cm[q, f]).then_inc(rows_in[f], 16)
                        for i in range(3):
                            sp.dma_start(st[3 + 4 * i:7 + 4 * i, f, :].rearrange("j (g t) -> j g t", t=P),
                                         cq[q, f, i]).then_inc(rows_in[f], 16)

                    decay_rows(0, 0)
                    decay_rows(0, 1)
                    read(sp, ("h", KH - 1))
                    sp.dma_start(x_in[:, :, :], x[bass.ds((b + 1) % BATCH, 1)]
                                 .rearrange("o (q p) d -> p (o q) d", p=P)).then_inc(s_xin, 16)

                    def residual(q):
                        if q:
                            sp.wait_ge(S["s_sx"], 16 * q)
                            sp.wait_ge(S["s_xn2"], q)
                        else:
                            k, n = place[("z", 2 * NQ - 1)]
                            sp.wait_ge(full[k], n)
                        sp.dma_start(x2, x[bass.ds(b, 1), q * P:(q + 1) * P, :]
                                     .rearrange("o p d -> (o p) d")).then_inc(S["s_xres"], 16)

                    def store(q):
                        sp.wait_ge(S["s_x2b"], q + 1)
                        sp.dma_start(x2_d[bass.ds(b * SEQ + q * P, P), :], x2[:, :]).then_inc(S["s_sx"], 16)
                        sp.wait_ge(S["s_h2"], q + 1)
                        sp.dma_start(h2_d[bass.ds(b * SEQ + q * P, P), :], h2[:, :]).then_inc(S["s_sh"], 16)

                    residual(0)
                    for q in range(NQ):
                        if q + 1 < NQ:
                            decay_rows(q + 1, 0)
                            decay_rows(q + 1, 1)
                        if q:
                            store(q - 1)
                            residual(q)
                    store(NQ - 1)
                    sp.wait_ge(S["s_sx"], 16 * NQ)
                    sp.wait_ge(S["s_sh"], 16 * NQ)
                    sp.wait_ge(s_xin, 16)

                @block.tensor
                def _(pe):
                    def open_bank(name):
                        k, n = place[name]
                        if n > 1:
                            pe.wait_ge(free[k], n - 1)
                        return bank[k]

                    def close_bank(name, last):
                        last.then_inc(full[place[name][0]], 1)

                    for q in range(NQ):
                        pe.wait_ge(S["s_xn"], q + 1)
                        for k in range(KH):
                            last = nc.tensor.transpose(bank[k][:, q * P:(q + 1) * P], x_in[:, q, k * P:(k + 1) * P],
                                                       ident[:, :])
                            if q == NQ - 1:
                                close_bank(("h", k), last)
                    for k in range(KH):
                        read(pe, ("h", k))
                    for name in order_a[KH:]:
                        kind = name if isinstance(name, str) else name[0]
                        t = open_bank(name)
                        if kind == "dt":
                            for q in range(NQ):
                                for k in range(KH):
                                    last = nc.tensor.matmul(t[:, q * HEADS:(q + 1) * HEADS],
                                                            hT[:, k, q * P:(q + 1) * P], win[:, k, PROJ - HEADS:PROJ],
                                                            start=(k == 0), stop=(k == KH - 1))
                        elif kind == "ch":
                            c0 = DI + CH[name[1]] * P
                            for k in range(KH):
                                last = nc.tensor.matmul(t[:, :], win[:, k, c0:c0 + P], hT[:, k, :],
                                                        start=(k == 0), stop=(k == KH - 1))
                        elif kind == "cum":
                            pe.wait_ge(S["s_a"], 1)
                            nc.tensor.matmul(t[:, 0:256], upto[:, :], tmp[0], start=True, stop=True)
                            last = nc.tensor.matmul(t[:, 256:512], ones[:, :], tmp[0], start=True, stop=True)
                        elif kind == "cumT":
                            read(pe, "cum")
                            for q in range(NQ):
                                last = nc.tensor.transpose(t[0:HEADS, q * P:(q + 1) * P],
                                                           cums[:, q * HEADS:(q + 1) * HEADS], ident[:, :])
                        elif kind == "turn":
                            n = name[1]
                            pe.wait_ge(S["s_silu2"], n + 1)
                            src = BT if n == 0 else cv[:, n % 4, :]
                            for q in range(NQ):
                                last = nc.tensor.transpose(t[:, q * P:(q + 1) * P], src[:, q * P:(q + 1) * P],
                                                           ident[:, :])
                        else:
                            c0 = name[1] * P
                            for k in range(KH):
                                last = nc.tensor.matmul(t[:, :], win[:, k, c0:c0 + P], hT[:, k, :],
                                                        start=(k == 0), stop=(k == KH - 1))
                        close_bank(name, last)

                    def arg(q, a):
                        n = q * NG + a
                        if n == 0:
                            for k in range(4):
                                pe.wait_ge(free[k], stage_a[k])
                        if n >= 2:
                            pe.wait_ge(S["s_exp"], n - 1)
                        if a % 4 == 0:
                            pe.wait_ge(rows_in[a // 4], 64 * (q + 1))
                        for i in range(2):
                            gl = (a % 4) * 2 + i
                            last = nc.tensor.matmul(bank[2 * (n % 2) + i][:, :], st[:, a // 4, gl * P:(gl + 1) * P],
                                                    mv[:, a // 4, gl * 512:(gl + 1) * 512], start=True, stop=True)
                        last.then_inc(S["s_arg"], 1)

                    def heads(q, a):
                        n = q * NG + a
                        name = ("y", q, a // 4)
                        if a % 4 == 0:
                            open_bank(name)
                        t = bank[place[name][0]][:, (a % 4) * P:(a % 4 + 1) * P]
                        if a == 0:
                            pe.wait_ge(S["s_xdt"], q + 1)
                        pe.wait_ge(S["s_m"], n + 1)
                        rows = xdt[q % 2][:, :, :].rearrange("p h c -> p (h c)")
                        for odd in range(2):
                            for pair in range(GRP // 2):
                                i = 2 * pair + odd
                                c = (a * GRP + i) * 2 * HD - odd * HD
                                last = nc.tensor.matmul(t[32 * pair:32 * (pair + 1), :], rows[:, c:c + 2 * HD],
                                                        M[n % 3][:, i * P:(i + 1) * P], start=(odd == 0),
                                                        stop=(odd == 1))
                        last.then_inc(S["s_heads"], 1)

                    def work(name):
                        t = open_bank(name)
                        kind, q = name[0], name[1]
                        if kind == "cb":
                            if q == 0:
                                read(pe, ("turn", NCH - 1))
                            last = nc.tensor.matmul(t[:, 0:P], BT[:, q * P:(q + 1) * P], CT[:, q * P:(q + 1) * P],
                                                    start=True, stop=True)
                        elif kind == "ex":
                            for j in range(4):
                                h = slice(32 * name[2], 32 * name[2] + 32)
                                for i in range(3):
                                    last = nc.tensor.matmul(t[:, j * P:(j + 1) * P], head_of[h, j * P:(j + 1) * P],
                                                            parts[h, i, q * P:(q + 1) * P],
                                                            start=(i == 0), stop=(i == 2))
                        elif kind == "inter":
                            for i in range(2 if name[2] == 0 else 0):
                                read(pe, ("u", q - 1, i))
                            for j in range(4):
                                c = (4 * name[2] + j) * P
                                last = nc.tensor.matmul(t[:, j * P:(j + 1) * P], state[:, c:c + P],
                                                        CT[:, q * P:(q + 1) * P], start=True, stop=True)
                        elif kind == "u":
                            pe.wait_ge(S["s_xw"], q + 1)
                            c = name[2] * 512
                            last = nc.tensor.matmul(t[:, :], B_t[:, q, :], xw[:, c:c + 512], start=True, stop=True)
                        elif kind == "ss":
                            pe.wait_ge(S["s_g"], 2 * (q + 1))
                            for k in range(8):
                                last = nc.tensor.matmul(t[:, 0:P], yg[:, q % 2, k, :], yg[:, q % 2, k, :],
                                                        start=(k == 0), stop=(k == 7))
                        elif kind == "wo":
                            for k in range(8):
                                last = nc.tensor.matmul(t[:, :], yg[:, q % 2, k, :], wout[:, k, :], start=(k == 0),
                                                        stop=(k == 7))
                        elif kind == "h2T":
                            pe.wait_ge(S["s_h2"], q + 1)
                            for k in range(KH):
                                last = nc.tensor.transpose(t[:, k * P:(k + 1) * P], h2[:, k * P:(k + 1) * P],
                                                           ident[:, :])
                        else:
                            read(pe, ("h2T", q))
                            for k in range(KH):
                                last = nc.tensor.matmul(t[:, 0:EXP], h2T[:, k, :], gw[:, k, :], start=(k == 0),
                                                        stop=(k == KH - 1))
                        close_bank(name, last)

                    for name in work_at(-1, 4):
                        work(name)
                    arg(0, 0)
                    arg(0, 1)
                    for q in range(NQ + 1):
                        for a in range(NG):
                            n = q * NG + a
                            if n + 2 < NQ * NG:
                                arg(*divmod(n + 2, NG))
                            if q < NQ:
                                heads(q, a)
                            for name in work_at(q, a):
                                work(name)

                @block.scalar
                def _(act):
                    def filled(name):
                        k, n = place[name]
                        act.wait_ge(full[k], n)
                        return bank[k]

                    act.wait_ge(S["s_modb"], 1)
                    for k in range(KH):
                        t = filled(("h", k))
                        ins = nc.scalar.activation(hT[:, k, :], t[:, :], ACT.Identity, bias=modb[:, k:k + 1],
                                                   scale=modb[:, 4 + k:5 + k])
                        ins.then_inc(free[k], 1)
                    act.wait_ge(S["s_dtv"], 1)
                    nc.scalar.activation(tmp[1], tmp[1], ACT.Exp, scale=-1.0).then_inc(S["s_u"], 1)

                    def to_pre(n):
                        if n >= 4:
                            act.wait_ge(S["s_conv"], n - 3)
                        t = filled(("ch", n))
                        k = place[("ch", n)][0]
                        nc.scalar.activation(pre[:, n % 4, TAPS - 1:], t[:, :], ACT.Copy).then_inc(free[k], 1)

                    for n in range(4):
                        to_pre(n)
                    t = filled("cum")
                    nc.scalar.activation(etot[:, :], t[:, 256:512], ACT.Exp).then_inc(S["s_exps"], 1)
                    read(act, "cum")
                    nc.scalar.activation(edec[:, :], edec[:, :], ACT.Exp).then_inc(S["s_exps"], 1)

                    def turned(n):
                        t = filled(("turn", n))
                        k = place[("turn", n)][0]
                        c = CH[n]
                        dst = x_t[:, :, c * P:(c + 1) * P] if n else B_t[:, :, :]
                        src = t[:, :].rearrange("p (q c) -> p q c", c=P)
                        nc.scalar.activation(dst, src if n else src[:, 0:NQ - 1, :], ACT.Copy) \
                            .then_inc(free[k], 1)

                    def times_d(n):
                        act.wait_ge(S["s_silu2"], n + 1)
                        c = CH[n]
                        nc.scalar.activation(Dx[:, c, :], cv[:, n % 4, :], ACT.Copy,
                                             scale=dc[:, c:c + 1]).then_inc(S["s_dx"], 1)

                    for n in range(NCH):
                        act.wait_ge(S["s_conv"], n + 1)
                        dst = {0: BT[:, :], 1: CT[:, :]}.get(n, cv[:, n % 4, :])
                        nc.scalar.activation(dst, cv[:, n % 4, :], ACT.Silu).then_inc(S["s_silu2"], 1)
                        if n + 4 < NCH:
                            to_pre(n + 4)
                        if n >= 3:
                            times_d(n - 1)
                        if n - 1 in TURNED:
                            turned(n - 1)
                    times_d(NCH - 1)
                    turned(NCH - 1)
                    for j in range(2 * NQ):
                        t = filled(("z", j))
                        k = place[("z", j)][0]
                        ins = nc.scalar.activation(zs[:, j, :], t[:, :], ACT.Silu)
                        ins.then_inc(free[k], 1)

                    for q in range(NQ + 1):
                        for a in range(NG):
                            if q < NQ:
                                n = q * NG + a
                                act.wait_ge(S["s_arg"], n + 1)
                                if n >= 3:
                                    act.wait_ge(S["s_heads"], n - 2)
                                for i in range(2):
                                    ins = nc.scalar.activation(M[n % 3][:, i * 512:(i + 1) * 512],
                                                               bank[2 * (n % 2) + i][:, :], ACT.Exp)
                                ins.then_inc(S["s_exp"], 1)
                            before_q, before_a = divmod(q * NG + a - 2, NG)
                            for name in work_at(before_q, before_a) if before_q >= 0 else []:
                                if name[0] == "ex":
                                    t = filled(name)
                                    i = name[2]
                                    if before_q > 0:
                                        read(act, ("inter", before_q, i))
                                    nc.scalar.activation(ecx[:, i * 512:(i + 1) * 512], t[:, :],
                                                         ACT.Exp).then_inc(free[place[name][0]], 1)
                                if name[0] == "h2T":
                                    t = filled(name)
                                    nc.scalar.activation(h2T[:, :, :].rearrange("p k t -> p (k t)"), t[:, :],
                                                         ACT.Copy).then_inc(free[place[name][0]], 1)

                @block.gpsimd
                def _(pool):
                    steps = [0]

                    def link(instruction):
                        steps[0] += 1
                        instruction.then_inc(S["s_pool"], 1)
                        pool.wait_ge(S["s_pool"], steps[0])

                    nc.gpsimd.memset(pre[:, :, 0:TAPS - 1], 0.0).then_inc(S["s_pre"], 1)
                    pool.wait_ge(S["s_rstd"], NQ)
                    link(nc.gpsimd.tensor_scalar(rs4[:, :], mv4[:, :, 1], EPS, None, ALU.add))
                    nc.gpsimd.tensor_tensor(rs4[:, :], rs4[:, :], mhalf[:, :], ALU.pow).then_inc(S["s_pl2"], 1)

                    def norm_rows(q):
                        read(pool, ("ss", q))
                        link(nc.gpsimd.tensor_scalar(rms[:, :], ss[:, :], 1.0 / DI, EPS, ALU.mult, ALU.add))
                        nc.gpsimd.tensor_tensor(rms[:, :], rms[:, :], mhalf[:, 0:1], ALU.pow).then_inc(S["s_rms"], 1)

                    def norm2(q):
                        pool.wait_ge(S["s_agg"], q + 1)
                        link(nc.gpsimd.tensor_scalar(rs2[:, :], mv2[:, 1:2], EPS, None, ALU.add))
                        nc.gpsimd.tensor_tensor(rs2[:, :], rs2[:, :], mhalf[:, 0:1], ALU.pow).then_inc(S["s_rs2"], 1)
                        pool.wait_ge(S["s_xn2"], q + 1)
                        if q == 0:
                            pool.wait_ge(S["s_bc"], 48)
                        link(nc.gpsimd.tensor_tensor(h2[:, :], h2[:, :], cb_b[:, :], ALU.mult))
                        nc.gpsimd.tensor_tensor(h2[:, :], h2[:, :], sb_b[:, :], ALU.add).then_inc(S["s_h2"], 1)

                    def chunk_inputs(q):
                        c = slice(q * HEADS, (q + 1) * HEADS)
                        if q >= 2:
                            pool.wait_ge(S["s_heads"], NG * (q - 1))
                        rows = xdt[q % 2][:, :, 0:HD]
                        nc.gpsimd.tensor_tensor(rows, h3(x_t[:, q, :]), b3(dt[:, c], HD),
                                                ALU.mult).then_inc(S["s_xdt"], 1)
                        if q < NQ - 1:
                            pool.wait_ge(S["s_xdt"], q + 1)
                            if q:
                                k, n = place[("u", q - 1, 1)]
                                pool.wait_ge(full[k], n)
                            nc.gpsimd.tensor_tensor(h3(xw), rows, b3(edec[:, c], HD), ALU.mult).then_inc(S["s_xw"], 1)

                    for n in TURNED:
                        read(pool, ("turn", n))
                    pool.wait_ge(S["s_exps"], 2)
                    k, n = place[("z", 2 * NQ - 1)]
                    pool.wait_ge(full[k], n)
                    chunk_inputs(0)
                    for q in range(NQ + 1):
                        if 0 < q < NQ:
                            for i in range(2):
                                read(pool, ("inter", q, i))
                            if q < NQ - 1:
                                c = slice(q * HEADS, (q + 1) * HEADS)
                                nc.gpsimd.tensor_tensor(h3(state[:, :]), h3(state[:, :]), b3(etot[:, c], HD),
                                                        ALU.mult).then_inc(S["s_std"], 1)
                            y = yg[:, q % 2, :, :]
                            nc.gpsimd.tensor_tensor(y, y, Dx[:, :, q * P:(q + 1) * P], ALU.add).then_inc(S["s_yacc"], 1)
                        if q:
                            norm_rows(q - 1)
                            norm2(q - 1)
                        if q + 1 < NQ:
                            chunk_inputs(q + 1)

                @block.vector
                def _(dve):
                    steps = [0]

                    def link(instruction):
                        steps[0] += 1
                        instruction.then_inc(S["s_step"], 1)
                        dve.wait_ge(S["s_step"], steps[0])

                    def filled(name):
                        k, n = place[name]
                        dve.wait_ge(full[k], n)
                        return bank[k]

                    def reads(name, instruction):
                        instruction.then_inc(free[place[name][0]], 1)
                        read(dve, name)

                    nc.vector.tensor_copy(modb[:, :], modc[:, :, bass.ds(b, 1)].rearrange("p a o -> p (a o)")) \
                        .then_inc(S["s_modb"], 1)
                    for q in range(NQ):
                        link(nc.vector.bn_stats(bnst[:, q, :], x_in[:, q, :]))
                        nc.vector.bn_aggr(mv4[:, q, :], bnst[:, q, :]).then_inc(S["s_rstd"], 1)
                    dve.wait_ge(S["s_pl2"], 1)
                    for q in range(NQ):
                        nc.vector.tensor_scalar(x_in[:, q, :], x_in[:, q, :], mv4[:, q, 0:1], rs4[:, q:q + 1],
                                                ALU.subtract, ALU.mult).then_inc(S["s_xn"], 1)

                    t = filled("dt")
                    v, u, s, s2, p = dt[:, :], tmp[1], tmp[2], tmp[3], tmp[4]
                    reads("dt", nc.vector.tensor_tensor(v.rearrange("p (q h) -> p q h", q=NQ),
                                                        t[:, 0:256].rearrange("p (q h) -> p q h", q=NQ),
                                                        vrow[:, 0:HEADS].rearrange("p (o h) -> p o h", o=1)
                                                        .broadcast_to([P, NQ, HEADS]), ALU.add))
                    nc.vector.scalar_tensor_tensor(out=u, in0=v, scalar=-1.0, in1=v, op0=ALU.mult,
                                                   op1=ALU.max).then_inc(S["s_dtv"], 1)
                    dve.wait_ge(S["s_u"], 1)
                    link(nc.vector.tensor_scalar(s, u, 2.0, None, ALU.add))
                    link(nc.vector.reciprocal(s, s))
                    link(nc.vector.tensor_tensor(s, s, u, ALU.mult))
                    link(nc.vector.tensor_tensor(s2, s, s, ALU.mult))
                    link(nc.vector.tensor_scalar(p, s2, 1.0 / 13, None, ALU.mult))
                    for d in (11, 9, 7, 5, 3):
                        link(nc.vector.scalar_tensor_tensor(out=p, in0=p, scalar=1.0 / d, in1=s2, op0=ALU.add,
                                                            op1=ALU.mult))
                    link(nc.vector.scalar_tensor_tensor(out=p, in0=p, scalar=1.0, in1=s, op0=ALU.add, op1=ALU.mult))
                    link(nc.vector.tensor_scalar(v, v, 0.0, None, ALU.max))
                    link(nc.vector.scalar_tensor_tensor(out=v, in0=p, scalar=2.0, in1=v, op0=ALU.mult, op1=ALU.add))
                    link(nc.vector.tensor_tensor(tmp[0].rearrange("p (q h) -> p q h", q=NQ),
                                                 v.rearrange("p (q h) -> p q h", q=NQ),
                                                 vrow[:, HEADS:2 * HEADS].rearrange("p (o h) -> p o h", o=1)
                                                 .broadcast_to([P, NQ, HEADS]), ALU.mult))
                    nc.vector.tensor_scalar(tmp[0], tmp[0], LOWEST, None, ALU.max).then_inc(S["s_a"], 1)

                    def conv(n):
                        c = CH[n]
                        if n == 0:
                            dve.wait_ge(S["s_pre"], 1)
                        if n >= 4:
                            if n - 4 in TURNED[1:]:
                                k, m = place[("turn", n - 4)]
                                dve.wait_ge(full[k], m)
                                dve.wait_ge(S["s_dx"], n - 5)
                            else:
                                dve.wait_ge(S["s_silu2"], n - 3)
                        k, m = place[("ch", n)]
                        dve.wait_ge(free[k], m)
                        link(nc.vector.tensor_scalar(cv[:, n % 4, :], pre[:, n % 4, 0:SEQ], cvp[:, c, 0:1],
                                                     cvp[:, c, TAPS:TAPS + 1], ALU.mult, ALU.add))
                        for tap in range(1, TAPS):
                            ins = nc.vector.scalar_tensor_tensor(out=cv[:, n % 4, :], in0=pre[:, n % 4, tap:tap + SEQ],
                                                                 scalar=cvp[:, c, tap:tap + 1], in1=cv[:, n % 4, :],
                                                                 op0=ALU.mult, op1=ALU.add)
                            if tap < TAPS - 1:
                                link(ins)
                            else:
                                ins.then_inc(S["s_conv"], 1)

                    for n in range(3):
                        conv(n)
                    t = filled("cum")
                    dve.wait_ge(S["s_exps"], 1)
                    link(nc.vector.tensor_copy(cums[:, :], t[:, 0:256]))
                    reads("cum", nc.vector.tensor_tensor(edec[:, :], t[:, 256:512], cums[:, :], ALU.subtract))
                    conv(3)
                    t = filled("cumT")
                    nc.vector.tensor_copy(parts[:, 0, :], t[0:HEADS, :]).then_inc(S["s_parts"], 1)
                    dve.wait_ge(S["s_parts"], 1)
                    reads("cumT", nc.vector.tensor_tensor(rest, t[0:HEADS, :], parts[:, 0, :], ALU.subtract))
                    nc.vector.tensor_copy(parts[:, 1, :], rest).then_inc(S["s_parts"], 1)
                    dve.wait_ge(S["s_parts"], 2)
                    link(nc.vector.tensor_tensor(rest, rest, parts[:, 1, :], ALU.subtract))
                    nc.vector.tensor_copy(parts[:, 2, :], rest).then_inc(S["s_parts"], 1)
                    for n in range(4, NCH):
                        conv(n)

                    def gate(q, i):
                        dve.wait_ge(S["s_heads"], NG * q + 4 * (i + 1))
                        t = bank[place[("y", q, i)][0]][:, :].rearrange("p (j t) -> p j t", t=P)
                        tiles, now = slice(4 * i, 4 * i + 4), slice(q * P, (q + 1) * P)
                        y = yg[:, q % 2, tiles, :]
                        if i == 0:
                            if q:
                                dve.wait_ge(S["s_yacc"], q)
                            read(dve, ("z", 2 * NQ - 1))
                            dve.wait_ge(S["s_dx"], NCH - 2)
                        reads(("y", q, i), nc.vector.tensor_tensor(y, y if q else Dx[:, tiles, now], t, ALU.add))
                        nc.vector.tensor_tensor(y, y, zs[:, tiles, now], ALU.mult).then_inc(S["s_g"], 1)

                    def after(q, name):
                        kind, p1 = name[0], name[1]
                        if kind not in ("h2T", "ex"):
                            t = filled(name)
                        if kind == "cb":
                            reads(name, nc.vector.tensor_tensor(cbm[p1 % 2][:, :], t[:, 0:P], upto[:, :], ALU.mult))
                        elif kind == "inter":
                            i = name[2]
                            dve.wait_ge(free[place[("ex", q, i)][0]], place[("ex", q, i)][1])
                            nc.vector.tensor_tensor(yg[:, q % 2, 4 * i:4 * i + 4, :].rearrange("p j t -> p (j t)"),
                                                    t[:, :], ecx[:, i * 512:(i + 1) * 512],
                                                    ALU.mult).then_inc(free[place[name][0]], 1)
                        elif kind == "ss":
                            nc.vector.scalar_tensor_tensor(
                                out=t[:, 0:P], in0=t[:, 0:P], scalar=1.0, in1=ident[:, :], op0=ALU.mult,
                                op1=ALU.mult, accum_out=ss[:, :]).then_inc(free[place[name][0]], 1)
                        elif kind == "wo":
                            dve.wait_ge(S["s_rms"], p1 + 1)
                            if p1 == 0:
                                dve.wait_ge(S["s_bc"], 48)
                            else:
                                dve.wait_ge(S["s_sh"], 16 * p1)
                                read(dve, ("h2T", p1 - 1))
                            reads(name, nc.vector.scalar_tensor_tensor(
                                out=h2[:, :], in0=t[:, :], scalar=rms[:, 0:1], in1=ga_b[:, :], op0=ALU.mult,
                                op1=ALU.mult))
                            dve.wait_ge(S["s_xres"], 16 * (p1 + 1))
                            nc.vector.tensor_tensor(x2, x2, h2[:, :], ALU.add).then_inc(S["s_x2b"], 1)
                            dve.wait_ge(S["s_x2b"], p1 + 1)
                            link(nc.vector.bn_stats(bn2[:, :], x2))
                            nc.vector.bn_aggr(mv2[:, :], bn2[:, :]).then_inc(S["s_agg"], 1)
                        elif kind == "u":
                            half = slice(name[2] * 512, (name[2] + 1) * 512)
                            if q == 0:
                                ins = nc.vector.tensor_copy(state[:, half], t[:, :])
                            else:
                                dve.wait_ge(S["s_std"], q)
                                ins = nc.vector.tensor_tensor(state[:, half], state[:, half], t[:, :], ALU.add)
                            ins.then_inc(free[place[name][0]], 1)
                        elif kind == "lg":
                            reads(name, nc.vector.tensor_tensor(lg[:, :], t[:, 0:EXP], vrow[:, 2 * HEADS:], ALU.add))
                            link(nc.vector.max(tv[:, p1, :], lg[:, :]))
                            nc.vector.max_index(ti[:, p1, :], tv[:, p1, :], lg[:, :]).then_inc(S["s_lg"], 1)

                    for name in work_at(-1, 4):
                        after(-1, name)
                    for q in range(NQ + 1):
                        for a in range(NG):
                            if q < NQ:
                                n = q * NG + a
                                dve.wait_ge(S["s_exp"], n + 1)
                                nc.vector.tensor_tensor(
                                    M[n % 3].rearrange("p (h t) -> p h t", t=P),
                                    M[n % 3].rearrange("p (h t) -> p h t", t=P),
                                    cbm[q % 2][:, :].rearrange("p (o t) -> p o t", o=1).broadcast_to([P, GRP, P]),
                                    ALU.mult).then_inc(S["s_m"], 1)
                            for late in (2, 1):
                                before_q, before_a = divmod(q * NG + a - late, NG)
                                for name in work_at(before_q, before_a) if before_q >= 0 else []:
                                    if (name[0] == "wo") == (late == 2):
                                        after(before_q, name)
                            if q and a == 0:
                                gate(q - 1, 1)
                            if q and a == 4:
                                p1 = q - 1
                                dve.wait_ge(S["s_rs2"], p1 + 1)
                                nc.vector.tensor_scalar(h2[:, :], x2, mv2[:, 0:1], rs2[:, 0:1], ALU.subtract,
                                                        ALU.mult).then_inc(S["s_xn2"], 1)
                            if q < NQ and a == 5:
                                gate(q, 0)
                    dve.wait_ge(S["s_lg"], NQ)
                    nc.vector.tensor_copy(top_v[:, bass.ds(b * NQ, NQ), :], tv[:, :, 0:TOPK]).then_inc(S["s_step"], 1)
                    nc.vector.tensor_copy(top_i[:, bass.ds(b * NQ, NQ), :], ti[:, :, 0:TOPK]).then_inc(S["s_step"], 1)
            with nc.Block() as block:
                @block.gpsimd
                def _(pool):
                    for s in per_loop:
                        pool.sem_clear(s)


def experts(nc, wexp, bexp, mod_d, x2_d, h2_d, out, bank, ident, upto, ones, top_v, top_i):
    TK = NT * TOPK
    COLS = SLOTS + 4
    perm_d = nc.dram_tensor("perm_d", [P * SLOTS, 1], I32, kind="Internal").ap()
    ys_d = nc.dram_tensor("ys_d", [SLOTS * P, HID], F32, kind="Internal").ap()
    with ExitStack() as ctx:
        def sb(name, shape, dt=F32, c=ctx):
            return c.enter_context(nc.sbuf_tensor(name, shape, dt))

        def sem(name):
            return ctx.enter_context(nc.semaphore(name))

        idx = sb("idx", [P, COLS], I32)
        tab_e = sb("tab_e", [1, COLS], I32)
        tab_n = sb("tab_n", [1, COLS], I32)
        tab_r = sb("tab_r", [1, COLS + 1], I32)
        dest = sb("dest", [P, TK], I32)
        wts = sb("wts", [P, TK])

        with ExitStack() as rt:
            def tb(name, shape, dt=F32):
                return sb(name, shape, dt, rt)

            iota_e = tb("iota_e", [P, EXP])
            iota_s = tb("iota_s", [P, COLS])
            tok = tb("tok", [P, NT], I32)
            zero = tb("zero", [P, SLOTS], I32)
            topf = tb("topf", [P, TK])
            hot = tb("hot", [P, TK, EXP])
            chosen = tb("chosen", [P, NT, EXP])
            acc = tb("acc", [P, NT + 1, EXP])
            cnt_i = tb("cnt_i", [P, EXP], I32)
            ntf = tb("ntf", [P, EXP])
            cin = tb("cin", [P, EXP])
            base = tb("base", [P, EXP])
            pos = tb("pos", [P, NT, EXP])
            destf = tb("destf", [P, TK])
            desti = tb("desti", [P, TK], I32)
            hi_i = tb("hi_i", [P, TK], I32)
            addr = tb("addr", [P, TK], I32)
            cmp = tb("cmp", [P, COLS, EXP])
            before = tb("before", [P, P])
            eid = tb("eid", [P, COLS])
            new = tb("new", [P, COLS])
            cnew = tb("cnew", [P, COLS])
            ev = tb("ev", [P, TK])
            ws = tb("ws", [P, NT])
            r_const = sem("r_const")
            r_step = sem("r_step")
            r_chosen = sem("r_chosen")
            r_pos = sem("r_pos")
            r_addr = sem("r_addr")
            r_zero = sem("r_zero")
            r_ev = sem("r_ev")
            r_exp = sem("r_exp")
            r_scat = sem("r_scat")
            r_idx = sem("r_idx")
            with nc.Block() as block:
                @block.gpsimd
                def _(pool):
                    nc.gpsimd.iota(iota_e[:, :], pattern=[[1, EXP]], base=0, channel_multiplier=0,
                                   allow_small_or_imprecise_dtypes=True).then_inc(r_const, 1)
                    nc.gpsimd.iota(iota_s[:, :], pattern=[[1, COLS]], base=0, channel_multiplier=0,
                                   allow_small_or_imprecise_dtypes=True).then_inc(r_const, 1)
                    nc.gpsimd.iota(tok[:, :], pattern=[[P, NT]], base=0, channel_multiplier=1).then_inc(r_const, 1)
                    nc.gpsimd.memset(zero[:, :], 0).then_inc(r_const, 1)
                    nc.gpsimd.memset(idx[:, SLOTS:], 0).then_inc(r_const, 1)
                    pool.wait_ge(r_zero, 16)
                    pool.wait_ge(r_addr, 1)
                    for c in range(TK):
                        pool.indirect_dma_start(perm_d, bass.IndirectOffsetOnAxis(addr[:, c:c + 1], 0),
                                                tok[:, c // TOPK:c // TOPK + 1], None).then_inc(r_scat, 16)

                @block.sync
                def _(sp):
                    sp.wait_ge(r_const, 5)
                    sp.dma_start(perm_d.rearrange("(p s) o -> p (s o)", p=P), zero[:, :]).then_inc(r_zero, 16)
                    sp.wait_ge(r_scat, 16 * TK)
                    sp.dma_start(idx[:, 0:SLOTS], perm_d.rearrange("(p s) o -> p (s o)", p=P)).then_inc(r_idx, 16)
                    sp.wait_ge(r_idx, 16)

                @block.scalar
                def _(act):
                    act.wait_ge(r_ev, 1)
                    nc.scalar.activation(ev[:, :], ev[:, :], ACT.Exp).then_inc(r_exp, 1)

                @block.tensor
                def _(pe):
                    pe.wait_ge(r_chosen, 1)
                    nc.tensor.matmul(bank[0][:, :], before[:, :], chosen[:, :, :].rearrange("p t e -> p (t e)"),
                                     start=True, stop=False)
                    nc.tensor.matmul(bank[0][:, :], ones[:, :], acc[:, 0:NT, :].rearrange("p t e -> p (t e)"),
                                     start=False, stop=True)
                    nc.tensor.matmul(bank[1][:, 0:EXP], ones[:, :], acc[:, NT, :], start=True,
                                     stop=True).then_inc(r_pos, 1)

                @block.vector
                def _(dve):
                    steps = [0]

                    def link(instruction):
                        steps[0] += 1
                        instruction.then_inc(r_step, 1)
                        dve.wait_ge(r_step, steps[0])

                    def col(ap, n):
                        return ap.rearrange("p (c o) -> p c o", o=1).broadcast_to([P, ap.shape[1], n])

                    def row(ap, n):
                        return ap.rearrange("p (o e) -> p o e", o=1).broadcast_to([P, n, ap.shape[1]])

                    link(nc.vector.tensor_tensor(before[:, :], upto[:, :], ident[:, :], ALU.subtract))
                    e4 = ev[:, :].rearrange("p (t k) -> p t k", k=TOPK)
                    nc.vector.tensor_tensor(e4, top_v[:, :, :], top_v[:, :, 0:1].broadcast_to([P, NT, TOPK]),
                                            ALU.subtract).then_inc(r_ev, 1)
                    link(nc.vector.tensor_copy(topf[:, :].rearrange("p (t k) -> p t k", k=TOPK), top_i[:, :, :]))
                    dve.wait_ge(r_const, 5)
                    link(nc.vector.tensor_tensor(hot[:, :, :], row(iota_e[:, :], TK), col(topf[:, :], EXP),
                                                 ALU.is_equal))
                    link(nc.vector.tensor_reduce(chosen[:, :, :], hot[:, :, :].rearrange("p (t k) e -> p t e k", k=TOPK),
                                                 AX.X, ALU.add))
                    link(nc.vector.memset(acc[:, 0, :], 0.0))
                    for t in range(NT):
                        ins = nc.vector.tensor_tensor(acc[:, t + 1, :], acc[:, t, :], chosen[:, t, :], ALU.add)
                        if t == NT - 1:
                            ins.then_inc(r_chosen, 1)
                        else:
                            link(ins)
                    dve.wait_ge(r_exp, 1)
                    link(nc.vector.tensor_reduce(ws[:, :], e4, AX.X, ALU.add))
                    link(nc.vector.reciprocal(ws[:, :], ws[:, :]))
                    link(nc.vector.tensor_tensor(wts[:, :].rearrange("p (t k) -> p t k", k=TOPK), e4,
                                                 col(ws[:, :], TOPK), ALU.mult))
                    dve.wait_ge(r_pos, 1)
                    link(nc.vector.tensor_scalar(cnt_i[:, :], bank[1][:, 0:EXP], float(P - 1), None, ALU.add))
                    link(nc.vector.tensor_scalar(cnt_i[:, :], cnt_i[:, :], 7, None, ALU.logical_shift_right))
                    link(nc.vector.tensor_copy(ntf[:, :], cnt_i[:, :]))
                    link(nc.vector.tensor_tensor_scan(cin[:, :], ones[:, 0:EXP], ntf[:, :], 0.0, ALU.mult, ALU.add))
                    link(nc.vector.tensor_tensor(base[:, :], cin[:, :], ntf[:, :], ALU.subtract))
                    link(nc.vector.scalar_tensor_tensor(out=pos[:, :, :], in0=row(base[:, :], NT), scalar=float(P),
                                                        in1=bank[0][:, :].rearrange("p (t e) -> p t e", e=EXP),
                                                        op0=ALU.mult, op1=ALU.add))
                    link(nc.vector.tensor_tensor(hot[:, :, :].rearrange("p (t k) e -> p t k e", k=TOPK),
                                                 hot[:, :, :].rearrange("p (t k) e -> p t k e", k=TOPK),
                                                 pos[:, :, :].rearrange("p t (o e) -> p t o e", o=1)
                                                 .broadcast_to([P, NT, TOPK, EXP]), ALU.mult))
                    link(nc.vector.tensor_reduce(destf[:, :], hot[:, :, :], AX.X, ALU.add))
                    link(nc.vector.tensor_copy(desti[:, :], destf[:, :]))
                    link(nc.vector.tensor_scalar(hi_i[:, :], desti[:, :], 7, None, ALU.logical_shift_right))
                    link(nc.vector.tensor_scalar(desti[:, :], desti[:, :], P - 1, None, ALU.bitwise_and))
                    nc.vector.scalar_tensor_tensor(out=addr[:, :], in0=desti[:, :], scalar=float(SLOTS), in1=hi_i[:, :],
                                                   op0=ALU.mult, op1=ALU.add).then_inc(r_addr, 1)
                    link(nc.vector.tensor_scalar(dest[:, :], destf[:, :], float(P), None, ALU.add))
                    link(nc.vector.tensor_tensor(cmp[:, :, :], row(cin[:, :], COLS), col(iota_s[:, :], EXP), ALU.is_le))
                    link(nc.vector.tensor_reduce(eid[:, :], cmp[:, :, :], AX.X, ALU.add))
                    link(nc.vector.tensor_scalar(eid[:, :], eid[:, :], float(EXP - 1), None, ALU.min))
                    link(nc.vector.memset(new[:, 0:1], 1.0))
                    link(nc.vector.tensor_tensor(new[:, 1:], eid[:, 1:], eid[:, 0:COLS - 1], ALU.not_equal))
                    link(nc.vector.tensor_tensor_scan(cnew[:, :], ones[:, 0:COLS], new[:, :], -1.0, ALU.mult, ALU.add))
                    link(nc.vector.tensor_copy(tab_e[:, :], eid[0:1, :]))
                    link(nc.vector.tensor_copy(tab_n[:, :], new[0:1, :]))
                    link(nc.vector.memset(tab_r[:, 0:1], 0))
                    link(nc.vector.tensor_copy(tab_r[:, 1:], cnew[0:1, :]))
                    link(nc.vector.tensor_scalar(tab_r[:, :], tab_r[:, :], RING - 1, None, ALU.bitwise_and))

        with ExitStack() as ex:
            def eb(name, shape, dt=F32):
                return sb(name, shape, dt, ex)

            wr = eb("wr", [P, RING, WEXP])
            br = eb("br", [P, RING, 2 * FF + HID])
            xg = [eb(f"xg{i}", [P, HID]) for i in range(2)]
            idc = [eb(f"idc{i}", [P, 1], I32) for i in range(2)]
            xT = [eb(f"xT{i}", [P, KH * P]) for i in range(2)]
            gu = [eb(f"gu{i}", [P, 2 * FF]) for i in range(2)]
            sg = [eb(f"sg{i}", [P, FF]) for i in range(2)]
            ac = [eb(f"ac{i}", [P, FF]) for i in range(2)]
            aT = [eb(f"aT{i}", [P, 2 * P]) for i in range(2)]
            yo = [eb(f"yo{i}", [P, HID]) for i in range(2)]
            w_in_ring = [sem(f"w_in_ring{i}") for i in range(4)]
            gathered = [sem(f"gathered{i}") for i in range(2)]
            stored = [sem(f"stored{i}") for i in range(2)]
            idx_first = sem("idx_first")
            idx_set = sem("idx_set")
            x_turned = sem("x_turned")
            x_ready = sem("x_ready")
            gu_made = sem("gu_made")
            gu_read = sem("gu_read")
            clamped = sem("clamped")
            sig_made = sem("sig_made")
            act_made = sem("act_made")
            act_turned = sem("act_turned")
            act_ready = sem("act_ready")
            y_made = sem("y_made")
            y_read = sem("y_read")
            e_step = sem("e_step")
            XTB, GUB, ATB, YB = bank[0:2], bank[2:4], bank[4:6], bank[6:8]

            with nc.Block() as block:
                @block.sync
                def _(sp):
                    def load(i, u):
                        e = sp.value_load(tab_e[0:1, bass.ds(i, 1)], min_val=0, max_val=EXP - 1)
                        n = sp.value_load(tab_n[0:1, bass.ds(i, 1)], min_val=0, max_val=1)
                        r = sp.value_load(tab_r[0:1, bass.ds(i + 1, 1)], min_val=0, max_val=RING - 1)
                        sp.dma_start(wr[:, bass.ds(r, 1), :].rearrange("p o w -> p (o w)"),
                                     wexp[bass.ds(e, 1)].rearrange("o p w -> (o p) w"),
                                     cond=(n == 1)).then_inc(w_in_ring[u % 4], 16)
                        sp.dma_start(br[:, bass.ds(r, 1), :].rearrange("p o w -> p (o w)"),
                                     bexp[bass.ds(e, 1), :].broadcast_to([P, 2 * FF + HID]),
                                     cond=(n == 1)).then_inc(w_in_ring[u % 4], 16)

                    for i in range(AHEAD):
                        load(i, i)
                    with sp.Fori(0, SLOTS // 4) as j:
                        for u in range(4):
                            i = 4 * j + u
                            sp.wait_ge(y_read, i + 3)
                            sp.dma_start(ys_d[bass.ds(i * P, P), :], yo[u % 2][:, :]).then_inc(stored[u % 2], 16)
                            load(i + AHEAD, u + AHEAD)
                    for k in range(2):
                        sp.wait_ge(stored[k], 16 + 16 * SLOTS // 2)
                    for u in range(AHEAD):
                        sp.wait_ge(w_in_ring[u], 32 * (SLOTS // 4 + 1))

                @block.gpsimd
                def _(pool):
                    def gather(i, u, copied, count):
                        nc.gpsimd.tensor_copy(idc[u % 2][:, :], idx[:, bass.ds(i, 1)]).then_inc(copied, 1)
                        pool.wait_ge(e_step, 1)
                        pool.wait_ge(copied, count)
                        pool.indirect_dma_start(xg[u % 2][:, :], None, h2_d,
                                                bass.IndirectOffsetOnAxis(idc[u % 2][:, :], 0)).then_inc(gathered[u % 2], 16)

                    gather(0, 0, idx_first, 1)
                    gather(1, 1, idx_first, 2)
                    with pool.Fori(0, SLOTS // 4) as j:
                        for u in range(4):
                            i = 4 * j + u
                            pool.wait_ge(x_turned, i + 1)
                            gather(i + 2, u, idx_set, i + 1)
                    for k in range(2):
                        pool.wait_ge(gathered[k], 16 * (SLOTS // 2 + 1))

                @block.tensor
                def _(pe):
                    def turn_x(v, count):
                        pe.wait_ge(gathered[v], count)
                        for k in range(KH):
                            last = nc.tensor.transpose(XTB[v][:, k * P:(k + 1) * P], xg[v][:, k * P:(k + 1) * P],
                                                       ident[:, :])
                        last.then_inc(x_turned, 1)

                    turn_x(0, 16)
                    with pe.Fori(0, SLOTS // 4) as j:
                        for u in range(4):
                            i = 4 * j + u
                            r = pe.value_load(tab_r[0:1, bass.ds(i + 1, 1)], min_val=0, max_val=RING - 1)
                            rp = pe.value_load(tab_r[0:1, bass.ds(i, 1)], min_val=0, max_val=RING - 1)
                            pe.wait_ge(w_in_ring[u], 32 * j + 32)
                            pe.wait_ge(x_ready, i + 1)
                            pe.wait_ge(gu_read, i + 1)
                            for k in range(KH):
                                last = nc.tensor.matmul(GUB[u % 2][:, :], xT[u % 2][:, k * P:(k + 1) * P],
                                                        wr[:, bass.ds(r, 1), k * 512:(k + 1) * 512]
                                                        .rearrange("p o w -> p (o w)"),
                                                        start=(k == 0), stop=(k == KH - 1))
                            last.then_inc(gu_made, 1)
                            v = (u + 1) % 2
                            pe.wait_ge(act_made, i + 1)
                            pe.wait_ge(act_ready, i + 1)
                            for k in range(2):
                                last = nc.tensor.transpose(ATB[v][:, k * P:(k + 1) * P], ac[v][:, k * P:(k + 1) * P],
                                                           ident[:, :])
                            last.then_inc(act_turned, 1)
                            turn_x(v, 32 * j + 16 * ((u + 1) // 2 + 1))
                            pe.wait_ge(act_ready, i + 3)
                            pe.wait_ge(y_read, i + 1)
                            for k in range(2):
                                last = nc.tensor.matmul(YB[v][:, :], aT[v][:, k * P:(k + 1) * P],
                                                        wr[:, bass.ds(rp, 1), 2048 + k * 512:2048 + (k + 1) * 512]
                                                        .rearrange("p o w -> p (o w)"), start=(k == 0), stop=(k == 1))
                            last.then_inc(y_made, 1)

                @block.scalar
                def _(act):
                    def x_out(i, u):
                        act.wait_ge(x_turned, i + 1)
                        nc.scalar.activation(xT[u % 2][:, :], XTB[u % 2][:, :], ACT.Copy).then_inc(x_ready, 1)

                    x_out(0, 0)
                    with act.Fori(0, SLOTS // 4) as j:
                        for u in range(4):
                            i = 4 * j + u
                            v = (u + 1) % 2
                            act.wait_ge(act_turned, i + 1)
                            nc.scalar.activation(aT[v][:, :], ATB[v][:, 0:2 * P], ACT.Copy).then_inc(act_ready, 1)
                            act.wait_ge(clamped, i + 1)
                            nc.scalar.activation(sg[u % 2][:, :], gu[u % 2][:, 0:FF], ACT.Sigmoid,
                                                 scale=1.702).then_inc(sig_made, 1)
                            x_out(i + 1, u + 1)

                @block.vector
                def _(dve):
                    for k in range(2):
                        nc.vector.memset(yo[k][:, :], 0.0).then_inc(stored[k], 16)
                    nc.vector.memset(ac[0][:, :], 0.0).then_inc(gu_read, 2)
                    nc.vector.memset(aT[1][:, :], 0.0).then_inc(act_ready, 2)
                    nc.vector.memset(aT[0][:, :], 0.0).then_inc(y_read, 2)
                    nc.vector.memset(ac[1][:, :], 0.0).then_inc(act_made, 1)
                    nc.vector.memset(sg[0][:, :], 0.0).then_inc(e_step, 1)
                    with dve.Fori(0, SLOTS // 4) as j:
                        for u in range(4):
                            i = 4 * j + u
                            v = (u + 1) % 2
                            r = dve.value_load(tab_r[0:1, bass.ds(i + 1, 1)], min_val=0, max_val=RING - 1)
                            rp = dve.value_load(tab_r[0:1, bass.ds(i, 1)], min_val=0, max_val=RING - 1)
                            c = u % 2
                            dve.wait_ge(gu_made, i + 1)
                            ins = nc.vector.tensor_tensor(gu[c][:, :], GUB[c][:, :],
                                                          br[:, bass.ds(r, 1), 0:512].rearrange("p o w -> p (o w)"), ALU.add)
                            ins.then_inc(gu_read, 1)
                            dve.wait_ge(gu_read, i + 3)
                            nc.vector.tensor_scalar(gu[c][:, 0:FF], gu[c][:, 0:FF], 7.0, None, ALU.min).then_inc(clamped, 1)
                            nc.vector.tensor_scalar(gu[c][:, FF:], gu[c][:, FF:], 7.0, -7.0, ALU.min,
                                                    ALU.max).then_inc(e_step, 1)
                            dve.wait_ge(sig_made, i + 1)
                            dve.wait_ge(clamped, i + 1)
                            nc.vector.tensor_tensor(sg[c][:, :], sg[c][:, :], gu[c][:, 0:FF], ALU.mult).then_inc(e_step, 1)
                            dve.wait_ge(e_step, 2 * i + 3)
                            nc.vector.scalar_tensor_tensor(out=ac[c][:, :], in0=gu[c][:, FF:], scalar=1.0, in1=sg[c][:, :],
                                                           op0=ALU.add, op1=ALU.mult).then_inc(act_made, 1)
                            dve.wait_ge(y_made, i + 1)
                            dve.wait_ge(stored[c], 32 * j + 16 * (u // 2 + 1))
                            nc.vector.tensor_tensor(yo[c][:, :], YB[v][:, :],
                                                    br[:, bass.ds(rp, 1), 512:1024].rearrange("p o w -> p (o w)"),
                                                    ALU.add).then_inc(y_read, 1)

        with ExitStack() as cb:
            def kb(name, shape, dt=F32):
                return sb(name, shape, dt, cb)

            yk = [kb(f"yk{i}", [P, TOPK, HID]) for i in range(2)]
            xr = [kb(f"xr{i}", [P, HID]) for i in range(2)]
            d4 = [kb(f"d4{i}", [P, TOPK], I32) for i in range(2)]
            w4 = [kb(f"w4{i}", [P, TOPK]) for i in range(2)]
            ac2 = [kb(f"ac2{i}", [P, HID]) for i in range(2)]
            gb = kb("gb", [P, BATCH, HID])
            c_gb = sem("c_gb")
            c_d4 = sem("c_d4")
            c_y = [sem(f"c_y{i}") for i in range(2)]
            c_x = [sem(f"c_x{i}") for i in range(2)]
            c_out = [sem(f"c_out{i}") for i in range(2)]
            c_done = sem("c_done")
            c_step = sem("c_step")
            with nc.Block() as block:
                @block.gpsimd
                def _(pool):
                    with pool.Fori(0, BATCH) as b:
                        for u in range(NQ):
                            t = NQ * b + u
                            pool.wait_ge(c_done, t + 1)
                            nc.gpsimd.tensor_copy(d4[u % 2][:, :], dest[:, bass.ds(t * TOPK, TOPK)]).then_inc(c_d4, 1)
                            pool.wait_ge(c_gb, 16 * BATCH)
                            pool.wait_ge(c_d4, t + 1)
                            for k in range(TOPK):
                                pool.indirect_dma_start(yk[u % 2][:, k, :], None, ys_d,
                                                        bass.IndirectOffsetOnAxis(d4[u % 2][:, k:k + 1], 0)) \
                                    .then_inc(c_y[u % 2], 16)

                @block.sync
                def _(sp):
                    for b in range(BATCH):
                        sp.dma_start(gb[:, b, :], mod_d[b:b + 1, 5 * HID:6 * HID].broadcast_to([P, HID])).then_inc(c_gb, 16)
                    with sp.Fori(0, BATCH) as b:
                        for u in range(NQ):
                            t = NQ * b + u
                            sp.wait_ge(c_done, t + 1)
                            sp.dma_start(xr[u % 2][:, :], x2_d[bass.ds(t * P, P), :]).then_inc(c_x[u % 2], 16)
                    for k in range(2):
                        sp.wait_ge(c_out[k], 16 + 16 * NT // 2)

                @block.scalar
                def _(act):
                    with act.Fori(0, BATCH) as b:
                        for u in range(NQ):
                            act.wait_ge(c_done, NQ * b + u + 3)
                            act.dma_start(out[bass.ds(b, 1), u * P:(u + 1) * P, :].rearrange("o p d -> (o p) d"),
                                          ac2[u % 2][:, :]).then_inc(c_out[u % 2], 16)

                @block.vector
                def _(dve):
                    nc.vector.memset(w4[0][:, :], 0.0).then_inc(c_done, 2)
                    for k in range(2):
                        nc.vector.memset(ac2[k][:, :], 0.0).then_inc(c_out[k], 16)
                    dve.wait_ge(c_done, 2)
                    dve.wait_ge(c_out[1], 16)
                    dve.wait_ge(c_gb, 16 * BATCH)
                    with dve.Fori(0, BATCH) as b:
                        for u in range(NQ):
                            t = NQ * b + u
                            c = u % 2
                            n = [0]

                            def link(instruction):
                                n[0] += 1
                                instruction.then_inc(c_step, 1)
                                dve.wait_ge(c_step, t * 6 + n[0])

                            link(nc.vector.tensor_copy(w4[c][:, :], wts[:, bass.ds(t * TOPK, TOPK)]))
                            dve.wait_ge(c_y[c], 128 * b + 64 * (u // 2 + 1))
                            dve.wait_ge(c_out[c], 32 * b + 16 * (u // 2 + 1))
                            link(nc.vector.tensor_scalar(ac2[c][:, :], yk[c][:, 0, :], w4[c][:, 0:1], None, ALU.mult))
                            for k in range(1, TOPK):
                                link(nc.vector.scalar_tensor_tensor(out=ac2[c][:, :], in0=yk[c][:, k, :],
                                                                    scalar=w4[c][:, k:k + 1], in1=ac2[c][:, :],
                                                                    op0=ALU.mult, op1=ALU.add))
                            link(nc.vector.tensor_tensor(ac2[c][:, :], ac2[c][:, :],
                                                         gb[:, bass.ds(b, 1), :].rearrange("p o d -> p (o d)"), ALU.mult))
                            dve.wait_ge(c_x[c], 32 * b + 16 * (u // 2 + 1))
                            nc.vector.tensor_tensor(ac2[c][:, :], ac2[c][:, :], xr[c][:, :], ALU.add).then_inc(c_done, 1)


def layouts(i):
    f = {k[3:]: np.asarray(v) for k, v in i.items()}

    def rows(a):
        return a.reshape(-1, P, *a.shape[1:]).swapaxes(0, 1)

    c_rows = rows(f["c"].T)
    wmod = f["wmod"].reshape(KH, P, 6, HID).transpose(2, 1, 0, 3)
    conv = np.concatenate([f["attn_conv_w"], f["attn_conv_b"][:, None]], axis=1)
    vecs = np.concatenate([f["attn_dt_bias"], f["attn_A_log"], f["ffn_gate_b"]])[None]
    gate_up = np.concatenate([f["ffn_w_gate"], f["ffn_w_up"]], axis=2)
    gate_up = gate_up.reshape(EXP, KH, P, 2 * FF).transpose(0, 2, 1, 3).reshape(EXP, P, KH * 2 * FF)
    down = f["ffn_w_down"].reshape(EXP, 2, P, HID).transpose(0, 2, 1, 3).reshape(EXP, P, 2 * HID)
    return {
        "x": f["attn_hidden_states"], "cT": c_rows, "wmod": wmod, "w_in": rows(f["attn_W_in"]),
        "w_out": rows(f["attn_W_out"]), "convp": rows(conv), "vecs": vecs, "mup": f["attn_mup_vector"][None],
        "nw": f["attn_norm_w"].reshape(8, P).T, "dcol": np.repeat(f["attn_D"], HD).reshape(8, P).T,
        "gwT": rows(f["ffn_gate_w"].T),
        "wexp": np.concatenate([gate_up, down], axis=2),
        "bexp": np.concatenate([f["ffn_b_gate"], f["ffn_b_up"], f["ffn_b_down"]], axis=1),
    }


def kernel(**inputs):
    import concourse.bacc as _bacc
    from concourse.bass_utils import run_bass_kernel_spmd as _run

    nc = _bacc.Bacc("TRN2", target_bir_lowering=False, num_devices=1)
    arrays, args = {}, []
    for name, a in layouts(inputs).items():
        a = np.ascontiguousarray(a)
        arrays[f"in_{name}"] = a
        args.append(nc.dram_tensor(f"in_{name}", a.shape, mybir.dt.from_np(a.dtype), kind="ExternalInput").ap())
    out = nc.dram_tensor("out_0", (BATCH, SEQ, HID), F32, kind="ExternalOutput").ap()
    build(nc, args, out)
    return _run(nc, [arrays], core_ids=[0]).results[0]["out_0"]
```

```python
from contextlib import ExitStack

import numpy as np

import concourse.bass as bass
from concourse import mybir

F32 = mybir.dt.float32
BF16 = mybir.dt.bfloat16
F32R = mybir.dt.float32r
I32 = mybir.dt.int32
U32 = mybir.dt.uint32
ALU = mybir.AluOpType
ACT = mybir.ActivationFunctionType
AX = mybir.AxisListType

P = 128
BATCH, SEQ, HID = 4, 512, 512
KH = HID // P
DI = 1024
HEADS, HD = 64, 16
STATE = 128
TAPS = 4
CONV = DI + 2 * STATE
NCH = CONV // P
PROJ = 2 * DI + 2 * STATE + HEADS
NQ = SEQ // P
NT = BATCH * NQ
EXP, TOPK, FF = 32, 4, 256
SLOTS = 96
RING = 4
DEEP = NQ
USED = NT * TOPK + 4
AHEAD = RING - 1
WEXP = KH * 2 * FF + 2 * HID
EPS = 1e-5
GRP = 8
NG = HEADS // GRP
DEC = 3 + 12
ROWS = DEC + P // 2
FAR = -32768.0
LOWEST = -88.0
CH = [8, 9, 0, 1, 2, 3, 4, 5, 6, 7]
TURNED = [0] + list(range(2, NCH))


def plan_banks():
    order = ["cum", ("ch", 0), ("ch", 1), "cumT", ("ch", 2), ("ch", 3), ("turn", 0)]
    for n in range(4, NCH):
        order += [("ch", n)] + [("turn", n - 2)] * (n >= 4)
    order += [("z", 4), ("turn", 8), ("z", 5), ("turn", 9)]
    uses = [0] * 8
    place = {}

    def put(name, k):
        uses[k] += 1
        place[name] = (k, uses[k])

    for i, name in enumerate(order):
        put(name, i % 8)
    stage_a = list(uses)
    for q in range(NQ):
        for half in range(2):
            put(("y", q, half), 4 + half)
    n = 0
    for name in (w for q in range(-1, NQ + 1) for a in range(NG) for w in work_at(q, a)):
        if name == ("dt",):
            put(name, 0)
        elif name[0] == "z" and name[1] < 4:
            put(name, (name[1] + 1) % 4)
        else:
            put(name, 6 + n % 2)
            n += 1
    first = {("h", k): (k, 1) for k in range(KH)}
    first[("dt",)] = (4, 1)
    first.update({("z", j): ((5 + j) % 8, 1 + j // 3) for j in range(4)})
    return order, place, stage_a, first


def work_at(q, a):
    if a == 0 and 0 < q < NQ:
        return [("inter", q, 0), ("inter", q, 1)]
    if a == 1 and q > 0:
        return [("ss", q - 1), ("wo", q - 1)]
    if a == 3 and 0 <= q < NQ - 1:
        return [("u", q, 0), ("u", q, 1)]
    if a == 4 and q < NQ - 1:
        return [("cb", q + 1)]
    if a == 7 and 0 <= q < NQ - 1:
        return [("ex", q + 1, 0), ("ex", q + 1, 1)]
    if q == -1 and a == 7:
        return [("z", 6), ("z", 7)]
    if q == NQ - 1 and a in (3, 4):
        return [("h", 2 * (a - 3)), ("h", 2 * (a - 3) + 1)]
    if q == NQ:
        ahead = {0: [("dt",)], 2: [("z", 0), ("z", 1)], 5: [("h2T", q - 1), ("z", 2)],
                 6: [("lg", q - 1)], 7: [("z", 3)]}
        return ahead.get(a, [])
    if a == 5 and q > 0:
        return [("h2T", q - 1)]
    if a == 6 and q > 0:
        return [("lg", q - 1)]
    return []


def build(nc, ins, out):
    x, cT, wmod, w_in, w_out, convp, vecs, mup, nw, dcol, gwT, wexp, bexp = ins
    plan = plan_banks()

    mod_d = nc.dram_tensor("mod_d", [BATCH, 6 * HID], F32, kind="Internal").ap()
    cum_d = nc.dram_tensor("cum_d", [HEADS, 3, SEQ], BF16, kind="Internal").ap()
    x2_d = nc.dram_tensor("x2_d", [NT * P, HID], F32, kind="Internal").ap()
    h2_d = nc.dram_tensor("h2_d", [NT * P, HID], F32, kind="Internal").ap()
    ys_d = nc.dram_tensor("ys_d", [SLOTS * P, HID], F32, kind="Internal").ap()

    with ExitStack() as whole:
        def sb(name, shape, dt=F32, ctx=whole):
            return ctx.enter_context(nc.sbuf_tensor(name, shape, dt))

        def sem(name):
            return whole.enter_context(nc.semaphore(name))

        bank = [whole.enter_context(nc.psum_tensor(f"bank{i}", [P, 512], F32)) for i in range(8)]
        ident = sb("ident", [P, P])
        upto = sb("upto", [P, P])
        ones = sb("ones", [P, P])
        top_v = sb("top_v", [P, NT, TOPK])
        top_i = sb("top_i", [P, NT, TOPK], U32)
        mixer(nc, plan, x, cT, wmod, w_in, w_out, convp, vecs, mup, nw, dcol, gwT,
              mod_d, cum_d, x2_d, h2_d, ys_d, bank, ident, upto, ones, top_v, top_i)
        experts(nc, wexp, bexp, mod_d, x2_d, h2_d, ys_d, out, bank, ident, upto, ones, top_v, top_i)


def mixer(nc, plan, x, cT, wmod, w_in, w_out, convp, vecs, mup, nw, dcol, gwT,
          mod_d, cum_d, x2_d, h2_d, ys_d, bank, ident, upto, ones, top_v, top_i):
    order_a, place, stage_a, first = plan
    with ExitStack() as ctx:
        def sb(name, shape, dt=F32):
            return ctx.enter_context(nc.sbuf_tensor(name, shape, dt))

        def sem(name):
            return ctx.enter_context(nc.semaphore(name))

        win = sb("win", [P, KH, PROJ])
        wout = sb("wout", [P, 8, HID])
        gw = sb("gw", [P, KH, EXP])
        cvp = sb("cvp", [P, NCH, TAPS + 1])
        nwc = sb("nwc", [P, 8])
        dc = sb("dc", [P, 8])
        vrow = sb("vrow", [P, 2 * HEADS + EXP])
        modc = sb("modc", [P, 8, BATCH])
        modb = sb("modb", [P, 8])
        sct = sb("sct", [P, KH, BATCH])
        x_in = sb("x_in", [P, NQ, HID])
        hT = sb("hT", [P, KH, SEQ])
        pre = sb("pre", [P, 4, SEQ + TAPS - 1])
        cv = sb("cv", [P, 4, SEQ])
        BT = sb("BT", [P, SEQ])
        CT = sb("CT", [P, SEQ])
        x_t = sb("x_t", [P, NQ, DI])
        B_t = sb("B_t", [P, NQ - 1, STATE])
        Dx = sb("Dx", [P, 8, SEQ])
        zs = sb("zs", [P, 8, SEQ])
        dt = sb("dt", [P, NQ * HEADS])
        edec = sb("edec", [P, NQ * HEADS])
        etot = sb("etot", [P, NQ * HEADS])
        parts = sb("parts", [HEADS, 3, SEQ], BF16)
        ga_b = sb("ga_b", [P, HID])
        cb_b = sb("cb_b", [P, HID])
        sb_b = sb("sb_b", [P, HID])
        mv = sb("mv", [ROWS, 2, 32 * P], BF16)
        st = sb("st", [ROWS, 2, 8 * P], BF16)
        head_of = sb("head_of", [HEADS, 4 * P], BF16)
        state = sb("state", [P, DI])
        yg = sb("yg", [P, 2, 8, P])
        xdt = [sb(f"xdt{i}", [P, HEADS, 2 * HD]) for i in range(2)]
        cbm = [sb(f"cbm{i}", [P, P]) for i in range(2)]
        lg = sb("lg", [P, EXP])
        bnst = sb("bnst", [P, NQ, 6])
        mv4 = sb("mv4", [P, NQ, 2])
        rs4 = sb("rs4", [P, NQ])
        mhalf = sb("mhalf", [P, NQ])
        ss = sb("ss", [P, 1])
        rms = sb("rms", [P, 1])
        bn2 = sb("bn2", [P, 6])
        mv2 = sb("mv2", [P, 2])
        rs2 = sb("rs2", [P, 1])
        tv = sb("tv", [P, NQ, 8])
        ti = sb("ti", [P, NQ, 8], U32)

        M = [pre[:, :, :].rearrange("p a t -> p (a t)")[:, i * GRP * P:(i + 1) * GRP * P] for i in range(2)]
        M += [cv[:, 0:2, :].rearrange("p a t -> p (a t)")]
        ecx = cv[:, 2:4, :].rearrange("p a t -> p (a t)")
        x2 = x_t[:, 0, 0:HID]
        h2T = x_t[:, 0, HID:2 * HID].rearrange("p (k t) -> p k t", t=P)
        before = cbm[0]
        flat = yg[:, :, :, :].rearrange("p i j t -> p (i j t)")
        a_log = flat[:, 0:256]
        u, s1, s2, p1 = [flat[:, 256 * i:256 * (i + 1)] for i in range(4)]
        cums = s1
        rest = flat[0:HEADS, 2 * SEQ:3 * SEQ]
        modr = Dx[0:BATCH, 0:6, :].rearrange("p a b -> p (a b)")
        wm = [x_t[:, 2 * i:2 * i + 2, :].rearrange("p a (k n) -> p (a k) n", n=HID) for i in range(2)]
        wm += [cv[:, :, :], yg[:, :, :, :].rearrange("p i (k a) t -> p (i k) (a t)", a=4)]
        wm += [xdt[i][:, :, :].rearrange("p (k h) c -> p k (h c)", k=KH) for i in range(2)]
        mupb = zs[:, :, :].rearrange("p a b -> p (a b)")[:, 0:PROJ]

        s_const = sem("s_const")
        s_ld = sem("s_ld")
        s_wm = [sem(f"s_wm{j}") for j in range(6)]
        s_c = sem("s_c")
        s_vec = sem("s_vec")
        s_wo = sem("s_wo")
        s_silu = sem("s_silu")
        s_mod = sem("s_mod")
        s_row = sem("s_row")
        s_mup = sem("s_mup")
        s_expa = sem("s_expa")
        s_rows = sem("s_rows")
        s_modT = sem("s_modT")
        s_v = sem("s_v")

        with ExitStack() as setup:
          one_of_4 = setup.enter_context(nc.sbuf_tensor("one_of_4", [ROWS, 4, P], BF16))
          two_of_t = setup.enter_context(nc.sbuf_tensor("two_of_t", [ROWS, 4, P], BF16))
          with nc.Block() as block:
              @block.sync
              def _(sp):
                  sp.dma_start(sct[:, :, :], cT).then_inc(s_c, 16)
                  for j in range(6):
                      sp.dma_start(wm[j], wmod[j]).then_inc(s_wm[j], 16)
                  sp.dma_start(x_in[:, :, :], x[0].rearrange("(q p) d -> p q d", p=P)).then_inc(s_rows, 16)
                  sp.dma_start(wout[:, :, :], w_out).then_inc(s_wo, 16)
                  sp.wait_ge(s_row, 1)
                  sp.dma_start(mod_d[:, :], modr).then_inc(s_rows, 16)
                  sp.wait_ge(s_rows, 32)

              @block.scalar
              def _(act):
                  act.dma_start(vrow[:, :], vecs[0:1, :].broadcast_to([P, 2 * HEADS + EXP])).then_inc(s_vec, 16)
                  act.dma_start(mupb, mup[0:1, :].broadcast_to([P, PROJ])).then_inc(s_ld, 16)
                  act.dma_start(nwc[:, :], nw).then_inc(s_ld, 16)
                  act.dma_start(dc[:, :], dcol).then_inc(s_ld, 16)
                  act.dma_start(gw[:, :, :], gwT).then_inc(s_ld, 16)
                  act.dma_start(cvp[:, :, :], convp).then_inc(s_ld, 16)
                  act.dma_start(win[:, :, :], w_in).then_inc(s_ld, 16)
                  act.wait_ge(s_c, 16)
                  nc.scalar.activation(sct[:, :, :], sct[:, :, :], ACT.Silu).then_inc(s_silu, 1)
                  act.wait_ge(s_vec, 16)
                  nc.scalar.activation(vrow[:, HEADS:2 * HEADS], vrow[:, HEADS:2 * HEADS], ACT.Exp).then_inc(s_expa, 1)

              @block.gpsimd
              def _(pool):
                  nc.gpsimd.memset(ones[:, :], 1.0).then_inc(s_const, 1)
                  nc.gpsimd.memset(mhalf[:, :], -0.5).then_inc(s_const, 1)
                  nc.gpsimd.memset(one_of_4[:, :, :], -1.0).then_inc(s_const, 1)
                  nc.gpsimd.memset(st[:, :, :], 1.0).then_inc(s_const, 1)
                  nc.gpsimd.memset(two_of_t[:, :, :], FAR).then_inc(s_const, 1)
                  pool.wait_ge(s_const, 5)
                  nc.gpsimd.affine_select(out=upto[:, :], in_=ones[:, :], compare_op=ALU.is_ge, fill=0.0, base=0,
                                          pattern=[[1, P]], channel_multiplier=-1).then_inc(s_const, 1)
                  nc.gpsimd.affine_select(out=before[:, :], in_=ones[:, :], compare_op=ALU.is_ge, fill=0.0, base=-1,
                                          pattern=[[1, P]], channel_multiplier=-1).then_inc(s_const, 1)
                  def keep(tile, pattern, base, by_row, op=ALU.is_ge):
                      nc.gpsimd.affine_select(out=tile, in_=tile, compare_op=op, fill=0.0, base=base, pattern=pattern,
                                              channel_multiplier=by_row).then_inc(s_const, 1)

                  keep(st[:, :, :].rearrange("p f (g s) -> p (f g) s", s=P), [[0, 16], [1, P]], 2 * (DEC - 1), -2)
                  keep(two_of_t[:, :, :], [[0, 4], [1, P]], 2 * DEC, -2)
                  pool.wait_ge(s_const, 9)
                  keep(two_of_t[:, :, :], [[0, 4], [-1, P]], 1 - 2 * DEC, 2)
                  keep(one_of_4[:, :, :], [[0, 4], [0, P]], DEC - 1, -1)
                  for n, off in enumerate(o for o in range(-3, 12) if o % 4):
                      pool.wait_ge(s_const, 11 + n)
                      keep(one_of_4[:, :, :], [[-1, 4], [0, P]], -3 - off, 1, ALU.not_equal)
                  pool.wait_ge(s_const, 23)
                  nc.gpsimd.tensor_tensor(one_of_4[:, :, :], one_of_4[:, :, :], two_of_t[:, :, :],
                                          ALU.add).then_inc(s_const, 1)
                  nc.gpsimd.tensor_tensor(ident[:, :], upto[:, :], before[:, :], ALU.subtract).then_inc(s_const, 1)
                  pool.wait_ge(s_mod, 6)
                  for i in range(2):
                      nc.gpsimd.memset(xdt[i][:, :, :], 0.0).then_inc(s_const, 1)

              @block.tensor
              def _(pe):
                  pe.wait_ge(s_silu, 1)
                  for j in range(6):
                      pe.wait_ge(s_wm[j], 16)
                      for k in range(KH):
                          last = nc.tensor.matmul(bank[j][0:BATCH, :], sct[:, k, :], wm[j][:, k, :],
                                                  start=(k == 0), stop=(k == KH - 1))
                      last.then_inc(s_mod, 1)
                  pe.wait_ge(s_row, 1)
                  pe.wait_ge(s_const, 27)
                  for j in range(8):
                      last = nc.tensor.transpose(bank[6][:, 4 * j:4 * j + 4], modr[:, P * j:P * (j + 1)],
                                                 ident[0:BATCH, 0:BATCH])
                  last.then_inc(s_modT, 1)

              @block.vector
              def _(dve):
                  steps = [0]

                  def link(instruction):
                      steps[0] += 1
                      instruction.then_inc(s_v, 1)
                      dve.wait_ge(s_v, steps[0])

                  sgn = hT[0:BATCH, 0, :]
                  for j in range(6):
                      row = modr[:, j * HID:(j + 1) * HID]
                      dve.wait_ge(s_mod, j + 1)
                      if j in (0, 3):
                          link(nc.vector.tensor_copy(row, bank[j][0:BATCH, :]))
                      elif j in (1, 4):
                          link(nc.vector.tensor_scalar(row, bank[j][0:BATCH, :], 1.0, None, ALU.add))
                      else:
                          link(nc.vector.tensor_scalar(sgn, bank[j][0:BATCH, :], 0.0, 2.0, ALU.is_ge, ALU.mult))
                          link(nc.vector.tensor_copy(row, bank[j][0:BATCH, :]))
                          link(nc.vector.scalar_tensor_tensor(out=row, in0=bank[j][0:BATCH, :], scalar=-1.0, in1=row,
                                                              op0=ALU.mult, op1=ALU.max))
                          link(nc.vector.tensor_scalar(row, row, 0.25, None, ALU.max))
                          last = nc.vector.scalar_tensor_tensor(out=row, in0=sgn, scalar=-1.0, in1=row,
                                                                op0=ALU.add, op1=ALU.mult)
                          if j == 5:
                              last.then_inc(s_row, 1)
                          else:
                              link(last)
                  dve.wait_ge(s_const, 27)
                  nc.vector.tensor_copy(mv[:, :, :].rearrange("p f (g c) -> p (f g) c", c=4 * P),
                                        one_of_4[:, :, :].rearrange("p (o j) t -> p o (j t)", o=1)
                                        .broadcast_to([ROWS, 16, 4 * P])).then_inc(s_mup, 1)
                  dve.wait_ge(s_modT, 1)
                  for r in range(0, HEADS, 32):
                      link(nc.vector.tensor_copy(head_of[r:r + 32, :].rearrange("p (h c) -> p h c", c=HD),
                                                 ident[r:r + 32, r:r + 32].rearrange("p (h o) -> p h o", o=1)
                                                 .broadcast_to([32, 32, HD])))
                  link(nc.vector.tensor_copy(modc[:, :, :].rearrange("p a b -> p (a b)"), bank[6][:, 0:32]))
                  dve.wait_ge(s_ld, 16 * 6)
                  for k in range(KH):
                      nc.vector.tensor_tensor(win[:, k, :], win[:, k, :], mupb, ALU.mult).then_inc(s_mup, 1)
                  dve.wait_ge(s_expa, 1)
                  nc.vector.tensor_scalar(vrow[:, HEADS:2 * HEADS], vrow[:, HEADS:2 * HEADS], -1.0, None,
                                          ALU.mult).then_inc(s_mup, 1)
                  dve.wait_ge(s_wo, 16)
                  for k in range(8):
                      nc.vector.tensor_scalar(wout[:, k, :], wout[:, k, :], nwc[:, k:k + 1], None,
                                              ALU.mult).then_inc(s_mup, 1)

        h2 = sb("h2", [P, HID])

        full = [sem(f"full{i}") for i in range(8)]
        free = [sem(f"free{i}") for i in range(8)]
        names = """s_agg s_arg s_bc s_conv s_cumd s_dtv s_dx s_ecx s_exp s_exps s_fill s_g s_h2 s_heads
                   s_lg s_m s_modb s_parts s_pl2 s_pool s_pre s_rms s_rs2 s_rstd s_sh
                   s_silu2 s_std s_step s_sx s_u s_x2b s_xdt s_xn s_xn2 s_xres
                   s_xw s_yacc""".split()
        S = {n: sem(n) for n in names}
        s_xin = sem("s_xin")
        rows_in = [sem(f"rows_in{i}") for i in range(2)]
        per_loop = full + free + list(S.values()) + rows_in + [s_xin]

        def b3(ap, n):
            return ap.rearrange("p (h o) -> p h o", o=1).broadcast_to([P, ap.shape[1], n])

        def h3(ap):
            return ap.rearrange("p (h d) -> p h d", d=HD)

        def read(eng, name, where=place):
            eng.wait_ge(free[where[name][0]], where[name][1])

        def clear_semaphores():
            with nc.Block() as block:
                @block.gpsimd
                def _(pool):
                    for s in per_loop:
                        pool.sem_clear(s)

        def stats(link, q):
            link(nc.vector.bn_stats(bnst[:, q, :], x_in[:, q, :]))
            nc.vector.bn_aggr(mv4[:, q, :], bnst[:, q, :]).then_inc(S["s_rstd"], 1)

        def deviations(pool, link):
            pool.wait_ge(S["s_rstd"], NQ)
            link(nc.gpsimd.tensor_scalar(rs4[:, :], mv4[:, :, 1], EPS, None, ALU.add))
            nc.gpsimd.tensor_tensor(rs4[:, :], rs4[:, :], mhalf[:, :], ALU.pow).then_inc(S["s_pl2"], 1)

        def normed(dve, q):
            if q == 0:
                dve.wait_ge(S["s_pl2"], 1)
            nc.vector.tensor_scalar(x_in[:, q, :], x_in[:, q, :], mv4[:, q, 0:1], rs4[:, q:q + 1],
                                    ALU.subtract, ALU.mult).then_inc(S["s_xn"], 1)

        def ahead(pe, name, t, where):
            if name[0] == "h":
                pe.wait_ge(S["s_xn"], NQ)
                for q in range(NQ):
                    last = nc.tensor.transpose(t[:, q * P:(q + 1) * P], x_in[:, q, name[1] * P:(name[1] + 1) * P],
                                               ident[:, :])
            elif name[0] == "dt":
                for k in range(KH):
                    read(pe, ("h", k), where)
                for q in range(NQ):
                    for k in range(KH):
                        last = nc.tensor.matmul(t[:, q * HEADS:(q + 1) * HEADS], hT[:, k, q * P:(q + 1) * P],
                                                win[:, k, PROJ - HEADS:PROJ], start=(k == 0), stop=(k == KH - 1))
            else:
                for k in range(KH):
                    last = nc.tensor.matmul(t[:, :], win[:, k, name[1] * P:(name[1] + 1) * P], hT[:, k, :],
                                            start=(k == 0), stop=(k == KH - 1))
            last.then_inc(full[where[name][0]], 1)

        def ahead_read(act, name, where):
            t = bank[where[name][0]]
            if name[0] == "h":
                act.wait_ge(S["s_modb"], 1)
                act.wait_ge(full[where[name][0]], where[name][1])
                k = name[1]
                nc.scalar.activation(hT[:, k, :], t[:, :], ACT.Identity, bias=modb[:, k:k + 1],
                                     scale=modb[:, 4 + k:5 + k]).then_inc(free[where[name][0]], 1)
            elif name[0] == "dt":
                act.wait_ge(S["s_dtv"], 1)
                nc.scalar.activation(u, u, ACT.Exp, scale=-1.0).then_inc(S["s_u"], 1)
            else:
                act.wait_ge(full[where[name][0]], where[name][1])
                nc.scalar.activation(zs[:, name[1], :], t[:, :], ACT.Silu).then_inc(free[where[name][0]], 1)

        def dt_sum(dve, where):
            k, n = where[("dt",)]
            dve.wait_ge(full[k], n)
            nc.vector.tensor_tensor(dt[:, :].rearrange("p (q h) -> p q h", q=NQ),
                                    bank[k][:, 0:256].rearrange("p (q h) -> p q h", q=NQ),
                                    vrow[:, 0:HEADS].rearrange("p (o h) -> p o h", o=1)
                                    .broadcast_to([P, NQ, HEADS]), ALU.add).then_inc(free[k], 1)
            read(dve, ("dt",), where)
            nc.vector.scalar_tensor_tensor(out=u, in0=dt[:, :], scalar=-1.0, in1=dt[:, :], op0=ALU.mult,
                                           op1=ALU.max).then_inc(S["s_dtv"], 1)

        def softplus(dve, link):
            v = dt[:, :]
            dve.wait_ge(S["s_u"], 1)
            link(nc.vector.tensor_scalar(s1, u, 2.0, None, ALU.add))
            link(nc.vector.reciprocal(s1, s1))
            link(nc.vector.tensor_tensor(s1, s1, u, ALU.mult))
            link(nc.vector.tensor_tensor(s2, s1, s1, ALU.mult))
            link(nc.vector.tensor_scalar(p1, s2, 1.0 / 13, None, ALU.mult))
            for d in (11, 9, 7, 5, 3):
                link(nc.vector.scalar_tensor_tensor(out=p1, in0=p1, scalar=1.0 / d, in1=s2, op0=ALU.add,
                                                    op1=ALU.mult))
            link(nc.vector.scalar_tensor_tensor(out=p1, in0=p1, scalar=1.0, in1=s1, op0=ALU.add, op1=ALU.mult))
            link(nc.vector.tensor_scalar(v, v, 0.0, None, ALU.max))
            link(nc.vector.scalar_tensor_tensor(out=v, in0=p1, scalar=2.0, in1=v, op0=ALU.mult, op1=ALU.add))
            link(nc.vector.tensor_tensor(a_log.rearrange("p (q h) -> p q h", q=NQ),
                                         v.rearrange("p (q h) -> p q h", q=NQ),
                                         vrow[:, HEADS:2 * HEADS].rearrange("p (o h) -> p o h", o=1)
                                         .broadcast_to([P, NQ, HEADS]), ALU.mult))
            link(nc.vector.tensor_scalar(a_log, a_log, LOWEST, None, ALU.max))

        with nc.Block() as block:
            @block.gpsimd
            def _(pool):
                def link(instruction):
                    instruction.then_inc(S["s_pool"], 1)
                    pool.wait_ge(S["s_pool"], 1)

                deviations(pool, link)

            @block.tensor
            def _(pe):
                for name, (k, n) in first.items():
                    if n > 1:
                        pe.wait_ge(free[k], n - 1)
                    ahead(pe, name, bank[k], first)

            @block.scalar
            def _(act):
                for name in first:
                    ahead_read(act, name, first)

            @block.vector
            def _(dve):
                steps = [0]

                def link(instruction):
                    steps[0] += 1
                    instruction.then_inc(S["s_step"], 1)
                    dve.wait_ge(S["s_step"], steps[0])

                nc.vector.tensor_copy(modb[:, :], modc[:, :, 0]).then_inc(S["s_modb"], 1)
                for q in range(NQ):
                    stats(link, q)
                for q in range(NQ):
                    normed(dve, q)
                dt_sum(dve, first)
                softplus(dve, link)
        clear_semaphores()


        with nc.Fori(0, BATCH) as b:
            with nc.Block() as block:
                @block.sync
                def _(sp):
                    sp.dma_start(x_in[:, :, :], x[bass.ds((b + 1) % BATCH, 1)]
                                 .rearrange("o (q p) d -> p (o q) d", p=P)).then_inc(s_xin, 16)
                    for j, dst in ((2, ga_b), (4, cb_b), (3, sb_b)):
                        sp.dma_start(dst[:, :], mod_d[bass.ds(b, 1), j * HID:(j + 1) * HID]
                                     .broadcast_to([P, HID])).then_inc(S["s_bc"], 16)
                    sp.wait_ge(S["s_parts"], 3)
                    sp.dma_start(cum_d[:, :, :], parts[:, :, :]).then_inc(S["s_cumd"], 16)
                    sp.wait_ge(S["s_cumd"], 16)
                    cq = cum_d.rearrange("(f g j) i (q t) -> q f i j g t", f=2, j=4, t=P)
                    cm = cum_d.rearrange("(f h) i (q t) -> q f i h t", f=2, t=P)

                    def decay_rows(q, f):
                        n = 2 * q + f
                        if q:
                            sp.wait_ge(S["s_arg"], 8 * (q - 1) + 4 * f + 4)
                        sp.dma_start(mv[0:3, f, :].rearrange("i (h t) -> i h t", t=P), cm[q, f]).then_inc(rows_in[f], 16)
                        for i in range(3):
                            sp.dma_start(st[3 + 4 * i:7 + 4 * i, f, :].rearrange("j (g t) -> j g t", t=P),
                                         cq[q, f, i]).then_inc(rows_in[f], 16)

                    decay_rows(0, 0)
                    decay_rows(0, 1)
                    def residual(q):
                        if q:
                            sp.wait_ge(S["s_sx"], 16 * q)
                            sp.wait_ge(S["s_xn2"], q)
                        else:
                            for i in range(2):
                                k, n = place[("u", 0, i)]
                                sp.wait_ge(full[k], n)
                        sp.dma_start(x2, x[bass.ds(b, 1), q * P:(q + 1) * P, :]
                                     .rearrange("o p d -> (o p) d")).then_inc(S["s_xres"], 16)

                    def store(q):
                        sp.wait_ge(S["s_x2b"], q + 1)
                        sp.dma_start(x2_d[bass.ds(b * SEQ + q * P, P), :], x2[:, :]).then_inc(S["s_sx"], 16)
                        sp.wait_ge(S["s_h2"], q + 1)
                        sp.dma_start(h2_d[bass.ds(b * SEQ + q * P, P), :], h2[:, :]).then_inc(S["s_sh"], 16)

                    residual(0)
                    for q in range(NQ):
                        if q + 1 < NQ:
                            decay_rows(q + 1, 0)
                            decay_rows(q + 1, 1)
                        if q == NQ - 2:
                            part = (SLOTS - USED) // BATCH
                            sp.dma_start(ys_d[bass.ds((b * part + USED) * P, part * P), :].rearrange("(n p) d -> p n d", p=P),
                                         wout[:, 0:1, :].broadcast_to([P, part, HID])).then_inc(S["s_fill"], 16)
                        if q:
                            store(q - 1)
                            residual(q)
                    store(NQ - 1)
                    sp.wait_ge(S["s_fill"], 16)
                    sp.wait_ge(S["s_sx"], 16 * NQ)
                    sp.wait_ge(S["s_sh"], 16 * NQ)
                    sp.wait_ge(s_xin, 16)

                @block.tensor
                def _(pe):
                    def open_bank(name):
                        k, n = place[name]
                        if n > 1:
                            pe.wait_ge(free[k], n - 1)
                        return bank[k]

                    def close_bank(name, last):
                        last.then_inc(full[place[name][0]], 1)

                    for name in order_a:
                        kind = name if isinstance(name, str) else name[0]
                        t = open_bank(name)
                        if kind == "ch":
                            c0 = DI + CH[name[1]] * P
                            for k in range(KH):
                                last = nc.tensor.matmul(t[:, :], win[:, k, c0:c0 + P], hT[:, k, :],
                                                        start=(k == 0), stop=(k == KH - 1))
                        elif kind == "cum":
                            nc.tensor.matmul(t[:, 0:256], upto[:, :], a_log, start=True, stop=True)
                            last = nc.tensor.matmul(t[:, 256:512], ones[:, :], a_log, start=True, stop=True)
                        elif kind == "cumT":
                            read(pe, "cum")
                            for q in range(NQ):
                                last = nc.tensor.transpose(t[0:HEADS, q * P:(q + 1) * P],
                                                           cums[:, q * HEADS:(q + 1) * HEADS], ident[:, :])
                        elif kind == "turn":
                            n = name[1]
                            pe.wait_ge(S["s_silu2"], n + 1)
                            src = BT if n == 0 else cv[:, n % 4, :]
                            for q in range(NQ):
                                last = nc.tensor.transpose(t[:, q * P:(q + 1) * P], src[:, q * P:(q + 1) * P],
                                                           ident[:, :])
                        else:
                            c0 = name[1] * P
                            for k in range(KH):
                                last = nc.tensor.matmul(t[:, :], win[:, k, c0:c0 + P], hT[:, k, :],
                                                        start=(k == 0), stop=(k == KH - 1))
                        close_bank(name, last)

                    def arg(q, a):
                        n = q * NG + a
                        if n == 0:
                            for k in range(4):
                                pe.wait_ge(free[k], stage_a[k])
                        if n >= 2:
                            pe.wait_ge(S["s_exp"], n - 1)
                        if a % 4 == 0:
                            pe.wait_ge(rows_in[a // 4], 64 * (q + 1))
                        for i in range(2):
                            gl = (a % 4) * 2 + i
                            last = nc.tensor.matmul(bank[2 * (n % 2) + i][:, :], st[:, a // 4, gl * P:(gl + 1) * P],
                                                    mv[:, a // 4, gl * 512:(gl + 1) * 512], start=True, stop=True)
                        last.then_inc(S["s_arg"], 1)

                    def heads(q, a):
                        n = q * NG + a
                        name = ("y", q, a // 4)
                        if a % 4 == 0:
                            open_bank(name)
                        t = bank[place[name][0]][:, (a % 4) * P:(a % 4 + 1) * P]
                        if a == 0:
                            pe.wait_ge(S["s_xdt"], q + 1)
                        pe.wait_ge(S["s_m"], n + 1)
                        rows = xdt[q % 2][:, :, :].rearrange("p h c -> p (h c)")
                        for odd in range(2):
                            for pair in range(GRP // 2):
                                i = 2 * pair + odd
                                c = (a * GRP + i) * 2 * HD - odd * HD
                                last = nc.tensor.matmul(t[32 * pair:32 * (pair + 1), :], rows[:, c:c + 2 * HD],
                                                        M[n % 3][:, i * P:(i + 1) * P], start=(odd == 0),
                                                        stop=(odd == 1))
                        last.then_inc(S["s_heads"], 1)

                    def work(name):
                        if name[0] == "dt" or (name[0] == "z" and name[1] < 4):
                            pe.wait_ge(S["s_exp"], NQ * NG)
                        t = open_bank(name)
                        if name[0] in ("h", "dt", "z"):
                            ahead(pe, name, t, place)
                            return
                        kind, q = name[0], name[1]
                        if kind == "cb":
                            if q == 0:
                                read(pe, ("turn", NCH - 1))
                            last = nc.tensor.matmul(t[:, 0:P], BT[:, q * P:(q + 1) * P], CT[:, q * P:(q + 1) * P],
                                                    start=True, stop=True)
                        elif kind == "ex":
                            for j in range(4):
                                h = slice(32 * name[2], 32 * name[2] + 32)
                                for i in range(3):
                                    last = nc.tensor.matmul(t[:, j * P:(j + 1) * P], head_of[h, j * P:(j + 1) * P],
                                                            parts[h, i, q * P:(q + 1) * P],
                                                            start=(i == 0), stop=(i == 2))
                        elif kind == "inter":
                            for i in range(2 if name[2] == 0 else 0):
                                read(pe, ("u", q - 1, i))
                            for j in range(4):
                                c = (4 * name[2] + j) * P
                                last = nc.tensor.matmul(t[:, j * P:(j + 1) * P], state[:, c:c + P],
                                                        CT[:, q * P:(q + 1) * P], start=True, stop=True)
                        elif kind == "u":
                            pe.wait_ge(S["s_xw"], q + 1)
                            c = name[2] * 512
                            last = nc.tensor.matmul(t[:, :], B_t[:, q, :], x_t[:, q, c:c + 512], start=True, stop=True)
                        elif kind == "ss":
                            pe.wait_ge(S["s_g"], 2 * (q + 1))
                            for k in range(8):
                                last = nc.tensor.matmul(t[:, 0:P], yg[:, q % 2, k, :], yg[:, q % 2, k, :],
                                                        start=(k == 0), stop=(k == 7))
                        elif kind == "wo":
                            for k in range(8):
                                last = nc.tensor.matmul(t[:, :], yg[:, q % 2, k, :], wout[:, k, :], start=(k == 0),
                                                        stop=(k == 7))
                        elif kind == "h2T":
                            pe.wait_ge(S["s_h2"], q + 1)
                            for k in range(KH):
                                last = nc.tensor.transpose(t[:, k * P:(k + 1) * P], h2[:, k * P:(k + 1) * P],
                                                           ident[:, :])
                        else:
                            read(pe, ("h2T", q))
                            for k in range(KH):
                                last = nc.tensor.matmul(t[:, 0:EXP], h2T[:, k, :], gw[:, k, :], start=(k == 0),
                                                        stop=(k == KH - 1))
                        close_bank(name, last)

                    for name in work_at(-1, 4):
                        work(name)
                    arg(0, 0)
                    arg(0, 1)
                    for a in range(5, NG):
                        for name in work_at(-1, a):
                            work(name)
                    for q in range(NQ + 1):
                        for a in range(NG):
                            n = q * NG + a
                            if n + 2 < NQ * NG:
                                arg(*divmod(n + 2, NG))
                            if q < NQ:
                                heads(q, a)
                            for name in work_at(q, a):
                                work(name)

                @block.scalar
                def _(act):
                    def filled(name):
                        k, n = place[name]
                        act.wait_ge(full[k], n)
                        return bank[k]

                    def to_pre(n):
                        if n >= 4:
                            act.wait_ge(S["s_conv"], n - 3)
                        t = filled(("ch", n))
                        k = place[("ch", n)][0]
                        nc.scalar.activation(pre[:, n % 4, TAPS - 1:], t[:, :], ACT.Copy).then_inc(free[k], 1)

                    t = filled("cum")
                    nc.scalar.activation(etot[:, :], t[:, 256:512], ACT.Exp).then_inc(S["s_exps"], 1)
                    read(act, "cum")
                    nc.scalar.activation(edec[:, :], edec[:, :], ACT.Exp).then_inc(S["s_exps"], 1)
                    for n in range(2):
                        to_pre(n)

                    def turned(n):
                        t = filled(("turn", n))
                        k = place[("turn", n)][0]
                        c = CH[n]
                        dst = x_t[:, :, c * P:(c + 1) * P] if n else B_t[:, :, :]
                        src = t[:, :].rearrange("p (q c) -> p q c", c=P)
                        nc.scalar.activation(dst, src if n else src[:, 0:NQ - 1, :], ACT.Copy) \
                            .then_inc(free[k], 1)

                    def times_d(n):
                        act.wait_ge(S["s_silu2"], n + 1)
                        c = CH[n]
                        nc.scalar.activation(Dx[:, c, :], cv[:, n % 4, :], ACT.Copy,
                                             scale=dc[:, c:c + 1]).then_inc(S["s_dx"], 1)

                    def silu_z(j):
                        t = filled(("z", j))
                        nc.scalar.activation(zs[:, j, :], t[:, :], ACT.Silu).then_inc(free[place[("z", j)][0]], 1)

                    for n in range(NCH):
                        act.wait_ge(S["s_conv"], n + 1)
                        dst = {0: BT[:, :], 1: CT[:, :]}.get(n, cv[:, n % 4, :])
                        nc.scalar.activation(dst, cv[:, n % 4, :], ACT.Silu).then_inc(S["s_silu2"], 1)
                        if n + 2 < NCH:
                            to_pre(n + 2)
                        if n >= 3:
                            times_d(n - 1)
                        if n - 1 in TURNED:
                            turned(n - 1)
                    times_d(NCH - 1)
                    silu_z(4)
                    silu_z(5)
                    turned(NCH - 1)

                    for m in range((NQ + 1) * NG + 2):
                        if m < NQ * NG:
                            act.wait_ge(S["s_arg"], m + 1)
                            if m >= 3:
                                act.wait_ge(S["s_heads"], m - 2)
                            for i in range(2):
                                ins = nc.scalar.activation(M[m % 3][:, i * 512:(i + 1) * 512],
                                                           bank[2 * (m % 2) + i][:, :], ACT.Exp)
                            ins.then_inc(S["s_exp"], 1)
                        before_q, before_a = divmod(m - 2, NG)
                        for name in work_at(before_q, before_a):
                            if name[0] in ("h", "dt", "z"):
                                if name[0] == "z" and name[1] < 4:
                                    act.wait_ge(S["s_g"], 2 * NQ - 1)
                                ahead_read(act, name, place)
                            if name[0] == "ex":
                                t = filled(name)
                                i = name[2]
                                if before_q > 0:
                                    read(act, ("inter", before_q, i))
                                nc.scalar.activation(ecx[:, i * 512:(i + 1) * 512], t[:, :],
                                                     ACT.Exp).then_inc(free[place[name][0]], 1)
                            if name[0] == "h2T":
                                t = filled(name)
                                nc.scalar.activation(h2T[:, :, :].rearrange("p k t -> p (k t)"), t[:, :],
                                                     ACT.Copy).then_inc(free[place[name][0]], 1)

                @block.gpsimd
                def _(pool):
                    steps = [0]

                    def link(instruction):
                        steps[0] += 1
                        instruction.then_inc(S["s_pool"], 1)
                        pool.wait_ge(S["s_pool"], steps[0])

                    nc.gpsimd.memset(pre[:, :, 0:TAPS - 1], 0.0).then_inc(S["s_pre"], 1)

                    def norm_rows(q):
                        read(pool, ("ss", q))
                        link(nc.gpsimd.tensor_scalar(rms[:, :], ss[:, :], 1.0 / DI, EPS, ALU.mult, ALU.add))
                        nc.gpsimd.tensor_tensor(rms[:, :], rms[:, :], mhalf[:, 0:1], ALU.pow).then_inc(S["s_rms"], 1)

                    def norm2(q):
                        pool.wait_ge(S["s_agg"], q + 1)
                        link(nc.gpsimd.tensor_scalar(rs2[:, :], mv2[:, 1:2], EPS, None, ALU.add))
                        nc.gpsimd.tensor_tensor(rs2[:, :], rs2[:, :], mhalf[:, 0:1], ALU.pow).then_inc(S["s_rs2"], 1)
                        pool.wait_ge(S["s_xn2"], q + 1)
                        if q == 0:
                            pool.wait_ge(S["s_bc"], 48)
                        link(nc.gpsimd.tensor_tensor(h2[:, :], h2[:, :], cb_b[:, :], ALU.mult))
                        nc.gpsimd.tensor_tensor(h2[:, :], h2[:, :], sb_b[:, :], ALU.add).then_inc(S["s_h2"], 1)

                    def chunk_inputs(q):
                        c = slice(q * HEADS, (q + 1) * HEADS)
                        if q >= 2:
                            pool.wait_ge(S["s_heads"], NG * (q - 1))
                        rows = xdt[q % 2][:, :, 0:HD]
                        nc.gpsimd.tensor_tensor(rows, h3(x_t[:, q, :]), b3(dt[:, c], HD),
                                                ALU.mult).then_inc(S["s_xdt"], 1)
                        if q < NQ - 1:
                            pool.wait_ge(S["s_xdt"], q + 1)
                            nc.gpsimd.tensor_tensor(h3(x_t[:, q, :]), rows, b3(edec[:, c], HD),
                                                    ALU.mult).then_inc(S["s_xw"], 1)

                    for n in TURNED:
                        read(pool, ("turn", n))
                    pool.wait_ge(S["s_exps"], 2)
                    chunk_inputs(0)
                    for q in range(NQ + 1):
                        if 0 < q < NQ:
                            for i in range(2):
                                read(pool, ("inter", q, i))
                            if q < NQ - 1:
                                c = slice(q * HEADS, (q + 1) * HEADS)
                                nc.gpsimd.tensor_tensor(h3(state[:, :]), h3(state[:, :]), b3(etot[:, c], HD),
                                                        ALU.mult).then_inc(S["s_std"], 1)
                            y = yg[:, q % 2, :, :]
                            nc.gpsimd.tensor_tensor(y, y, Dx[:, :, q * P:(q + 1) * P], ALU.add).then_inc(S["s_yacc"], 1)
                        if q:
                            norm_rows(q - 1)
                            norm2(q - 1)
                        if q + 1 < NQ:
                            chunk_inputs(q + 1)
                        if q == NQ - 2:
                            deviations(pool, link)

                @block.vector
                def _(dve):
                    steps = [0]

                    def link(instruction):
                        steps[0] += 1
                        instruction.then_inc(S["s_step"], 1)
                        dve.wait_ge(S["s_step"], steps[0])

                    def filled(name):
                        k, n = place[name]
                        dve.wait_ge(full[k], n)
                        return bank[k]

                    def reads(name, instruction):
                        instruction.then_inc(free[place[name][0]], 1)
                        read(dve, name)

                    def conv(n):
                        c = CH[n]
                        if n == 0:
                            dve.wait_ge(S["s_pre"], 1)
                        if n >= 4:
                            if n - 4 in TURNED[1:]:
                                k, m = place[("turn", n - 4)]
                                dve.wait_ge(full[k], m)
                                dve.wait_ge(S["s_dx"], n - 5)
                            else:
                                dve.wait_ge(S["s_silu2"], n - 3)
                        k, m = place[("ch", n)]
                        dve.wait_ge(free[k], m)
                        link(nc.vector.tensor_scalar(cv[:, n % 4, :], pre[:, n % 4, 0:SEQ], cvp[:, c, 0:1],
                                                     cvp[:, c, TAPS:TAPS + 1], ALU.mult, ALU.add))
                        for tap in range(1, TAPS):
                            ins = nc.vector.scalar_tensor_tensor(out=cv[:, n % 4, :], in0=pre[:, n % 4, tap:tap + SEQ],
                                                                 scalar=cvp[:, c, tap:tap + 1], in1=cv[:, n % 4, :],
                                                                 op0=ALU.mult, op1=ALU.add)
                            if tap < TAPS - 1:
                                link(ins)
                            else:
                                ins.then_inc(S["s_conv"], 1)

                    t = filled("cum")
                    dve.wait_ge(S["s_exps"], 1)
                    link(nc.vector.tensor_copy(cums[:, :], t[:, 0:256]))
                    reads("cum", nc.vector.tensor_tensor(edec[:, :], t[:, 256:512], cums[:, :], ALU.subtract))
                    conv(0)
                    t = filled("cumT")
                    nc.vector.tensor_copy(parts[:, 0, :], t[0:HEADS, :]).then_inc(S["s_parts"], 1)
                    dve.wait_ge(S["s_parts"], 1)
                    reads("cumT", nc.vector.tensor_tensor(rest, t[0:HEADS, :], parts[:, 0, :], ALU.subtract))
                    nc.vector.tensor_copy(parts[:, 1, :], rest).then_inc(S["s_parts"], 1)
                    dve.wait_ge(S["s_parts"], 2)
                    link(nc.vector.tensor_tensor(rest, rest, parts[:, 1, :], ALU.subtract))
                    nc.vector.tensor_copy(parts[:, 2, :], rest).then_inc(S["s_parts"], 1)
                    for n in range(1, NCH):
                        conv(n)

                    def gate(q, i):
                        dve.wait_ge(S["s_heads"], NG * q + 4 * (i + 1))
                        t = bank[place[("y", q, i)][0]][:, :].rearrange("p (j t) -> p j t", t=P)
                        tiles, now = slice(4 * i, 4 * i + 4), slice(q * P, (q + 1) * P)
                        y = yg[:, q % 2, tiles, :]
                        if i == 0:
                            if q:
                                dve.wait_ge(S["s_yacc"], q)
                            dve.wait_ge(S["s_dx"], NCH - 2)
                        else:
                            read(dve, ("z", 2 * NQ - 1))
                        reads(("y", q, i), nc.vector.tensor_tensor(y, y if q else Dx[:, tiles, now], t, ALU.add))
                        nc.vector.tensor_tensor(y, y, zs[:, tiles, now], ALU.mult).then_inc(S["s_g"], 1)

                    def after(q, name):
                        kind, p1 = name[0], name[-1 if len(name) < 3 else 1]
                        if kind in ("h2T", "ex", "h", "z"):
                            return
                        if kind == "dt":
                            dt_sum(dve, place)
                            return
                        t = filled(name)
                        if kind == "cb":
                            reads(name, nc.vector.tensor_tensor(cbm[p1 % 2][:, :], t[:, 0:P], upto[:, :], ALU.mult))
                        elif kind == "inter":
                            i = name[2]
                            dve.wait_ge(free[place[("ex", q, i)][0]], place[("ex", q, i)][1])
                            nc.vector.tensor_tensor(yg[:, q % 2, 4 * i:4 * i + 4, :].rearrange("p j t -> p (j t)"),
                                                    t[:, :], ecx[:, i * 512:(i + 1) * 512],
                                                    ALU.mult).then_inc(free[place[name][0]], 1)
                        elif kind == "ss":
                            nc.vector.scalar_tensor_tensor(
                                out=t[:, 0:P], in0=t[:, 0:P], scalar=1.0, in1=ident[:, :], op0=ALU.mult,
                                op1=ALU.mult, accum_out=ss[:, :]).then_inc(free[place[name][0]], 1)
                        elif kind == "wo":
                            dve.wait_ge(S["s_rms"], p1 + 1)
                            if p1 == 0:
                                dve.wait_ge(S["s_bc"], 48)
                            else:
                                dve.wait_ge(S["s_sh"], 16 * p1)
                                read(dve, ("h2T", p1 - 1))
                            reads(name, nc.vector.scalar_tensor_tensor(
                                out=h2[:, :], in0=t[:, :], scalar=rms[:, 0:1], in1=ga_b[:, :], op0=ALU.mult,
                                op1=ALU.mult))
                            dve.wait_ge(S["s_xres"], 16 * (p1 + 1))
                            nc.vector.tensor_tensor(x2, x2, h2[:, :], ALU.add).then_inc(S["s_x2b"], 1)
                            dve.wait_ge(S["s_x2b"], p1 + 1)
                            link(nc.vector.bn_stats(bn2[:, :], x2))
                            nc.vector.bn_aggr(mv2[:, :], bn2[:, :]).then_inc(S["s_agg"], 1)
                        elif kind == "u":
                            half = slice(name[2] * 512, (name[2] + 1) * 512)
                            if q == 0:
                                ins = nc.vector.tensor_copy(state[:, half], t[:, :])
                            else:
                                dve.wait_ge(S["s_std"], q)
                                ins = nc.vector.tensor_tensor(state[:, half], state[:, half], t[:, :], ALU.add)
                            ins.then_inc(free[place[name][0]], 1)
                        elif kind == "lg":
                            reads(name, nc.vector.tensor_tensor(lg[:, :], t[:, 0:EXP], vrow[:, 2 * HEADS:], ALU.add))
                            link(nc.vector.max(tv[:, p1, :], lg[:, :]))
                            nc.vector.max_index(ti[:, p1, :], tv[:, p1, :], lg[:, :]).then_inc(S["s_lg"], 1)

                    for name in work_at(-1, 4):
                        after(-1, name)
                    for q in range(NQ + 1):
                        for a in range(NG):
                            if q < NQ:
                                n = q * NG + a
                                dve.wait_ge(S["s_exp"], n + 1)
                                nc.vector.tensor_tensor(
                                    M[n % 3].rearrange("p (h t) -> p h t", t=P),
                                    M[n % 3].rearrange("p (h t) -> p h t", t=P),
                                    cbm[q % 2][:, :].rearrange("p (o t) -> p o t", o=1).broadcast_to([P, GRP, P]),
                                    ALU.mult).then_inc(S["s_m"], 1)
                            for late in (2, 1):
                                before_q, before_a = divmod(q * NG + a - late, NG)
                                for name in work_at(before_q, before_a) if before_q >= 0 else []:
                                    if (name[0] == "wo") == (late == 2):
                                        after(before_q, name)
                            if q and a == 0:
                                gate(q - 1, 1)
                            if q == NQ - 2 and a > 3:
                                if a == 4:
                                    dve.wait_ge(s_xin, 16)
                                stats(link, a - 4)
                            if q == NQ - 1 and a < 4:
                                normed(dve, a)
                            if q == NQ - 1 and a == 2:
                                nc.vector.tensor_copy(modb[:, :], modc[:, :, bass.ds((b + 1) % BATCH, 1)]
                                                      .rearrange("p a o -> p (a o)")).then_inc(S["s_modb"], 1)
                            if q and a == 4:
                                p1 = q - 1
                                dve.wait_ge(S["s_rs2"], p1 + 1)
                                nc.vector.tensor_scalar(h2[:, :], x2, mv2[:, 0:1], rs2[:, 0:1], ALU.subtract,
                                                        ALU.mult).then_inc(S["s_xn2"], 1)
                            if q < NQ and a == 5:
                                gate(q, 0)
                            if q == NQ and a == 2:
                                softplus(dve, link)
                    dve.wait_ge(S["s_lg"], NQ)
                    nc.vector.tensor_copy(top_v[:, bass.ds(b * NQ, NQ), :], tv[:, :, 0:TOPK]).then_inc(S["s_step"], 1)
                    nc.vector.tensor_copy(top_i[:, bass.ds(b * NQ, NQ), :], ti[:, :, 0:TOPK]).then_inc(S["s_step"], 1)
            clear_semaphores()


def experts(nc, wexp, bexp, mod_d, x2_d, h2_d, ys_d, out, bank, ident, upto, ones, top_v, top_i):
    TK = NT * TOPK
    COLS = SLOTS + 4
    with ExitStack() as ctx:
        def sb(name, shape, dt=F32, c=ctx):
            return c.enter_context(nc.sbuf_tensor(name, shape, dt))

        def sem(name):
            return ctx.enter_context(nc.semaphore(name))

        idx = sb("idx", [P, COLS], I32)
        tab_e = sb("tab_e", [1, COLS], I32)
        tab_n = sb("tab_n", [1, COLS], I32)
        tab_r = sb("tab_r", [1, COLS + 1], I32)
        tab_u = sb("tab_u", [1, SLOTS // 4], I32)
        dest = sb("dest", [P, TK], I32)
        wts = sb("wts", [P, TK])

        with ExitStack() as rt:
            def tb(name, shape, dt=F32):
                return sb(name, shape, dt, rt)

            iota_e = tb("iota_e", [P, EXP])
            iota_s = tb("iota_s", [P, COLS])
            iota_r = tb("iota_r", [P, P])
            tok = tb("tok", [P, NT])
            topf = tb("topf", [P, TK])
            hot = tb("hot", [P, TK, EXP])
            chosen = tb("chosen", [P, NT, EXP])
            acc = tb("acc", [P, NT + 1, EXP])
            cnt_i = tb("cnt_i", [P, EXP], I32)
            ntf = tb("ntf", [P, EXP])
            cin = tb("cin", [P, EXP])
            base = tb("base", [P, EXP])
            pos = tb("pos", [P, NT, EXP])
            destf = tb("destf", [P, TK])
            desti = tb("desti", [P, TK], I32)
            hi_i = tb("hi_i", [P, TK], I32)
            lo = tb("lo", [P, TK])
            hi = tb("hi", [P, TK])
            in_row = tb("in_row", [P, TK, P], F32R)
            in_slot = tb("in_slot", [P, TK, SLOTS], F32R)
            cmp = tb("cmp", [P, COLS, EXP])
            used = tb("used", [1, SLOTS // 4])
            before = tb("before", [P, P])
            eid = tb("eid", [P, COLS])
            new = tb("new", [P, COLS])
            cnew = tb("cnew", [P, COLS])
            ev = tb("ev", [P, TK])
            ws = tb("ws", [P, NT])
            r_const = sem("r_const")
            r_step = sem("r_step")
            r_chosen = sem("r_chosen")
            r_pos = sem("r_pos")
            r_dest = sem("r_dest")
            r_row = sem("r_row")
            r_slot = sem("r_slot")
            r_tok = sem("r_tok")
            r_idx = sem("r_idx")
            r_ev = sem("r_ev")
            r_exp = sem("r_exp")
            HALF = TK // 2
            with nc.Block() as block:
                @block.gpsimd
                def _(pool):
                    nc.gpsimd.iota(iota_e[:, :], pattern=[[1, EXP]], base=0, channel_multiplier=0,
                                   allow_small_or_imprecise_dtypes=True).then_inc(r_const, 1)
                    nc.gpsimd.iota(iota_s[:, :], pattern=[[1, COLS]], base=0, channel_multiplier=0,
                                   allow_small_or_imprecise_dtypes=True).then_inc(r_const, 1)
                    nc.gpsimd.iota(iota_r[:, :], pattern=[[1, P]], base=0, channel_multiplier=0,
                                   allow_small_or_imprecise_dtypes=True).then_inc(r_const, 1)
                    nc.gpsimd.iota(tok[:, :], pattern=[[P, NT]], base=0, channel_multiplier=1,
                                   allow_small_or_imprecise_dtypes=True).then_inc(r_const, 1)
                    nc.gpsimd.memset(idx[:, SLOTS:], 0).then_inc(r_const, 1)

                @block.scalar
                def _(act):
                    act.wait_ge(r_ev, 1)
                    nc.scalar.activation(ev[:, :], ev[:, :], ACT.Exp).then_inc(r_exp, 1)
                    act.wait_ge(r_slot, 1)
                    for t in range(NT):
                        c = slice(t * TOPK, (t + 1) * TOPK)
                        nc.scalar.activation(in_slot[:, c, :], in_slot[:, c, :], ACT.Copy,
                                             scale=tok[:, t:t + 1]).then_inc(r_tok, 1)

                @block.tensor
                def _(pe):
                    pe.wait_ge(r_chosen, 1)
                    nc.tensor.matmul(bank[0][:, :], before[:, :], chosen[:, :, :].rearrange("p t e -> p (t e)"),
                                     start=True, stop=False)
                    nc.tensor.matmul(bank[0][:, :], ones[:, :], acc[:, 0:NT, :].rearrange("p t e -> p (t e)"),
                                     start=False, stop=True)
                    nc.tensor.matmul(bank[1][:, 0:EXP], ones[:, :], acc[:, NT, :], start=True,
                                     stop=True).then_inc(r_pos, 1)
                    for c in range(TK):
                        if c in (0, HALF):
                            pe.wait_ge(r_row, 1 + c // HALF)
                        if c % TOPK == 0:
                            pe.wait_ge(r_tok, 1 + c // TOPK)
                        last = nc.tensor.matmul(bank[2][:, 0:SLOTS], in_row[:, c, :], in_slot[:, c, :],
                                                start=(c == 0), stop=(c == TK - 1))
                    last.then_inc(r_idx, 1)

                @block.vector
                def _(dve):
                    steps = [0]

                    def link(instruction):
                        steps[0] += 1
                        instruction.then_inc(r_step, 1)
                        dve.wait_ge(r_step, steps[0])

                    def col(ap, n):
                        return ap.rearrange("p (c o) -> p c o", o=1).broadcast_to([P, ap.shape[1], n])

                    def row(ap, n):
                        return ap.rearrange("p (o e) -> p o e", o=1).broadcast_to([P, n, ap.shape[1]])

                    link(nc.vector.tensor_tensor(before[:, :], upto[:, :], ident[:, :], ALU.subtract))
                    e4 = ev[:, :].rearrange("p (t k) -> p t k", k=TOPK)
                    nc.vector.tensor_tensor(e4, top_v[:, :, :], top_v[:, :, 0:1].broadcast_to([P, NT, TOPK]),
                                            ALU.subtract).then_inc(r_ev, 1)
                    link(nc.vector.tensor_copy(topf[:, :].rearrange("p (t k) -> p t k", k=TOPK), top_i[:, :, :]))
                    dve.wait_ge(r_const, 5)
                    link(nc.vector.tensor_tensor(hot[:, :, :], row(iota_e[:, :], TK), col(topf[:, :], EXP),
                                                 ALU.is_equal))
                    link(nc.vector.tensor_reduce(chosen[:, :, :], hot[:, :, :].rearrange("p (t k) e -> p t e k", k=TOPK),
                                                 AX.X, ALU.add))
                    link(nc.vector.memset(acc[:, 0, :], 0.0))
                    for t in range(NT):
                        ins = nc.vector.tensor_tensor(acc[:, t + 1, :], acc[:, t, :], chosen[:, t, :], ALU.add)
                        if t == NT - 1:
                            ins.then_inc(r_chosen, 1)
                        else:
                            link(ins)
                    dve.wait_ge(r_exp, 1)
                    link(nc.vector.tensor_reduce(ws[:, :], e4, AX.X, ALU.add))
                    link(nc.vector.reciprocal(ws[:, :], ws[:, :]))
                    link(nc.vector.tensor_tensor(wts[:, :].rearrange("p (t k) -> p t k", k=TOPK), e4,
                                                 col(ws[:, :], TOPK), ALU.mult))
                    dve.wait_ge(r_pos, 1)
                    link(nc.vector.tensor_scalar(cnt_i[:, :], bank[1][:, 0:EXP], float(P - 1), None, ALU.add))
                    link(nc.vector.tensor_scalar(cnt_i[:, :], cnt_i[:, :], 7, None, ALU.logical_shift_right))
                    link(nc.vector.tensor_copy(ntf[:, :], cnt_i[:, :]))
                    link(nc.vector.tensor_tensor_scan(cin[:, :], ones[:, 0:EXP], ntf[:, :], 0.0, ALU.mult, ALU.add))
                    link(nc.vector.tensor_tensor(base[:, :], cin[:, :], ntf[:, :], ALU.subtract))
                    link(nc.vector.scalar_tensor_tensor(out=pos[:, :, :], in0=row(base[:, :], NT), scalar=float(P),
                                                        in1=bank[0][:, :].rearrange("p (t e) -> p t e", e=EXP),
                                                        op0=ALU.mult, op1=ALU.add))
                    link(nc.vector.tensor_tensor(hot[:, :, :].rearrange("p (t k) e -> p t k e", k=TOPK),
                                                 hot[:, :, :].rearrange("p (t k) e -> p t k e", k=TOPK),
                                                 pos[:, :, :].rearrange("p t (o e) -> p t o e", o=1)
                                                 .broadcast_to([P, NT, TOPK, EXP]), ALU.mult))
                    link(nc.vector.tensor_reduce(destf[:, :], hot[:, :, :], AX.X, ALU.add))
                    link(nc.vector.tensor_copy(desti[:, :], destf[:, :]))
                    link(nc.vector.tensor_scalar(hi_i[:, :], desti[:, :], 7, None, ALU.logical_shift_right))
                    link(nc.vector.tensor_scalar(desti[:, :], desti[:, :], P - 1, None, ALU.bitwise_and))
                    nc.vector.tensor_copy(lo[:, :], desti[:, :]).then_inc(r_dest, 1)
                    nc.vector.tensor_copy(hi[:, :], hi_i[:, :]).then_inc(r_dest, 1)
                    dve.wait_ge(r_dest, 2)
                    nc.vector.tensor_tensor(in_slot[:, :, :], row(iota_s[:, 0:SLOTS], TK), col(hi[:, :], SLOTS),
                                            ALU.is_equal).then_inc(r_slot, 1)
                    for i in range(2):
                        half = slice(i * HALF, (i + 1) * HALF)
                        nc.vector.tensor_tensor(in_row[:, half, :], row(iota_r[:, :], HALF), col(lo[:, half], P),
                                                ALU.is_equal).then_inc(r_row, 1)
                    link(nc.vector.tensor_scalar(dest[:, :], destf[:, :], float(P), None, ALU.add))
                    link(nc.vector.tensor_tensor(cmp[:, :, :], row(cin[:, :], COLS), col(iota_s[:, :], EXP), ALU.is_le))
                    link(nc.vector.tensor_reduce(eid[:, :], cmp[:, :, :], AX.X, ALU.add))
                    link(nc.vector.tensor_scalar(eid[:, :], eid[:, :], float(EXP - 1), None, ALU.min))
                    link(nc.vector.memset(new[:, 0:1], 1.0))
                    link(nc.vector.tensor_tensor(new[:, 1:], eid[:, 1:], eid[:, 0:COLS - 1], ALU.not_equal))
                    link(nc.vector.tensor_copy(tab_e[:, :], eid[0:1, :]))
                    link(nc.vector.tensor_tensor(eid[:, :], iota_s[:, :], cin[:, EXP - 1:EXP].broadcast_to([P, COLS]),
                                                 ALU.is_lt))
                    link(nc.vector.tensor_tensor(new[:, :], new[:, :], eid[:, :], ALU.mult))
                    link(nc.vector.tensor_tensor_scan(cnew[:, :], ones[:, 0:COLS], new[:, :], -1.0, ALU.mult, ALU.add))
                    link(nc.vector.tensor_copy(tab_n[:, :], new[0:1, :]))
                    link(nc.vector.tensor_tensor(used[:, :], cin[0:1, EXP - 1:EXP].broadcast_to([1, SLOTS // 4]),
                                                 iota_s[0:1, 0:SLOTS].rearrange("p (j u) -> p j u", u=4)[:, :, 0],
                                                 ALU.is_ge))
                    link(nc.vector.tensor_copy(tab_u[:, :], used[:, :]))
                    link(nc.vector.memset(tab_r[:, 0:1], 0))
                    link(nc.vector.tensor_copy(tab_r[:, 1:], cnew[0:1, :]))
                    link(nc.vector.tensor_scalar(tab_r[:, :], tab_r[:, :], RING - 1, None, ALU.bitwise_and))
                    dve.wait_ge(r_idx, 1)
                    link(nc.vector.tensor_copy(idx[:, 0:SLOTS], bank[2][:, 0:SLOTS]))

        with ExitStack() as ex:
            def eb(name, shape, dt=F32):
                return sb(name, shape, dt, ex)

            wr = eb("wr", [P, RING, WEXP])
            br = eb("br", [P, RING, 2 * FF + HID])
            xg = [eb(f"xg{i}", [P, HID]) for i in range(2)]
            idc = [eb(f"idc{i}", [P, 1], I32) for i in range(2)]
            spent = eb("spent", [P, 1], I32)
            idle = eb("idle", [1, 1])
            xT = [eb(f"xT{i}", [P, KH * P]) for i in range(2)]
            gu = [eb(f"gu{i}", [P, 2 * FF]) for i in range(2)]
            sg = [eb(f"sg{i}", [P, FF]) for i in range(2)]
            ac = [eb(f"ac{i}", [P, FF]) for i in range(2)]
            aT = [eb(f"aT{i}", [P, 2 * P]) for i in range(2)]
            yo = [eb(f"yo{i}", [P, HID]) for i in range(2)]
            w_in_ring = [sem(f"w_in_ring{i}") for i in range(4)]
            gathered = [sem(f"gathered{i}") for i in range(2)]
            stored = [sem(f"stored{i}") for i in range(2)]
            idx_first = sem("idx_first")
            idx_set = sem("idx_set")
            x_turned = sem("x_turned")
            x_ready = sem("x_ready")
            gu_made = sem("gu_made")
            gu_read = sem("gu_read")
            clamped = sem("clamped")
            sig_made = sem("sig_made")
            act_made = sem("act_made")
            act_turned = sem("act_turned")
            act_ready = sem("act_ready")
            y_made = sem("y_made")
            y_read = sem("y_read")
            e_step = sem("e_step")
            XTB, GUB, ATB, YB = bank[0:2], bank[2:4], bank[4:6], bank[6:8]

            with nc.Block() as block:
                @block.sync
                def _(sp):
                    def load(i, u):
                        e = sp.value_load(tab_e[0:1, bass.ds(i, 1)], min_val=0, max_val=EXP - 1)
                        n = sp.value_load(tab_n[0:1, bass.ds(i, 1)], min_val=0, max_val=1)
                        r = sp.value_load(tab_r[0:1, bass.ds(i + 1, 1)], min_val=0, max_val=RING - 1)
                        sp.dma_start(wr[:, bass.ds(r, 1), :].rearrange("p o w -> p (o w)"),
                                     wexp[bass.ds(e, 1)].rearrange("o p w -> (o p) w"),
                                     cond=(n == 1)).then_inc(w_in_ring[u % 4], 16)
                        sp.dma_start(br[:, bass.ds(r, 1), :].rearrange("p o w -> p (o w)"),
                                     bexp[bass.ds(e, 1), :].broadcast_to([P, 2 * FF + HID]),
                                     cond=(n == 1)).then_inc(w_in_ring[u % 4], 16)

                    for i in range(AHEAD):
                        load(i, i)
                    with sp.Fori(0, SLOTS // 4) as j:
                        used = sp.value_load(tab_u[0:1, bass.ds(j, 1)], min_val=0, max_val=1)
                        with sp.If(used == 1):
                            for u in range(4):
                                i = 4 * j + u
                                sp.wait_ge(y_read, i + 3)
                                sp.dma_start(ys_d[bass.ds(i * P, P), :], yo[u % 2][:, :]).then_inc(stored[u % 2], 16)
                                load(i + AHEAD, u + AHEAD)
                        with sp.Else():
                            for u in range(4):
                                sp.dma_start(idle[:, :], bexp[0:1, 0:1], cond=(used == 1)) \
                                    .then_inc(stored[u % 2], 16)
                                for _ in range(2):
                                    sp.dma_start(idle[:, :], bexp[0:1, 0:1], cond=(used == 1)) \
                                        .then_inc(w_in_ring[(u + AHEAD) % 4], 16)
                    for k in range(2):
                        sp.wait_ge(stored[k], 16 + 16 * SLOTS // 2)
                    for u in range(4):
                        sp.wait_ge(w_in_ring[u], 32 * (SLOTS // 4 + (u < AHEAD)))

                @block.gpsimd
                def _(pool):
                    def gather(i, u, copied, count):
                        nc.gpsimd.tensor_copy(idc[u % 2][:, :], idx[:, bass.ds(i, 1)]).then_inc(copied, 1)
                        pool.wait_ge(e_step, 1)
                        pool.wait_ge(copied, count)
                        pool.indirect_dma_start(xg[u % 2][:, :], None, h2_d,
                                                bass.IndirectOffsetOnAxis(idc[u % 2][:, :], 0)).then_inc(gathered[u % 2], 16)

                    gather(0, 0, idx_first, 1)
                    gather(1, 1, idx_first, 2)
                    with pool.Fori(0, SLOTS // 4) as j:
                        used = pool.value_load(tab_u[0:1, bass.ds(j, 1)], min_val=0, max_val=1)
                        with pool.If(used == 1):
                            for u in range(4):
                                i = 4 * j + u
                                pool.wait_ge(x_turned, i + 1)
                                gather(i + 2, u, idx_set, i + 1)
                            pool.wait_ge(gathered[0], 32 * j + 48)
                            pool.wait_ge(gathered[1], 32 * j + 48)
                            nc.gpsimd.tensor_copy(spent[:, :], idx[:, bass.ds(i + 3, 1)])

                @block.tensor
                def _(pe):
                    def turn_x(v, count):
                        pe.wait_ge(gathered[v], count)
                        for k in range(KH):
                            last = nc.tensor.transpose(XTB[v][:, k * P:(k + 1) * P], xg[v][:, k * P:(k + 1) * P],
                                                       ident[:, :])
                        last.then_inc(x_turned, 1)

                    turn_x(0, 16)
                    with pe.Fori(0, SLOTS // 4) as j:
                        used = pe.value_load(tab_u[0:1, bass.ds(j, 1)], min_val=0, max_val=1)
                        with pe.If(used == 1):
                            for u in range(4):
                                i = 4 * j + u
                                r = pe.value_load(tab_r[0:1, bass.ds(i + 1, 1)], min_val=0, max_val=RING - 1)
                                rp = pe.value_load(tab_r[0:1, bass.ds(i, 1)], min_val=0, max_val=RING - 1)
                                pe.wait_ge(w_in_ring[u], 32 * j + 32)
                                pe.wait_ge(x_ready, i + 1)
                                pe.wait_ge(gu_read, i + 1)
                                for k in range(KH):
                                    last = nc.tensor.matmul(GUB[u % 2][:, :], xT[u % 2][:, k * P:(k + 1) * P],
                                                            wr[:, bass.ds(r, 1), k * 512:(k + 1) * 512]
                                                            .rearrange("p o w -> p (o w)"),
                                                            start=(k == 0), stop=(k == KH - 1))
                                last.then_inc(gu_made, 1)
                                v = (u + 1) % 2
                                pe.wait_ge(act_made, i + 1)
                                pe.wait_ge(act_ready, i + 1)
                                for k in range(2):
                                    last = nc.tensor.transpose(ATB[v][:, k * P:(k + 1) * P], ac[v][:, k * P:(k + 1) * P],
                                                               ident[:, :])
                                last.then_inc(act_turned, 1)
                                turn_x(v, 32 * j + 16 * ((u + 1) // 2 + 1))
                                pe.wait_ge(act_ready, i + 3)
                                pe.wait_ge(y_read, i + 1)
                                for k in range(2):
                                    last = nc.tensor.matmul(YB[v][:, :], aT[v][:, k * P:(k + 1) * P],
                                                            wr[:, bass.ds(rp, 1), 2048 + k * 512:2048 + (k + 1) * 512]
                                                            .rearrange("p o w -> p (o w)"), start=(k == 0), stop=(k == 1))
                                last.then_inc(y_made, 1)

                @block.scalar
                def _(act):
                    def x_out(i, u):
                        act.wait_ge(x_turned, i + 1)
                        nc.scalar.activation(xT[u % 2][:, :], XTB[u % 2][:, :], ACT.Copy).then_inc(x_ready, 1)

                    x_out(0, 0)
                    with act.Fori(0, SLOTS // 4) as j:
                        used = act.value_load(tab_u[0:1, bass.ds(j, 1)], min_val=0, max_val=1)
                        with act.If(used == 1):
                            for u in range(4):
                                i = 4 * j + u
                                v = (u + 1) % 2
                                act.wait_ge(act_turned, i + 1)
                                nc.scalar.activation(aT[v][:, :], ATB[v][:, 0:2 * P], ACT.Copy).then_inc(act_ready, 1)
                                act.wait_ge(clamped, i + 1)
                                nc.scalar.activation(sg[u % 2][:, :], gu[u % 2][:, 0:FF], ACT.Sigmoid,
                                                     scale=1.702).then_inc(sig_made, 1)
                                x_out(i + 1, u + 1)

                @block.vector
                def _(dve):
                    for k in range(2):
                        nc.vector.memset(yo[k][:, :], 0.0).then_inc(stored[k], 16)
                    nc.vector.memset(ac[0][:, :], 0.0).then_inc(gu_read, 2)
                    nc.vector.memset(aT[1][:, :], 0.0).then_inc(act_ready, 2)
                    nc.vector.memset(aT[0][:, :], 0.0).then_inc(y_read, 2)
                    nc.vector.memset(ac[1][:, :], 0.0).then_inc(act_made, 1)
                    nc.vector.memset(sg[0][:, :], 0.0).then_inc(e_step, 1)
                    with dve.Fori(0, SLOTS // 4) as j:
                        used = dve.value_load(tab_u[0:1, bass.ds(j, 1)], min_val=0, max_val=1)
                        with dve.If(used == 1):
                            for u in range(4):
                                i = 4 * j + u
                                v = (u + 1) % 2
                                r = dve.value_load(tab_r[0:1, bass.ds(i + 1, 1)], min_val=0, max_val=RING - 1)
                                rp = dve.value_load(tab_r[0:1, bass.ds(i, 1)], min_val=0, max_val=RING - 1)
                                c = u % 2
                                dve.wait_ge(gu_made, i + 1)
                                ins = nc.vector.tensor_tensor(gu[c][:, :], GUB[c][:, :],
                                                              br[:, bass.ds(r, 1), 0:512].rearrange("p o w -> p (o w)"), ALU.add)
                                ins.then_inc(gu_read, 1)
                                dve.wait_ge(gu_read, i + 3)
                                nc.vector.tensor_scalar(gu[c][:, 0:FF], gu[c][:, 0:FF], 7.0, None, ALU.min).then_inc(clamped, 1)
                                nc.vector.tensor_scalar(gu[c][:, FF:], gu[c][:, FF:], 7.0, -7.0, ALU.min,
                                                        ALU.max).then_inc(e_step, 1)
                                dve.wait_ge(sig_made, i + 1)
                                dve.wait_ge(clamped, i + 1)
                                nc.vector.tensor_tensor(sg[c][:, :], sg[c][:, :], gu[c][:, 0:FF], ALU.mult).then_inc(e_step, 1)
                                dve.wait_ge(e_step, 2 * i + 3)
                                nc.vector.scalar_tensor_tensor(out=ac[c][:, :], in0=gu[c][:, FF:], scalar=1.0, in1=sg[c][:, :],
                                                               op0=ALU.add, op1=ALU.mult).then_inc(act_made, 1)
                                dve.wait_ge(y_made, i + 1)
                                dve.wait_ge(stored[c], 32 * j + 16 * (u // 2 + 1))
                                nc.vector.tensor_tensor(yo[c][:, :], YB[v][:, :],
                                                        br[:, bass.ds(rp, 1), 512:1024].rearrange("p o w -> p (o w)"),
                                                        ALU.add).then_inc(y_read, 1)

        with ExitStack() as cb:
            def kb(name, shape, dt=F32):
                return sb(name, shape, dt, cb)

            yk = [kb(f"yk{i}", [P, TOPK, HID]) for i in range(DEEP)]
            xr = [kb(f"xr{i}", [P, HID]) for i in range(DEEP)]
            acc = [kb(f"acc{i}", [P, HID]) for i in range(DEEP)]
            d4 = [kb(f"d4{i}", [P, TOPK], I32) for i in range(DEEP)]
            w4 = [kb(f"w4{i}", [P, TOPK]) for i in range(DEEP)]
            gb = kb("gb", [P, BATCH, HID])
            c_gb = sem("c_gb")
            c_d4 = sem("c_d4")
            c_y = [sem(f"c_y{i}") for i in range(DEEP)]
            c_x = [sem(f"c_x{i}") for i in range(DEEP)]
            c_out = [sem(f"c_out{i}") for i in range(DEEP)]
            c_done = sem("c_done")
            c_step = sem("c_step")
            with nc.Block() as block:
                @block.gpsimd
                def _(pool):
                    with pool.Fori(0, BATCH) as b:
                        for u in range(NQ):
                            t = NQ * b + u
                            pool.wait_ge(c_done, t + 1)
                            nc.gpsimd.tensor_copy(d4[u][:, :], dest[:, bass.ds(t * TOPK, TOPK)]).then_inc(c_d4, 1)
                            pool.wait_ge(c_gb, 16 * BATCH)
                            pool.wait_ge(c_d4, t + 1)
                            for k in range(TOPK):
                                pool.indirect_dma_start(yk[u][:, k, :], None, ys_d,
                                                        bass.IndirectOffsetOnAxis(d4[u][:, k:k + 1], 0)) \
                                    .then_inc(c_y[u], 16)

                @block.sync
                def _(sp):
                    for b in range(BATCH):
                        sp.dma_start(gb[:, b, :], mod_d[b:b + 1, 5 * HID:6 * HID].broadcast_to([P, HID])).then_inc(c_gb, 16)
                    with sp.Fori(0, BATCH) as b:
                        for u in range(NQ):
                            t = NQ * b + u
                            sp.wait_ge(c_done, t + 1)
                            sp.dma_start(xr[u][:, :], x2_d[bass.ds(t * P, P), :]).then_inc(c_x[u], 16)
                    for k in range(DEEP):
                        sp.wait_ge(c_out[k], 16 + 16 * BATCH)

                @block.scalar
                def _(act):
                    with act.Fori(0, BATCH) as b:
                        for u in range(NQ):
                            act.wait_ge(c_done, NQ * b + u + 1 + DEEP)
                            act.dma_start(out[bass.ds(b, 1), u * P:(u + 1) * P, :].rearrange("o p d -> (o p) d"),
                                          acc[u][:, :]).then_inc(c_out[u], 16)

                @block.vector
                def _(dve):
                    nc.vector.memset(w4[0][:, :], 0.0).then_inc(c_done, DEEP)
                    for k in range(DEEP):
                        nc.vector.memset(acc[k][:, :], 0.0).then_inc(c_out[k], 16)
                    dve.wait_ge(c_done, DEEP)
                    dve.wait_ge(c_out[DEEP - 1], 16)
                    dve.wait_ge(c_gb, 16 * BATCH)
                    with dve.Fori(0, BATCH) as b:
                        for u in range(NQ):
                            t = NQ * b + u
                            n = [0]

                            def link(instruction):
                                n[0] += 1
                                instruction.then_inc(c_step, 1)
                                dve.wait_ge(c_step, t * 6 + n[0])

                            link(nc.vector.tensor_copy(w4[u][:, :], wts[:, bass.ds(t * TOPK, TOPK)]))
                            dve.wait_ge(c_y[u], 64 * b + 64)
                            dve.wait_ge(c_out[u], 16 * b + 16)
                            link(nc.vector.tensor_scalar(acc[u][:, :], yk[u][:, 0, :], w4[u][:, 0:1], None, ALU.mult))
                            for k in range(1, TOPK):
                                link(nc.vector.scalar_tensor_tensor(out=acc[u][:, :], in0=yk[u][:, k, :],
                                                                    scalar=w4[u][:, k:k + 1], in1=acc[u][:, :],
                                                                    op0=ALU.mult, op1=ALU.add))
                            link(nc.vector.tensor_tensor(acc[u][:, :], acc[u][:, :],
                                                         gb[:, bass.ds(b, 1), :].rearrange("p o d -> p (o d)"), ALU.mult))
                            dve.wait_ge(c_x[u], 16 * b + 16)
                            nc.vector.tensor_tensor(acc[u][:, :], acc[u][:, :], xr[u][:, :], ALU.add).then_inc(c_done, 1)


def layouts(i):
    f = {k[3:]: np.asarray(v) for k, v in i.items()}

    def rows(a):
        return a.reshape(-1, P, *a.shape[1:]).swapaxes(0, 1)

    c_rows = rows(f["c"].T)
    wmod = f["wmod"].reshape(KH, P, 6, HID).transpose(2, 1, 0, 3)
    conv = np.concatenate([f["attn_conv_w"], f["attn_conv_b"][:, None]], axis=1)
    vecs = np.concatenate([f["attn_dt_bias"], f["attn_A_log"], f["ffn_gate_b"]])[None]
    gate_up = np.concatenate([f["ffn_w_gate"], f["ffn_w_up"]], axis=2)
    gate_up = gate_up.reshape(EXP, KH, P, 2 * FF).transpose(0, 2, 1, 3).reshape(EXP, P, KH * 2 * FF)
    down = f["ffn_w_down"].reshape(EXP, 2, P, HID).transpose(0, 2, 1, 3).reshape(EXP, P, 2 * HID)
    return {
        "x": f["attn_hidden_states"], "cT": c_rows, "wmod": wmod, "w_in": rows(f["attn_W_in"]),
        "w_out": rows(f["attn_W_out"]), "convp": rows(conv), "vecs": vecs, "mup": f["attn_mup_vector"][None],
        "nw": f["attn_norm_w"].reshape(8, P).T, "dcol": np.repeat(f["attn_D"], HD).reshape(8, P).T,
        "gwT": rows(f["ffn_gate_w"].T),
        "wexp": np.concatenate([gate_up, down], axis=2),
        "bexp": np.concatenate([f["ffn_b_gate"], f["ffn_b_up"], f["ffn_b_down"]], axis=1),
    }


def kernel(**inputs):
    import concourse.bacc as _bacc
    from concourse.bass_utils import run_bass_kernel_spmd as _run

    nc = _bacc.Bacc("TRN2", target_bir_lowering=False, num_devices=1)
    arrays, args = {}, []
    for name, a in layouts(inputs).items():
        a = np.ascontiguousarray(a)
        arrays[f"in_{name}"] = a
        args.append(nc.dram_tensor(f"in_{name}", a.shape, mybir.dt.from_np(a.dtype), kind="ExternalInput").ap())
    out = nc.dram_tensor("out_0", (BATCH, SEQ, HID), F32, kind="ExternalOutput").ap()
    build(nc, args, out)
    return _run(nc, [arrays], core_ids=[0]).results[0]["out_0"]
```
